# Optimizing a Trainium2 kernel written in Bass

```python
import numpy as np
import jax
import jax.numpy as jnp

def _softmax(x, axis=-1):
    return jax.nn.softmax(x, axis=axis)

def _gelu(x):
    return jax.nn.gelu(x, approximate=True)

def _silu(x):
    return jax.nn.silu(x)

def _sigmoid(x):
    return jax.nn.sigmoid(x)

def _layernorm(x, axis=-1, eps=1e-05):
    m = jnp.mean(x, axis=axis, keepdims=True)
    v = jnp.var(x, axis=axis, keepdims=True)
    return (x - m) / jnp.sqrt(v + eps)

def _scatter_add(tgt, idx, src, axis=0):
    return tgt.at[idx].add(src)

def _segment_sum(src, seg, n):
    return jax.ops.segment_sum(src, seg, n)
kernel_name = 'mk_xattn_ffn_d4_seqx_r8_d84889'

def setup_inputs(seed: int=0):
    np.random.seed(seed)
    _w = jnp.asarray

    def _rec_inputs():
        import jax
        import jax.numpy as jnp
        _rk = jax.random.key(seed)
        x = -0.0003929 + 0.9999 * jax.random.normal(jax.random.fold_in(_rk, 1), (32, 128, 128), jnp.float32)
        _lenS = 128 - jax.random.randint(jax.random.fold_in(_rk, 7), (32,), 0, max(1, 128 // 4) + 1, jnp.int32)
        _lenS2 = 120 - jax.random.randint(jax.random.fold_in(_rk, 8), (32,), 0, max(1, 120 // 4) + 1, jnp.int32)
        _ctx_1024P = jax.random.normal(jax.random.fold_in(_rk, 11), (32, 16, 128), jnp.float32)
        _ctx_1024c = jax.random.dirichlet(jax.random.fold_in(_rk, 511), 0.3 * jnp.ones((16,), jnp.float32), (32, 120))
        _ctx_1024t = jnp.einsum('bsk,bkd->bsd', _ctx_1024c, _ctx_1024P)
        _ctx_1024t = _ctx_1024t * jax.lax.rsqrt(jnp.mean(jnp.square(_ctx_1024t)) + 1e-12) * 0.953939
        ctx_1024 = 2.81802e-05 + 1.00001 * (_ctx_1024t + 0.3 * jax.random.normal(jax.random.fold_in(_rk, 611), (32, 120, 128), jnp.float32))
        itok_BxS2_0_2047 = jax.random.randint(jax.random.fold_in(_rk, 14), (32, 120), 0, 256, jnp.int32)
        _validS = jnp.arange(128)[None, :] < _lenS[:, None]
        _validS2 = jnp.arange(120)[None, :] < _lenS2[:, None]
        _causal = jnp.tril(jnp.ones((128, 128), dtype=bool))
        mask_SxS2_ik1 = jnp.where(jnp.broadcast_to(_validS2[0:1, :], (128, 120)), 1, 0).astype(jnp.int32)
        mask_1x1xSxS2_ik0 = jnp.where(jnp.broadcast_to(_validS2[0:1, None, None, :], (1, 1, 128, 120)), 0, 1).astype(jnp.int32)
        return (x, ctx_1024, itok_BxS2_0_2047, mask_SxS2_ik1, mask_1x1xSxS2_ik0)
    x, ctx_1024, itok_BxS2_0_2047, mask_SxS2_ik1, mask_1x1xSxS2_ik0 = _rec_inputs()

    def _L0_xattn_setup():
        import jax, jax.numpy as jnp
        import numpy as np
        B, T, C, H = (4, 512, 128, 16)
        D = C // H

        def _heads(t):
            b, n, c = t.shape
            return t.reshape(b, n, H, D).transpose(0, 2, 1, 3)
        key = jax.random.key(seed)
        ks = jax.random.split(key, 10)
        s = 1.0 / np.sqrt(C)
        return {'x': jax.random.normal(ks[0], (B, T, C), jnp.float32), 'y': jax.random.normal(ks[1], (B, T, C), jnp.float32), 'Wq': jax.random.normal(ks[2], (C, C), jnp.float32) * s, 'bq': jnp.zeros((C,), jnp.float32), 'Wk': jax.random.normal(ks[3], (C, C), jnp.float32) * s, 'bk': jnp.zeros((C,), jnp.float32), 'Wv': jax.random.normal(ks[4], (C, C), jnp.float32) * s, 'bv': jnp.zeros((C,), jnp.float32), 'Wp': jax.random.normal(ks[5], (C, C), jnp.float32) * s, 'bp': jnp.zeros((C,), jnp.float32)}
    _L0_xattn_all = _L0_xattn_setup()
    _L0_xattn_in = {k: v for k, v in _L0_xattn_all.items() if k in ('Wq', 'bq', 'Wk', 'bk', 'Wv', 'bv', 'Wp', 'bp')}
    del _L0_xattn_all

    def _L0_ffn_setup():
        import jax, jax.numpy as jnp
        import numpy as np

        def _bitlinear(x, w_latent):
            scale = jax.lax.stop_gradient(jnp.clip(jnp.mean(jnp.abs(w_latent), axis=1, keepdims=True), 1e-05, None))
            tern = jnp.clip(jnp.round(w_latent / scale), -1.0, 1.0)
            w = w_latent + jax.lax.stop_gradient(tern - w_latent)
            return x @ (w * scale).T
        key = jax.random.key(seed)
        ks = jax.random.split(key, 6)
        dim, hidden, rank = (128, 512, 16)
        B, S = (4, 512)
        x = jax.random.normal(ks[0], (B, S, dim), dtype=jnp.float32)
        w_fc = 0.02 * jax.random.normal(ks[1], (hidden, dim), dtype=jnp.float32)
        w_proj = 0.02 * jax.random.normal(ks[2], (dim, hidden), dtype=jnp.float32)
        u = 0.02 * jax.random.normal(ks[3], (hidden, rank), dtype=jnp.float32)
        v = 0.02 * jax.random.normal(ks[4], (rank, dim), dtype=jnp.float32)
        fast_b = jax.random.normal(ks[5], (rank, rank), dtype=jnp.float32)
        gate = jnp.float32(0.05)
        return {'x': x, 'fast_b': fast_b, 'w_fc': w_fc, 'w_proj': w_proj, 'u': u, 'v': v, 'gate': gate}
    _L0_ffn_all = _L0_ffn_setup()
    _L0_ffn_in = {k: v for k, v in _L0_ffn_all.items() if k in ('fast_b', 'w_fc', 'w_proj', 'u', 'v', 'gate')}
    del _L0_ffn_all

    def _L1_xattn_setup():
        import jax, jax.numpy as jnp
        import numpy as np
        B, T, E = (8, 256, 128)
        key = jax.random.key(seed)
        k1, k2, k3, k4, k5, k6, k7 = jax.random.split(key, 7)
        return {'q': jax.random.normal(k1, (B, T, E), jnp.float32), 'k': jax.random.normal(k2, (B, T, E), jnp.float32), 'v': jax.random.normal(k3, (B, T, E), jnp.float32), 'mask': jax.random.randint(k4, (T, T), 0, 2, jnp.int32), 'Wq': jax.random.normal(k5, (E, E), jnp.float32) / np.sqrt(E), 'Wk': jax.random.normal(k6, (E, E), jnp.float32) / np.sqrt(E), 'Wv': jax.random.normal(k7, (E, E), jnp.float32) / np.sqrt(E)}
    _L1_xattn_all = _L1_xattn_setup()
    _L1_xattn_in = {k: v for k, v in _L1_xattn_all.items() if k in ('Wq', 'Wk', 'Wv')}
    del _L1_xattn_all

    def _L1_ffn_setup():
        import jax, jax.numpy as jnp
        import numpy as np
        E, K, D, F = (8, 2, 128, 512)
        EPS = 1e-06
        B, S = (2, 128)
        key = jax.random.key(seed)
        ks = jax.random.split(key, 6)
        s_in = 1.0 / np.sqrt(D)
        s_mid = 1.0 / np.sqrt(F)
        return {'x': jax.random.normal(ks[0], (B, S, D), dtype=jnp.float32), 'Wg': jax.random.normal(ks[1], (D, E), dtype=jnp.float32) * s_in, 'gamma': jnp.ones((E, D), dtype=jnp.float32), 'beta': jnp.zeros((E, D), dtype=jnp.float32), 'W1': jax.random.normal(ks[2], (E, D, F), dtype=jnp.float32) * s_in, 'b1': jnp.zeros((E, F), dtype=jnp.float32), 'W2': jax.random.normal(ks[3], (E, F, D), dtype=jnp.float32) * s_mid, 'b2': jnp.zeros((E, D), dtype=jnp.float32)}
    _L1_ffn_all = _L1_ffn_setup()
    _L1_ffn_in = {k: v for k, v in _L1_ffn_all.items() if k in ('Wg', 'gamma', 'beta', 'W1', 'b1', 'W2', 'b2')}
    del _L1_ffn_all

    def _L2_xattn_setup():
        import jax, jax.numpy as jnp
        import numpy as np
        from math import sqrt
        HEADS = 16
        D_MODEL = 128
        HEAD_DIM = D_MODEL // HEADS
        B, SEQ = (2, 256)
        key = jax.random.key(seed)
        ks = jax.random.split(key, 8)
        k = jax.random.normal(ks[0], (B, SEQ, D_MODEL), dtype=jnp.float32)
        q = jax.random.normal(ks[1], (B, SEQ, D_MODEL), dtype=jnp.float32)
        v = jax.random.normal(ks[2], (B, SEQ, D_MODEL), dtype=jnp.float32)
        mask = jnp.tril(jnp.ones((SEQ, SEQ), dtype=jnp.int32))[None, None, :, :]
        s = 1.0 / sqrt(HEAD_DIM)
        Wq = jax.random.normal(ks[3], (HEAD_DIM, HEAD_DIM), dtype=jnp.float32) * s
        Wk = jax.random.normal(ks[4], (HEAD_DIM, HEAD_DIM), dtype=jnp.float32) * s
        Wv = jax.random.normal(ks[5], (HEAD_DIM, HEAD_DIM), dtype=jnp.float32) * s
        Wo = jax.random.normal(ks[6], (D_MODEL, D_MODEL), dtype=jnp.float32) * (1.0 / sqrt(D_MODEL))
        bo = jax.random.normal(ks[7], (D_MODEL,), dtype=jnp.float32) * 0.01
        return {'key': k, 'query': q, 'value': v, 'mask': mask, 'Wq': Wq, 'Wk': Wk, 'Wv': Wv, 'Wo': Wo, 'bo': bo}
    _L2_xattn_all = _L2_xattn_setup()
    _L2_xattn_in = {k: v for k, v in _L2_xattn_all.items() if k in ('Wq', 'Wk', 'Wv', 'Wo', 'bo')}
    del _L2_xattn_all

    def _L2_ffn_setup():
        import jax, jax.numpy as jnp
        import numpy as np
        B, N, D = (4, 512, 128)
        E, S, F = (16, 64, 256)
        DO = 128
        EPS = 1e-05

        def _layernorm(x, g, b):
            mu = jnp.mean(x, axis=-1, keepdims=True)
            var = jnp.mean(jnp.square(x - mu), axis=-1, keepdims=True)
            return (x - mu) * jax.lax.rsqrt(var + EPS) * g + b
        key = jax.random.key(seed)
        ks = jax.random.split(key, 8)
        d = {'x': jax.random.normal(ks[0], (B, N, D), dtype=jnp.float32), 'norm_g': jnp.ones((D,), jnp.float32), 'norm_b': jnp.zeros((D,), jnp.float32), 'slot_g': jnp.ones((D,), jnp.float32), 'slot_b': jnp.zeros((D,), jnp.float32), 'scale': jnp.ones((1,), jnp.float32), 'slot_embeds': jax.random.normal(ks[1], (E, S, D), jnp.float32) / np.sqrt(D), 'Wg': jax.random.normal(ks[2], (E, D, F), jnp.float32) * np.sqrt(2.0 / (D + F)), 'bg': jnp.zeros((E, F), jnp.float32), 'Wu': jax.random.normal(ks[3], (E, D, F), jnp.float32) * np.sqrt(2.0 / (D + F)), 'bu': jnp.zeros((E, F), jnp.float32), 'Wd': jax.random.normal(ks[4], (E, F, DO), jnp.float32) * np.sqrt(2.0 / (F + DO)), 'bd': jnp.zeros((E, DO), jnp.float32)}
        return d
    _L2_ffn_all = _L2_ffn_setup()
    _L2_ffn_in = {k: v for k, v in _L2_ffn_all.items() if k in ('norm_g', 'norm_b', 'slot_g', 'slot_b', 'scale', 'slot_embeds', 'Wg', 'bg', 'Wu', 'bu', 'Wd', 'bd')}
    del _L2_ffn_all

    def _L3_xattn_setup():
        import jax, jax.numpy as jnp
        import numpy as np
        DIM = 128
        HEADS = 16
        HEAD_DIM = DIM // HEADS
        SCALE = HEAD_DIM ** (-0.5)
        key = jax.random.key(seed)
        ks = jax.random.split(key, 13)
        B, Nq, Nk = (4, 256, 256)
        s = DIM ** (-0.5)
        return {'query': jax.random.normal(ks[0], (B, Nq, DIM), jnp.float32), 'key': jax.random.normal(ks[1], (B, Nk, DIM), jnp.float32), 'value': jax.random.normal(ks[2], (B, Nk, DIM), jnp.float32), 'qpos': jax.random.randint(ks[3], (B, Nq), 0, Nq), 'kpos': jax.random.randint(ks[4], (B, Nk), 0, Nk), 'Wq': jax.random.normal(ks[5], (DIM, DIM), jnp.float32) * s, 'bq': jnp.zeros((DIM,), jnp.float32), 'Wk': jax.random.normal(ks[6], (DIM, DIM), jnp.float32) * s, 'bk': jnp.zeros((DIM,), jnp.float32), 'Wv': jax.random.normal(ks[7], (DIM, DIM), jnp.float32) * s, 'bv': jnp.zeros((DIM,), jnp.float32), 'Wo': jax.random.normal(ks[8], (DIM, DIM), jnp.float32) * s, 'bo': jnp.zeros((DIM,), jnp.float32)}
    _L3_xattn_all = _L3_xattn_setup()
    _L3_xattn_in = {k: v for k, v in _L3_xattn_all.items() if k in ('Wq', 'bq', 'Wk', 'bk', 'Wv', 'bv', 'Wo', 'bo')}
    del _L3_xattn_all

    def _L3_ffn_setup():
        import jax, jax.numpy as jnp
        import numpy as np
        EPS = 1e-06
        N_EXPERTS = 8

        def _rms_norm(x, scale, eps=EPS):
            mean_sq = jnp.mean(x.astype(jnp.float32) ** 2, axis=-1, keepdims=True)
            s = scale.astype(jnp.float32) * jax.lax.rsqrt(mean_sq + eps)
            return x * s.astype(x.dtype)

        def _dist2(x, y):
            nx = jnp.sum(x ** 2, axis=-1)[..., :, None]
            ny = jnp.sum(y ** 2, axis=-1)[..., None, :]
            return nx + ny - 2.0 * (x @ y.T)
        key = jax.random.key(seed)
        ks = jax.random.split(key, 5)
        dim, hidden, E = (128, 256, N_EXPERTS)
        x = jax.random.normal(ks[0], (4, 256, dim), dtype=jnp.float32)
        scale = jnp.ones((dim,), dtype=jnp.float32)
        centroids = jax.random.normal(ks[1], (E, dim), dtype=jnp.float32)
        up_w = jax.random.normal(ks[2], (E, dim, hidden * 2), dtype=jnp.float32) * dim ** (-0.5)
        down_w = jax.random.normal(ks[3], (E, hidden, dim), dtype=jnp.float32) * hidden ** (-0.5)
        return {'x': x, 'scale': scale, 'centroids': centroids, 'up_w': up_w, 'down_w': down_w}
    _L3_ffn_all = _L3_ffn_setup()
    _L3_ffn_in = {k: v for k, v in _L3_ffn_all.items() if k in ('scale', 'centroids', 'up_w', 'down_w')}
    del _L3_ffn_all
    return {'x': x, 'ctx_1024': ctx_1024, 'itok_BxS2_0_2047': itok_BxS2_0_2047, 'mask_SxS2_ik1': mask_SxS2_ik1, 'mask_1x1xSxS2_ik0': mask_1x1xSxS2_ik0, 'L0_xattn_Wq': _L0_xattn_in['Wq'], 'L0_xattn_bq': _L0_xattn_in['bq'], 'L0_xattn_Wk': _L0_xattn_in['Wk'], 'L0_xattn_bk': _L0_xattn_in['bk'], 'L0_xattn_Wv': _L0_xattn_in['Wv'], 'L0_xattn_bv': _L0_xattn_in['bv'], 'L0_xattn_Wp': _L0_xattn_in['Wp'], 'L0_xattn_bp': _L0_xattn_in['bp'], 'L0_ffn_fast_b': _L0_ffn_in['fast_b'], 'L0_ffn_w_fc': _L0_ffn_in['w_fc'], 'L0_ffn_w_proj': _L0_ffn_in['w_proj'], 'L0_ffn_u': _L0_ffn_in['u'], 'L0_ffn_v': _L0_ffn_in['v'], 'L0_ffn_gate': _L0_ffn_in['gate'], 'L1_xattn_Wq': _L1_xattn_in['Wq'], 'L1_xattn_Wk': _L1_xattn_in['Wk'], 'L1_xattn_Wv': _L1_xattn_in['Wv'], 'L1_ffn_Wg': _L1_ffn_in['Wg'], 'L1_ffn_gamma': _L1_ffn_in['gamma'], 'L1_ffn_beta': _L1_ffn_in['beta'], 'L1_ffn_W1': _L1_ffn_in['W1'], 'L1_ffn_b1': _L1_ffn_in['b1'], 'L1_ffn_W2': _L1_ffn_in['W2'], 'L1_ffn_b2': _L1_ffn_in['b2'], 'L2_xattn_Wq': _L2_xattn_in['Wq'], 'L2_xattn_Wk': _L2_xattn_in['Wk'], 'L2_xattn_Wv': _L2_xattn_in['Wv'], 'L2_xattn_Wo': _L2_xattn_in['Wo'], 'L2_xattn_bo': _L2_xattn_in['bo'], 'L2_ffn_norm_g': _L2_ffn_in['norm_g'], 'L2_ffn_norm_b': _L2_ffn_in['norm_b'], 'L2_ffn_slot_g': _L2_ffn_in['slot_g'], 'L2_ffn_slot_b': _L2_ffn_in['slot_b'], 'L2_ffn_scale': _L2_ffn_in['scale'], 'L2_ffn_slot_embeds': _L2_ffn_in['slot_embeds'], 'L2_ffn_Wg': _L2_ffn_in['Wg'], 'L2_ffn_bg': _L2_ffn_in['bg'], 'L2_ffn_Wu': _L2_ffn_in['Wu'], 'L2_ffn_bu': _L2_ffn_in['bu'], 'L2_ffn_Wd': _L2_ffn_in['Wd'], 'L2_ffn_bd': _L2_ffn_in['bd'], 'L3_xattn_Wq': _L3_xattn_in['Wq'], 'L3_xattn_bq': _L3_xattn_in['bq'], 'L3_xattn_Wk': _L3_xattn_in['Wk'], 'L3_xattn_bk': _L3_xattn_in['bk'], 'L3_xattn_Wv': _L3_xattn_in['Wv'], 'L3_xattn_bv': _L3_xattn_in['bv'], 'L3_xattn_Wo': _L3_xattn_in['Wo'], 'L3_xattn_bo': _L3_xattn_in['bo'], 'L3_ffn_scale': _L3_ffn_in['scale'], 'L3_ffn_centroids': _L3_ffn_in['centroids'], 'L3_ffn_up_w': _L3_ffn_in['up_w'], 'L3_ffn_down_w': _L3_ffn_in['down_w']}

def reference(x, ctx_1024, itok_BxS2_0_2047, mask_SxS2_ik1, mask_1x1xSxS2_ik0, L0_xattn_Wq, L0_xattn_bq, L0_xattn_Wk, L0_xattn_bk, L0_xattn_Wv, L0_xattn_bv, L0_xattn_Wp, L0_xattn_bp, L0_ffn_fast_b, L0_ffn_w_fc, L0_ffn_w_proj, L0_ffn_u, L0_ffn_v, L0_ffn_gate, L1_xattn_Wq, L1_xattn_Wk, L1_xattn_Wv, L1_ffn_Wg, L1_ffn_gamma, L1_ffn_beta, L1_ffn_W1, L1_ffn_b1, L1_ffn_W2, L1_ffn_b2, L2_xattn_Wq, L2_xattn_Wk, L2_xattn_Wv, L2_xattn_Wo, L2_xattn_bo, L2_ffn_norm_g, L2_ffn_norm_b, L2_ffn_slot_g, L2_ffn_slot_b, L2_ffn_scale, L2_ffn_slot_embeds, L2_ffn_Wg, L2_ffn_bg, L2_ffn_Wu, L2_ffn_bu, L2_ffn_Wd, L2_ffn_bd, L3_xattn_Wq, L3_xattn_bq, L3_xattn_Wk, L3_xattn_bk, L3_xattn_Wv, L3_xattn_bv, L3_xattn_Wo, L3_xattn_bo, L3_ffn_scale, L3_ffn_centroids, L3_ffn_up_w, L3_ffn_down_w):
    import jax
    import jax.numpy as jnp

    def _L0_xattn_ref(x, y, Wq, bq, Wk, bk, Wv, bv, Wp, bp):
        import jax, jax.numpy as jnp
        import numpy as np
        B, T, C, H = (4, 512, 128, 16)
        D = C // H

        def _heads(t):
            b, n, c = t.shape
            return t.reshape(b, n, H, D).transpose(0, 2, 1, 3)
        q = jax.nn.softmax(_heads(x @ Wq.T + bq), axis=-1)
        k = jax.nn.softmax(_heads(y @ Wk.T + bk), axis=-1)
        v = _heads(y @ Wv.T + bv)
        k_cumsum = jnp.sum(k, axis=-2, keepdims=True)
        D_inv = 1.0 / jnp.sum(q * k_cumsum, axis=-1, keepdims=True)
        kv = jnp.einsum('bhnd,bhne->bhde', k, v)
        out = q + jnp.einsum('bhnd,bhde->bhne', q, kv) * D_inv
        out = out.transpose(0, 2, 1, 3).reshape(x.shape[0], x.shape[1], C)
        return out @ Wp.T + bp

    def _L0_ffn_ref(x, fast_b, w_fc, w_proj, u, v, gate):
        import jax, jax.numpy as jnp
        import numpy as np

        def _bitlinear(x, w_latent):
            scale = jax.lax.stop_gradient(jnp.clip(jnp.mean(jnp.abs(w_latent), axis=1, keepdims=True), 1e-05, None))
            tern = jnp.clip(jnp.round(w_latent / scale), -1.0, 1.0)
            w = w_latent + jax.lax.stop_gradient(tern - w_latent)
            return x @ (w * scale).T
        h = _bitlinear(x, w_fc) + gate * (x @ v.T @ fast_b.T @ u.T)
        r = jnp.maximum(h, 0.0)
        return _bitlinear(r * r, w_proj)

    def _L1_xattn_ref(q, k, v, mask, Wq, Wk, Wv):
        import jax, jax.numpy as jnp
        import numpy as np
        B, T, E = (8, 256, 128)
        query = jnp.einsum('bte,oe->bto', q, Wq)
        key_p = jnp.einsum('bse,oe->bso', k, Wk)
        value = jnp.einsum('bse,oe->bso', v, Wv)
        d = key_p.shape[-1]
        scores = jnp.einsum('bto,bso->bts', query, key_p) / np.sqrt(d).astype(jnp.float32)
        scores = jnp.where(mask[None, :, :] == 0, -jnp.inf, scores)
        weights = jax.nn.softmax(scores, axis=-1)
        return jnp.einsum('bts,bso->bto', weights, value)

    def _L1_ffn_ref(x, Wg, gamma, beta, W1, b1, W2, b2):
        import jax, jax.numpy as jnp
        import numpy as np
        E, K, D, F = (8, 2, 128, 512)
        EPS = 1e-06
        B, S = (2, 128)
        orig_shape = x.shape
        xf = x.reshape(-1, orig_shape[-1])
        scores = xf @ Wg
        w, idx = jax.lax.top_k(scores, K)
        w = jax.nn.softmax(w, axis=-1)
        mu = jnp.mean(xf, axis=-1, keepdims=True)
        var = jnp.var(xf, axis=-1, keepdims=True)
        xhat = (xf - mu) * jax.lax.rsqrt(var + EPS)
        normed = xhat[None, :, :] * gamma[:, None, :] + beta[:, None, :]
        h = jax.nn.relu(jnp.einsum('end,edf->enf', normed, W1) + b1[:, None, :])
        out = jnp.einsum('enf,efd->end', h, W2) + b2[:, None, :] + xf[None, :, :]
        cw = jnp.sum(w[..., None] * jax.nn.one_hot(idx, E, dtype=w.dtype), axis=1)
        y = jnp.einsum('ne,end->nd', cw, out)
        return y.reshape(orig_shape)

    def _L2_xattn_ref(key, query, value, mask, Wq, Wk, Wv, Wo, bo):
        import jax, jax.numpy as jnp
        import numpy as np
        from math import sqrt
        HEADS = 16
        D_MODEL = 128
        HEAD_DIM = D_MODEL // HEADS
        B, SEQ = (2, 256)
        b, q_len, d = query.shape
        k_len = key.shape[1]
        hd = d // HEADS
        k = key.reshape(b, k_len, HEADS, hd)
        q = query.reshape(b, q_len, HEADS, hd)
        v = value.reshape(b, k_len, HEADS, hd)
        k = jnp.einsum('bkhd,ed->bkhe', k, Wk)
        q = jnp.einsum('bqhd,ed->bqhe', q, Wq)
        v = jnp.einsum('bvhd,ed->bvhe', v, Wv)
        product = jnp.einsum('bqhd,bkhd->bhqk', q, k)
        product = jnp.where(mask == 0, jnp.float32(-1e+20), product)
        product = product / jnp.float32(sqrt(hd))
        score = jax.nn.softmax(product, axis=-1)
        out = jnp.einsum('bhqv,bvhd->bqhd', score, v).reshape(b, q_len, d)
        out = out @ Wo.T + bo
        return out

    def _L2_ffn_ref(x, norm_g, norm_b, slot_g, slot_b, scale, slot_embeds, Wg, bg, Wu, bu, Wd, bd):
        import jax, jax.numpy as jnp
        import numpy as np
        B, N, D = (4, 512, 128)
        E, S, F = (16, 64, 256)
        DO = 128
        EPS = 1e-05

        def _layernorm(x, g, b):
            mu = jnp.mean(x, axis=-1, keepdims=True)
            var = jnp.mean(jnp.square(x - mu), axis=-1, keepdims=True)
            return (x - mu) * jax.lax.rsqrt(var + EPS) * g + b
        x = _layernorm(x, norm_g, norm_b)
        se = _layernorm(slot_embeds, slot_g, slot_b) * scale
        logits = jnp.einsum('bnd,esd->bnes', x, se)
        dispatch = jax.nn.softmax(logits, axis=1)
        combine = jax.nn.softmax(logits.reshape(x.shape[0], x.shape[1], -1), axis=-1)
        slots = jnp.einsum('bnd,bnes->besd', x, dispatch)
        gate = jax.nn.gelu(jnp.einsum('besd,edf->besf', slots, Wg) + bg[None, :, None, :], approximate=False)
        up = jnp.einsum('besd,edf->besf', slots, Wu) + bu[None, :, None, :]
        eout = jnp.einsum('besf,efo->beso', gate * up, Wd) + bd[None, :, None, :]
        eout = eout.reshape(eout.shape[0], -1, eout.shape[-1])
        return jnp.einsum('bns,bso->bno', combine, eout)

    def _L3_xattn_ref(query, key, value, qpos, kpos, Wq, bq, Wk, bk, Wv, bv, Wo, bo):
        import jax, jax.numpy as jnp
        import numpy as np
        DIM = 128
        HEADS = 16
        HEAD_DIM = DIM // HEADS
        SCALE = HEAD_DIM ** (-0.5)
        B, Nq, C = query.shape

        def split_heads(x):
            return x.reshape(x.shape[0], x.shape[1], HEADS, HEAD_DIM).transpose(0, 2, 1, 3)
        q = split_heads(query @ Wq + bq)
        k = split_heads(key @ Wk + bk)
        v = split_heads(value @ Wv + bv)
        attn = jnp.einsum('bhqd,bhkd->bhqk', q, k) * SCALE
        attn = jax.nn.softmax(attn, axis=-1)
        x = jnp.einsum('bhqk,bhkd->bhqd', attn, v)
        x = x.transpose(0, 2, 1, 3).reshape(B, Nq, C)
        return x @ Wo + bo

    def _L3_ffn_ref(x, scale, centroids, up_w, down_w):
        import jax, jax.numpy as jnp
        import numpy as np
        EPS = 1e-06
        N_EXPERTS = 8

        def _rms_norm(x, scale, eps=EPS):
            mean_sq = jnp.mean(x.astype(jnp.float32) ** 2, axis=-1, keepdims=True)
            s = scale.astype(jnp.float32) * jax.lax.rsqrt(mean_sq + eps)
            return x * s.astype(x.dtype)

        def _dist2(x, y):
            nx = jnp.sum(x ** 2, axis=-1)[..., :, None]
            ny = jnp.sum(y ** 2, axis=-1)[..., None, :]
            return nx + ny - 2.0 * (x @ y.T)
        skip = x
        xn = _rms_norm(x, scale)
        ids = jnp.argmin(_dist2(xn, centroids), axis=-1)
        out = jnp.zeros_like(x)
        for e in range(N_EXPERTS):
            h = jnp.einsum('bsd,dh->bsh', xn, up_w[e])
            a, g = jnp.split(h, 2, axis=-1)
            y = jnp.einsum('bsh,hd->bsd', a * jax.nn.silu(g), down_w[e])
            out = jnp.where((ids == e)[..., None], y, out)
        return out + skip
    x = x + _L0_xattn_ref(_layernorm(x, axis=-1), ctx_1024, L0_xattn_Wq, L0_xattn_bq, L0_xattn_Wk, L0_xattn_bk, L0_xattn_Wv, L0_xattn_bv, L0_xattn_Wp, L0_xattn_bp)
    x = x + _L0_ffn_ref(_layernorm(x, axis=-1), L0_ffn_fast_b, L0_ffn_w_fc, L0_ffn_w_proj, L0_ffn_u, L0_ffn_v, L0_ffn_gate)
    x = x + _L1_xattn_ref(_layernorm(x, axis=-1), ctx_1024, ctx_1024, mask_SxS2_ik1, L1_xattn_Wq, L1_xattn_Wk, L1_xattn_Wv)
    x = x + _L1_ffn_ref(_layernorm(x, axis=-1), L1_ffn_Wg, L1_ffn_gamma, L1_ffn_beta, L1_ffn_W1, L1_ffn_b1, L1_ffn_W2, L1_ffn_b2)
    x = x + _L2_xattn_ref(ctx_1024, _layernorm(x, axis=-1), ctx_1024, mask_1x1xSxS2_ik0, L2_xattn_Wq, L2_xattn_Wk, L2_xattn_Wv, L2_xattn_Wo, L2_xattn_bo)
    x = x + _L2_ffn_ref(_layernorm(x, axis=-1), L2_ffn_norm_g, L2_ffn_norm_b, L2_ffn_slot_g, L2_ffn_slot_b, L2_ffn_scale, L2_ffn_slot_embeds, L2_ffn_Wg, L2_ffn_bg, L2_ffn_Wu, L2_ffn_bu, L2_ffn_Wd, L2_ffn_bd)
    x = x + _L3_xattn_ref(_layernorm(x, axis=-1), ctx_1024, ctx_1024, itok_BxS2_0_2047, itok_BxS2_0_2047, L3_xattn_Wq, L3_xattn_bq, L3_xattn_Wk, L3_xattn_bk, L3_xattn_Wv, L3_xattn_bv, L3_xattn_Wo, L3_xattn_bo)
    x = x + _L3_ffn_ref(_layernorm(x, axis=-1), L3_ffn_scale, L3_ffn_centroids, L3_ffn_up_w, L3_ffn_down_w)
    return x

_drawn_inputs = setup_inputs


def setup_inputs(seed=0):
    import zlib

    import numpy as np

    out = dict(_drawn_inputs(seed))
    spreads = {'L0_xattn_bq': (0.0, 0.1),
     'L0_xattn_bk': (0.0, 0.552),
     'L0_xattn_bv': (0.0, 0.1),
     'L0_xattn_bp': (0.0, 0.1),
     'L1_ffn_gamma': (1.0, 0.2),
     'L1_ffn_beta': (0.0, 0.1),
     'L1_ffn_b1': (0.0, 0.1),
     'L1_ffn_b2': (0.0, 0.1),
     'L2_ffn_norm_g': (1.0, 0.2),
     'L2_ffn_norm_b': (0.0, 0.1),
     'L2_ffn_slot_g': (1.0, 0.2),
     'L2_ffn_slot_b': (0.0, 0.27),
     'L2_ffn_bg': (0.0, 0.294),
     'L2_ffn_bu': (0.0, 0.294),
     'L2_ffn_bd': (0.0, 0.1),
     'L3_xattn_bq': (0.0, 0.458),
     'L3_xattn_bk': (0.0, 2.0),
     'L3_xattn_bv': (0.0, 0.1),
     'L3_xattn_bo': (0.0, 0.1),
     'L3_ffn_scale': (1.0, 0.2)}
    factors = {'L0_ffn_fast_b': 8.0, 'L0_ffn_u': 8.0, 'L0_ffn_v': 8.0, 'L2_xattn_bo': 5.703}
    for name, (base, spread) in spreads.items():
        noise = np.random.default_rng([zlib.crc32(name.encode()), seed]).standard_normal(out[name].shape)
        drawn = base * np.exp(spread * noise) if base else spread * noise
        out[name] = jnp.asarray(drawn.astype(out[name].dtype))
    for name, factor in factors.items():
        out[name] = (out[name] * factor).astype(out[name].dtype)
    return out
```

```python
from contextlib import ExitStack

import concourse.bass as bass
from concourse import mybir

F32 = mybir.dt.float32
BF16 = mybir.dt.bfloat16
F16 = mybir.dt.float16
I32 = mybir.dt.int32
ALU = mybir.AluOpType
ACT = mybir.ActivationFunctionType
AX = mybir.AxisListType

NBATCH, N, D = 32, 128, 128
S2 = 120
NB = 4
G = NBATCH // NB
T = NB * N
H, HD = 16, 8
E1, F1 = 8, 512
E2, SL2, F2 = 16, 64, 256
NS = E2 * SL2
E3, F3 = 8, 256
F0 = 512
HU = 8
UNITS = NB * H // HU
LN_EPS = 1e-5
BIG = 1e30

PER = {}


def per(phase, **counts):
    for name, n in counts.items():
        PER[f"{phase}_{name}"] = n


per("a1", ct_ps=1, ct=1, mv=6, rs=6, xn=3, xn_ps=3, xnt=3,
    xb=1, kv_ps=2, kv_sb=1, q_ps=1, q=3, exp=1, qk=3,
    kvs_ps=2, qt_ps=1, kvm=1, qt=1, num_ps=2, o=3, ot_ps=1, ot=1, proj_ps=1, x=2,
    h_ps=4, relu=4, sq=4, dn_ps=1,
    v_ps=1, v_sb=1, t_ps=1, t_sb=1, s_ps=1, nm=2, p=1, rsm=1, pt_ps=1, pt=1, pv_ps=1, done=1)
per("at", mv=2, rs=2, xn=1, xn_ps=1, xnt=1, xb=1, q_ps=1, qt=1,
    v=2, kb=NB, s_ps=UNITS, sub=2 * UNITS, exp=UNITS, et_ps=UNITS, eth=UNITS, etl=UNITS,
    pv_ps=UNITS, on=2 * UNITS, ot_ps=1, ot=1, proj_ps=1)
per("a2", done=1)
per("a3", k_ps=1, kt=1, v_ps=1, v32=1, done=1)
per("mn", mv=2, rs=6, xn=1, xh=1, xh_ps=1)
per("m1", xx=1, xn_ps=1, xht=2, sc_ps=1, top=19, e2=1, cw_ps=1, cwt=1, cb_ps=E1, ring=5 * E1,
    up_ps=4 * E1, dn_ps=4 * E1, t=E1, acc=E1 - 1, y_ps=1, done=1)
per("m2", xpt=1, lt_ps=8, nm=8, ex=8, rz=8, ed=8, pd_ps=8, pd=8, sl_ps=8, sl=8,
    gu_ps=2 * E2, gelu=2 * E2, ht=2 * E2, dn_ps=E2, eo=E2, es_ps=8, es=8,
    l_ps=NB, nr=NB + 1, ec=NB, ct_ps=2 * NB, ctt=2 * NB, cm_ps=NB, done=1)
per("m3", xx=1, xpt=2, ds_ps=1, top=6, oh_ps=1, oht=1, mk_ps=E3, mk=E3, xm=E3, up_ps=2 * E3,
    silu=2 * E3, hm=2 * E3, dn_ps=2 * E3, yt=1, y_ps=1, out=1)
PER["m3_stored"] = 16
BASE = dict(m3_out=1, m3_stored=1)
TURNS = dict(a1=2, at=4, a2=2, a3=2, mn=6, m1=2, m2=2, m3=2)
START = dict(a2=dict(at=0), a3=dict(at=2), m1=dict(mn=0), m2=dict(mn=2), m3=dict(mn=4))

A1S = dict(ct_ps=0, rs0=1, ct=1, xn0=2, kv_ps=2, xn_ps0=3, kv_sb=3, xnt0=4, q_ps=5, q_sb=6, exp=7, qk=8, kvs_ps=9,
           kvm=10, qt=10, num_ps=11, o=12, ot_ps=13, ot=14, proj_ps=15, x0=16, rs1=17, xn1=18, xn_ps1=19, xnt1=20,
           h01=21, relu01=22, h23=22, relu23=23, dn_ps=24, x1=25, rs2=26, xn2=27, xn_ps2=28, xnt2=29, v_ps=30,
           t_sb=31, s_ps=32, nm=33, p=34, pt_ps=35, pt=36, pv_ps=37, done=38)
A1N = 39
ATN = 7 + 4 * (UNITS - 1) + 6 + 1 + 4
M1N = 11 + 4 * (E1 + 1) + 2
M2E = 5 + 3 * 7 + 7 + 1
M2C = M2E + 3 * (E2 + 2)
M2N = M2C + 3 * NB + 1
M3N = 11 + 4 * E3 + 2 + 2


def weave(moe, att):
    (ng, nn), (ag, an) = moe, att
    a = 0
    for n in range(nn):
        next(ng, None)
        while a < an and a * nn <= (n + 0.5) * an:
            next(ag, None)
            a += 1
    for g in (ng, ag):
        for _ in g:
            raise AssertionError("a phase has more steps than it says")


def alone(phase):
    gen, n = phase
    for _ in gen:
        pass


class Pair:

    def __init__(self, eng, i):
        self.eng, self.i, self.n = eng, i, 0
        self.regs = [eng.alloc_register(f"value{k}") for k in range(4)]

    def times(self, a, b):
        reg = self.regs[self.n % len(self.regs)]
        self.n += 1
        self.eng.reg_mul(reg, self.i, a)
        self.eng.reg_add(reg, reg, b)
        return reg



def build(nc, t, out, groups=G, stop=8):
    ctx = ExitStack()
    with ctx:
        def sb(name, shape, dt=F32):
            return ctx.enter_context(nc.sbuf_tensor(name, shape, dt))

        sem = {name: ctx.enter_context(nc.semaphore(name)) for name in PER}
        x_in = [ctx.enter_context(nc.semaphore(f"x{p}_in")) for p in range(2)]
        c_in = [ctx.enter_context(nc.semaphore(f"c{p}_in")) for p in range(2)]
        setup = {name: ctx.enter_context(nc.semaphore("setup_" + name)) for name in (
            "small_in", "mat_in", "slot_in", "w1_in", "w2_in", "l2_in", "l3_in", "m8", "iota", "ps", "sb",
            "act", "slot_rs", "bc_in", "va")}

        W1 = sb("W1", [D, E1, F1])
        W2 = sb("W2", [128, E1, F1 // 128, D])
        WG = sb("WG", [D, E2, F2])
        WU = sb("WU", [D, E2, F2])
        WD = sb("WD", [128, E2, F2 // 128, D])
        WA = sb("WA", [D, E3, 2 * F3])
        WB = sb("WB", [128, E3, F3 // 128, D])
        SET = sb("SET", [D, NS])
        WFC = sb("WFC", [D, F0])
        WPJ = sb("WPJ", [128, F0 // 128, D])
        WT0 = sb("WT0", [D, 4, D])
        WT1 = sb("WT1", [D, 2, D])
        A1 = sb("A1", [D, D])
        BDA = sb("BDA", [D, D])
        W2O = sb("W2O", [D, D])
        W3 = sb("W3", [D, 4, D])
        BC = sb("BC", [128, 7, D])
        BQ0, BK0, BV0, BP0, BO2, BV3, BO3 = range(7)
        VT1 = sb("VT1", [D, 96])
        VT2 = sb("VT2", [D, 64])
        WGT = sb("WGT", [D, E1])
        B1P = sb("B1P", [128, 4 * E1])
        CM2 = sb("CM2", [D, E3])
        CSQ = sb("CSQ", [D, E3])
        SGB = sb("SGB", [D, 2])
        SCL = sb("SCL", [128, 2])
        IDN = sb("IDN", [128, 128])
        IDB = sb("IDB", [128, 128], BF16)
        ONE = sb("ONE", [128, E3])
        BD = sb("BD", [128, H, HD])
        M8 = sb("M8", [128, HU])
        E8 = sb("E8", [HD, H, HD])
        RANK = sb("RANK", [128, E1])
        EPS = sb("EPS", [128, 2, NB])
        PASS = sb("PASS", [128, 3])
        EXPO = sb("EXPO", [128, 8])
        MB1 = sb("MB1", [128, S2])
        MB2 = sb("MB2", [128, S2], BF16)

        X = [sb(f"X{p}", [128, NB, D]) for p in range(2)]
        C = [sb(f"C{p}", [S2, NB, D]) for p in range(2)]
        CT = [sb(f"CT{p}", [D, NB, S2]) for p in range(2)]

        AN = sb("AN", [128, NB, D])
        ANT = sb("ANT", [128, NB, D])
        AQT = sb("AQT", [128, NB, D])
        AST = sb("AST", [128, NB, 6])
        AMV = sb("AMV", [128, NB, 2])
        AVE = sb("AVE", [128, NB])
        ARS = sb("ARS", [128, NB])
        AA = sb("AA", [128, 5888])
        VAH = sb("VAH", [S2, NB, H, HD + 1], F16)
        VAL = sb("VAL", [S2, NB, H, HD + 1], F16)

        def aa(at, n, *shape):
            ap = AA[:, at:at + n]
            if len(shape) == 2:
                ap = ap.rearrange("p (a b) -> p a b", a=shape[0])
            if len(shape) == 3:
                ap = ap.rearrange("p (a b c) -> p a b c", a=shape[0], b=shape[1])
            return ap

        QK = aa(0, 1024, 2, NB, D)
        VV = sb("VV", [128, NB, D + 1])
        KVM = aa(1600, NB * 144, NB, 144)
        QKM = aa(2240, 128)
        QKS = aa(2368, 128)
        QKR = aa(2496, 128)
        OO = aa(2624, 512, NB, D)
        DIN = aa(3136, NB * H, NB, H)
        R1 = aa(0, 1024, 2, T)
        R2 = aa(1024, 2048, 4, T)
        SS = aa(3072, NB * S2, NB, S2)
        PTT = aa(3584, 512, NB, N)
        V1 = aa(4096, 512, NB, D)
        NM1 = aa(4608, NB)
        SM1 = aa(4616, NB)
        RM1 = aa(4624, NB)
        KB = [aa(0, HU * S2, HU, S2), aa(960, HU * S2, HU, S2)]
        EE = [aa(1920, HU * S2, HU, S2), aa(2880, HU * S2, HU, S2)]
        ETH = [aa(3840 + 512 * r, 512).bitcast(F16).rearrange("p (h n) -> p h n", h=HU) for r in range(2)]
        ETL = [aa(4864 + 512 * r, 512).bitcast(F16).rearrange("p (h n) -> p h n", h=HU) for r in range(2)]
        V32 = aa(1920, 512, NB, D)
        MXU = sb("MXU", [128, 2, HU])
        RDU = sb("RDU", [128, 2, HU])
        OB = AN

        MN = sb("MN", [128, NB, D])
        MH = sb("MH", [128, NB, D])
        MHT = sb("MHT", [128, NB, D])
        MST = sb("MST", [128, NB, 6])
        MMV = sb("MMV", [128, NB, 2])
        MVE = sb("MVE", [128, NB])
        MRS = sb("MRS", [128, NB])
        MF = sb("MF", [128, 3, NB])
        SMALL = sb("SMALL", [128, 13, NB, E1])
        SM4 = sb("SM4", [128, 8, NB])
        MA = sb("MA", [128, 7168])

        def ma(at, n, *shape):
            ap = MA[:, at:at + n]
            if len(shape) == 2:
                ap = ap.rearrange("p (a b) -> p a b", a=shape[0])
            if len(shape) == 3:
                ap = ap.rearrange("p (a b c) -> p a b c", a=shape[0], b=shape[1])
            return ap

        CBC = ma(0, 4096, E1, T)
        MNT = ma(4096, 512, NB, D)
        HID = ma(4608, 2048, 4, T)
        YT = ma(4096, 512)
        ACC = MH
        CWT = ma(6656, 512)
        SL = ma(0, 4096, E2, NB, SL2)
        ES = ma(0, 4096, 8, NB, D)
        ED = [ma(4096 + 512 * i, 512, NB, N) for i in range(2)]
        PD = [ma(5120 + 512 * i, 512, NB, N) for i in range(2)]
        GL = ma(4096, 512, 2, NB * SL2)
        HT = [ma(4608 + 512 * i, 512, 2, NB * SL2) for i in range(2)]
        EO = [ma(5632 + 512 * i, 512, NB, 2 * SL2) for i in range(2)]
        EC = ma(4096, 1024)
        CTT = [ma(5120 + 1024 * i, 1024, 8, N) for i in range(2)]
        NM2 = sb("NM2", [128, 8, NB])
        ZZ2 = sb("ZZ2", [128, 8, NB])
        RZ2 = sb("RZ2", [128, 8, NB])
        NR2 = sb("NR2", [128, 3, NB])
        MK = ma(0, 2048).bitcast(BF16).rearrange("p (e n) -> p e n", e=E3)
        XM = [ma(2048 + 512 * i, 512) for i in range(2)]
        SG = [ma(3072 + 512 * i, 512) for i in range(2)]
        HM = [ma(4096 + 512 * i, 512) for i in range(4)]
        SQT = ma(6144, 512, NB, N)
        YT3 = ma(6656, 512, NB, N)
        OHT = ma(3584, 256).bitcast(BF16)

        RAW = ma(0, 1024, 8, D)
        RW0Q, RW0K, RW0V, RW0P, RW1V, RW2O, RW1Q, RW1K = range(8)
        RFC = ma(1024, 512, 4, D)
        RPJ = ma(1536, 512, 4, 128)
        RU = ma(2048, 64, 4, 16)
        RFB = ma(2112, 16)
        RVV = ma(2128, 128)
        R8 = ma(2256, 24, 3, HD)
        UT = ma(2304, 512, 4, 128)
        FBT = ma(2816, 16)
        FBV = ma(2832, 128)
        A8 = ma(2960, HD)
        BDV = ma(2968, 128)
        TP = ma(3104, 512, 4, D)
        TM = ma(3616, 512, 4, D)
        BSC = ma(4128, 16)
        SE = ma(4160, 1024, 8, D)
        VEC1 = ma(5184, 128)
        VEC2 = ma(5312, 128)
        MKI = ma(5440, 240).bitcast(I32).rearrange("p (a b) -> p a b", a=2)
        SST = ma(5680, 48, 8, 6)
        SMV = ma(5728, 16, 8, 2)
        SVE = ma(5744, 8)
        SRS = ma(5752, 8)
        MKF = ma(5760, S2)

        PS = ctx.enter_context(nc.psum_tensor("PS", [128, 8, 512], F32))

        def bank(k, lo=0, hi=512, rows=128):
            return PS[0:rows, k, lo:hi]

        def bank4(k, n=128, rows=128):
            return PS[0:rows, k, 0:4 * n].rearrange("p (b n) -> p b n", b=4)

        IDX = IDN[:, :]
        VC = {}
        at = 0
        for name, n in (("gamma", 8), ("beta", 8), ("b2", 8), ("b1", 32), ("norm_g", 1), ("norm_b", 1), ("slot_g", 1),
                        ("slot_b", 1), ("bq3", 1), ("bk3", 1), ("scale3", 1), ("bd", 16), ("cent", 8)):
            VC[name] = at
            at += n
        NV1 = at

        def vec(name, k=0):
            return VT1[:, VC[name] + k:VC[name] + k + 1]

        def turn(g, phase="a1"):
            i, off = g

            def v(name, k):
                n, turns = PER[name], TURNS[name[:2]]
                k = k + BASE.get(name, 0)
                t = turns * (off // 2) + START.get(phase, {}).get(name[:2], 0) + off % 2
                return t * n + k if i is None else i.times(turns * n, t * n + k)
            return v

        block = ctx.enter_context(nc.Block())

        def phases(eng, a1, m1, a2, m2, a3, m3, between=None):
            pairs = groups // 2

            def pair(i, last):
                def group(k):
                    return (None, 2 * i + k) if isinstance(i, int) else (i, k)
                A, B = group(0), group(1)
                weave(m1(A, 0, ("m3_out", group(-1))), a1(B, 1, ("a1_done", A)))
                weave(m1(B, 1, ("m1_done", A)), a2(A, 0, ("a1_done", B)))
                weave(m2(A, 0, ("m1_done", B)), a2(B, 1, ("a2_done", A)))
                weave(m2(B, 1, ("m2_done", A)), a3(A, 0, ("a2_done", B)))
                weave(m3(A, 0, ("m2_done", B)), a3(B, 1, ("a3_done", A)))
                if last:
                    alone(m3(B, 1, ("m3_out", A)))
                else:
                    weave(m3(B, 1, ("m3_out", A)), a1(group(2), 0, ("a3_done", B)))

            alone(a1((None, 0), 0, None))
            if between is not None:
                between()
            if pairs > 1:
                with eng.Fori(0, pairs - 1) as i:
                    pair(Pair(eng, i), False)
            pair(pairs - 1, True)

        def last_of(eng, name, g):
            if g[0] is not None or g[1] >= 0:
                eng.wait_ge(sem[name], turn(g)(name, PER[name]))

        def first(eng, g, prev, *own):
            for name, k in own:
                eng.wait_ge(sem[name], turn(g)(name, k))
            if prev is not None:
                last_of(eng, *prev)

        def arrived(eng, sems, g, p):
            i, off = g
            eng.wait_ge(sems[p], 16 * (off // 2 + 1) if i is None else i.times(16, 16 * (off // 2 + 1)))

        @block.gpsimd
        def _(pool):
            pool.memset(IDN[:, :], 0.0)
            pool.memset(IDB[:, :], 0.0)
            pool.memset(ONE[:, :], 1.0)
            pool.memset(BD[:, :, :], 1.0)
            pool.memset(E8[:, :, :], 0.0)
            pool.memset(EXPO[:, :], -0.5)
            pool.memset(EPS[:, 0, :], LN_EPS)
            pool.memset(EPS[:, 1, :], 1e-6)
            pool.memset(QK[:, :, :, :], 0.0)
            pool.memset(VV[:, :, D:D + 1], 1.0)
            pool.memset(VAH[:, :, :, HD:HD + 1], 1.0)
            pool.memset(VAL[:, :, :, HD:HD + 1], 0.0).then_inc(setup["iota"], 1)
            pool.iota(RANK[:, :], [[-1, E1]], base=E1, channel_multiplier=0,
                      allow_small_or_imprecise_dtypes=True).then_inc(setup["iota"], 1)
            pool.wait_ge(setup["iota"], 2)
            for m in (IDN, IDB):
                pool.affine_select(out=m[:, :], in_=m[:, :], compare_op=ALU.not_equal, fill=1.0, base=0,
                                   pattern=[[-1, 128]], channel_multiplier=1)
            pool.affine_select(out=E8[:, :, :], in_=E8[:, :, :], compare_op=ALU.not_equal, fill=1.0, base=0,
                               pattern=[[0, H], [-1, HD]], channel_multiplier=1)
            pool.affine_select(out=BD[:, :, :], in_=BD[:, :, :], compare_op=ALU.is_ge, fill=0.0, base=0,
                               pattern=[[-HD, H], [0, HD]], channel_multiplier=1).then_inc(setup["iota"], 1)
            pool.wait_ge(setup["iota"], 3)
            pool.affine_select(out=BD[:, :, :], in_=BD[:, :, :], compare_op=ALU.is_ge, fill=0.0, base=HD - 1,
                               pattern=[[HD, H], [0, HD]], channel_multiplier=-1).then_inc(setup["iota"], 1)
            pool.wait_ge(setup["sb"], 1)
            pool.tensor_scalar(SVE[:, :], SMV[:, :, 1], LN_EPS, None, ALU.add).then_inc(setup["slot_rs"], 1)
            pool.wait_ge(setup["slot_rs"], 1)
            pool.tensor_tensor(SRS[:, :], SVE[:, :], EXPO[:, 0:8], ALU.pow).then_inc(setup["slot_rs"], 1)

            def rstd(v, fam, j, ve, rs, mv):
                pool.wait_ge(sem[f"{fam}_mv"], v(f"{fam}_mv", 2 * j + 2))
                pool.tensor_tensor(ve[:, :], mv[:, :, 1], EPS[:, 0, :], ALU.add).then_inc(sem[f"{fam}_rs"], 1)
                pool.wait_ge(sem[f"{fam}_rs"], v(f"{fam}_rs", 2 * j + 1))
                pool.tensor_tensor(rs[:, :], ve[:, :], EXPO[:, 0:NB], ALU.pow).then_inc(sem[f"{fam}_rs"], 1)

            def renorm(v, eps):
                pool.wait_ge(sem["mn_rs"], v("mn_rs", 2))
                pool.tensor_tensor(MF[:, 0, :], MRS[:, :], MRS[:, :], ALU.mult).then_inc(sem["mn_rs"], 1)
                pool.wait_ge(sem["mn_rs"], v("mn_rs", 3))
                pool.tensor_tensor(MF[:, 1, :], MF[:, 0, :], MMV[:, :, 1], ALU.mult).then_inc(sem["mn_rs"], 1)
                pool.wait_ge(sem["mn_rs"], v("mn_rs", 4))
                pool.tensor_tensor(MF[:, 0, :], MF[:, 1, :], EPS[:, eps, :], ALU.add).then_inc(sem["mn_rs"], 1)
                pool.wait_ge(sem["mn_rs"], v("mn_rs", 5))
                pool.tensor_tensor(MF[:, 2, :], MF[:, 0, :], EXPO[:, 0:NB], ALU.pow).then_inc(sem["mn_rs"], 1)

            def a1(g, p, prev):
                v = turn(g)

                def run():
                    first(pool, g, prev)
                    arrived(pool, x_in, g, p)
                    if prev is None:
                        pool.wait_ge(setup["bc_in"], 16 * 9)
                    yield
                    for s in range(1, A1N):
                        if s == A1S["xn0"]:
                            pool.wait_ge(sem["a1_xn"], v("a1_xn", 1))
                            pool.tensor_tensor(X[p][:, :, :], X[p][:, :, :], BC[:, BP0, :].unsqueeze(1).to_broadcast([128, NB, D]),
                                               ALU.add).then_inc(sem["a1_xb"], 1)
                        if s in (A1S["rs0"], A1S["rs1"], A1S["rs2"]):
                            rstd(v, "a1", (A1S["rs0"], A1S["rs1"], A1S["rs2"]).index(s), AVE, ARS, AMV)
                        yield
                return run(), A1N

            def attention(ph, g, p, prev):
                v = turn(g, ph)

                def run():
                    first(pool, g, prev, ("m1_done" if ph == "a2" else "m2_done", 1))
                    yield
                    rstd(v, "at", 0, AVE, ARS, AMV)
                    yield
                    pool.wait_ge(sem["at_xn"], v("at_xn", 1))
                    bo = BO2 if ph == "a2" else BO3
                    pool.tensor_tensor(X[p][:, :, :], X[p][:, :, :], BC[:, bo, :].unsqueeze(1).to_broadcast([128, NB, D]),
                                       ALU.add).then_inc(sem["at_xb"], 1)
                    for s in range(2, ATN):
                        if s == 4:
                            v32 = C[p] if ph == "a2" else V32
                            if ph == "a3":
                                pool.wait_ge(sem["a3_v32"], v("a3_v32", 1))
                            src = v32[0:S2, :, :].rearrange("p b (h d) -> p (b h) d", h=H)
                            high = VAH[:, :, :, 0:HD].rearrange("p b h d -> p (b h) d")
                            low = VAL[:, :, :, 0:HD].rearrange("p b h d -> p (b h) d")
                            pool.tensor_tensor(high, src, ONE[0:S2, :].unsqueeze(1).to_broadcast([S2, NB * H, HD]),
                                               ALU.mult).then_inc(sem["at_v"], 1)
                            pool.wait_ge(sem["at_v"], v("at_v", 1))
                            pool.tensor_tensor(low, src, high, ALU.subtract).then_inc(sem["at_v"], 1)
                        for b in range(NB):
                            if s == (5 + 8 * b if b else 3):
                                if b >= 2:
                                    pool.wait_ge(sem["at_s_ps"], v("at_s_ps", 2 * b - 2))
                                if ph == "a3":
                                    pool.wait_ge(sem["a3_kt"], v("a3_kt", 1))
                                pool.tensor_tensor(KB[b % 2][:, :, :], CT[p][:, b, :].unsqueeze(1).to_broadcast([128, HU, S2]),
                                                   M8[:, :].unsqueeze(2).to_broadcast([128, HU, S2]),
                                                   ALU.mult).then_inc(sem["at_kb"], 1)
                        yield
                return run(), ATN

            def m1(g, p, prev):
                v = turn(g, "m1")

                def run():
                    first(pool, g, prev)
                    yield
                    rstd(v, "mn", 0, MVE, MRS, MMV)
                    renorm(v, 1)
                    yield
                    pool.wait_ge(sem["mn_xn"], v("mn_xn", 1))
                    pool.tensor_tensor(X[p][:, :, :], X[p][:, :, :], MN[:, :, :], ALU.add).then_inc(sem["m1_xx"], 1)
                    for s in range(2, M1N):
                        yield
                return run(), M1N

            def m2(g, p, prev):
                v = turn(g, "m2")

                def run():
                    first(pool, g, prev)
                    yield
                    rstd(v, "mn", 0, MVE, MRS, MMV)
                    renorm(v, 0)
                    yield
                    for s in range(2, M2N):
                        k, j = divmod(s - 5 - 3, 3)
                        if j == 0 and 0 <= k < 8:
                            pool.wait_ge(sem["m2_rz"], v("m2_rz", k + 1))
                            pool.tensor_tensor(ED[k % 2][:, :, :], ED[k % 2][:, :, :],
                                               RZ2[:, k, :].unsqueeze(2).to_broadcast([128, NB, N]),
                                               ALU.mult).then_inc(sem["m2_ed"], 1)
                        yield
                return run(), M2N

            def m3(g, p, prev):
                v = turn(g, "m3")

                def run():
                    first(pool, g, prev)
                    yield
                    rstd(v, "mn", 0, MVE, MRS, MMV)
                    renorm(v, 1)
                    yield
                    pool.wait_ge(sem["mn_xn"], v("mn_xn", 1))
                    pool.wait_ge(sem["mn_xh"], v("mn_xh", 1))
                    pool.tensor_tensor(MN[:, :, :], X[p][:, :, :], MN[:, :, :], ALU.add).then_inc(sem["m3_xx"], 1)
                    for s in range(2, M3N):
                        yield
                return run(), M3N

            phases(pool, a1, m1, lambda *a: attention("a2", *a), m2, lambda *a: attention("a3", *a), m3)

        @block.scalar
        def _(act):
            def copy(dst, src, name):
                act.activation(dst, src, ACT.Copy).then_inc(sem[name], 1)

            act.wait_ge(setup["ps"], 1)
            act.activation(WT0[:, :, :], bank4(0), ACT.Copy)
            act.activation(WT1[:, :, :], bank(1, 0, 256).rearrange("p (a b) -> p a b", a=2), ACT.Copy)
            act.activation(VT1[:, 0:NV1], bank(2, 0, NV1), ACT.Copy)
            act.activation(VT2[:, :], bank(2, 128, 192), ACT.Copy)
            act.activation(A1[:, :], bank(3, 0, 128), ACT.Copy).then_inc(setup["act"], 1)
            act.wait_ge(setup["ps"], 5)
            act.activation(WPJ[:, :, :], bank4(0), ACT.Copy)
            act.activation(WFC[:, :], bank(1), ACT.Copy)
            act.wait_ge(setup["ps"], 6)
            act.wait_ge(setup["sb"], 6)
            for k in range(2):
                last = act.activation(SET[:, 512 * k:512 * k + 512], bank(2 + k), ACT.Identity,
                                      bias=SGB[:, 1:2], scale=SGB[:, 0:1])
            last.then_inc(setup["act"], 1)

            def a1(g, p, prev):
                v = turn(g)

                def run():
                    first(act, g, prev)
                    for s in range(A1N):
                        if s == A1S["ct"]:
                            act.wait_ge(sem["a1_ct_ps"], v("a1_ct_ps", 1))
                            copy(CT[p][:, :, :], bank4(1, S2), "a1_ct")
                        for j in range(3):
                            if s == A1S[f"xnt{j}"]:
                                act.wait_ge(sem["a1_xn_ps"], v("a1_xn_ps", j + 1))
                                copy(ANT[:, :, :], bank4(1 if j == 0 else 0), "a1_xnt")
                        if s == A1S["exp"]:
                            act.wait_ge(sem["a1_q"], v("a1_q", 3))
                            act.activation(QK[:, :, :, :], QK[:, :, :, :], ACT.Exp).then_inc(sem["a1_exp"], 1)
                        if s == A1S["qt"]:
                            act.wait_ge(sem["a1_qt_ps"], v("a1_qt_ps", 1))
                            copy(AQT[:, :, :], bank4(2), "a1_qt")
                        if s == A1S["ot"]:
                            act.wait_ge(sem["a1_ot_ps"], v("a1_ot_ps", 1))
                            copy(ANT[:, :, :], bank4(2), "a1_ot")
                        if s in (A1S["relu01"], A1S["relu23"]):
                            for c in (0, 1) if s == A1S["relu01"] else (2, 3):
                                act.wait_ge(sem["a1_h_ps"], v("a1_h_ps", c + 1))
                                if c >= 2:
                                    act.wait_ge(sem["a1_sq"], v("a1_sq", c - 1))
                                act.activation(R1[:, c % 2, :], bank((1, 2, 3, 0)[c]), ACT.Relu).then_inc(sem["a1_relu"], 1)
                        if s == A1S["t_sb"]:
                            act.wait_ge(sem["a1_v_ps"], v("a1_v_ps", 1))
                            copy(V1[0:S2, :, :], bank4(2, D, S2), "a1_v_sb")
                            act.wait_ge(sem["a1_t_ps"], v("a1_t_ps", 1))
                            act.activation(AQT[:, :, :], bank4(1), ACT.Copy, scale=float(D) ** -0.5).then_inc(sem["a1_t_sb"], 1)
                        if s == A1S["p"]:
                            act.wait_ge(sem["a1_nm"], v("a1_nm", 2))
                            for b in range(NB):
                                last = act.activation(SS[:, b, :], SS[:, b, :], ACT.Exp, bias=NM1[:, b:b + 1],
                                                      accum_out=SM1[:, b:b + 1])
                            last.then_inc(sem["a1_p"], 1)
                        if s == A1S["pt"]:
                            act.wait_ge(sem["a1_pt_ps"], v("a1_pt_ps", 1))
                            copy(PTT[0:S2, :, :], bank4(0, N, S2), "a1_pt")
                        yield
                return run(), A1N

            def attention(ph, g, p, prev):
                v = turn(g, ph)

                def run():
                    first(act, g, prev)
                    for s in range(ATN):
                        if s == 4:
                            act.wait_ge(sem["at_xn_ps"], v("at_xn_ps", 1))
                            copy(ANT[:, :, :], bank4(0), "at_xnt")
                        if s == 2 and ph == "a3":
                            act.wait_ge(sem["a3_k_ps"], v("a3_k_ps", 1))
                            act.wait_ge(sem["a3_v_ps"], v("a3_v_ps", 1))
                            act.activation(CT[p][:, :, :], bank4(2, S2), ACT.Identity, bias=vec("bk3")).then_inc(sem["a3_kt"], 1)
                        if s == 6:
                            act.wait_ge(sem["at_q_ps"], v("at_q_ps", 1))
                            if ph == "a2":
                                copy(AQT[:, :, :], bank4(1), "at_qt")
                            else:
                                act.activation(AQT[:, :, :], bank4(1), ACT.Identity, bias=vec("bq3")).then_inc(sem["at_qt"], 1)
                        for u in range(UNITS):
                            r = u % 2
                            j = s - 7 - 4 * u
                            if j == 2:
                                act.wait_ge(sem["at_sub"], v("at_sub", 2 * u + 2))
                                act.activation(EE[r][:, :, :], EE[r][:, :, :], ACT.Exp,
                                               scale=float(HD) ** -0.5).then_inc(sem["at_exp"], 1)
                            if j == 4:
                                act.wait_ge(sem["at_et_ps"], v("at_et_ps", u + 1))
                                if u >= 2:
                                    act.wait_ge(sem["at_pv_ps"], v("at_pv_ps", u - 1))
                                act.activation(ETH[r][0:S2].rearrange("p (a h) n -> p a (h n)", a=2), PS[0:S2, 2 * r:2 * r + 2, :],
                                               ACT.Copy).then_inc(sem["at_eth"], 1)
                        if s == ATN - 3:
                            act.wait_ge(sem["at_ot_ps"], v("at_ot_ps", 1))
                            copy(ANT[:, :, :], bank4(0), "at_ot")
                        yield
                return run(), ATN

            def m1(g, p, prev):
                v = turn(g, "m1")

                def run():
                    first(act, g, prev)
                    for s in range(M1N):
                        if s == 4:
                            act.wait_ge(sem["m1_xn_ps"], v("m1_xn_ps", 1))
                            copy(MNT[:, :, :], bank4(5), "m1_xht")
                            act.wait_ge(sem["mn_xh_ps"], v("mn_xh_ps", 1))
                            copy(MHT[:, :, :], bank4(6), "m1_xht")
                        if s == 7:
                            act.wait_ge(sem["m1_top"], v("m1_top", 14))
                            act.activation(SM4[:, 3, :], SM4[:, 2, :], ACT.Exp).then_inc(sem["m1_e2"], 1)
                        if s == 10:
                            act.wait_ge(sem["m1_cw_ps"], v("m1_cw_ps", 1))
                            copy(CWT[0:E1, :], bank(7, 0, T, E1), "m1_cwt")
                        if s >= 11:
                            e, c = divmod(s - 11, 4)
                            if e < E1:
                                act.wait_ge(sem["m1_up_ps"], v("m1_up_ps", 4 * e + c + 1))
                                if e:
                                    act.wait_ge(sem["m1_dn_ps"], v("m1_dn_ps", 4 * (e - 1) + c + 1))
                                act.activation(HID[:, c, :], bank(5 + (5 * e + c) % 3), ACT.Relu,
                                               bias=B1P[:, 4 * e + c:4 * e + c + 1]).then_inc(sem["m1_ring"], 1)
                                if c == 3:
                                    act.wait_ge(sem["m1_cb_ps"], v("m1_cb_ps", e + 1))
                                    act.activation(CBC[:, e, :], bank(5 + (5 * e + 4) % 3), ACT.Copy).then_inc(sem["m1_ring"], 1)
                        yield
                return run(), M1N

            def m2(g, p, prev):
                v = turn(g, "m2")

                def run():
                    first(act, g, prev)
                    for s in range(M2N):
                        if s == 4:
                            act.wait_ge(sem["mn_xh_ps"], v("mn_xh_ps", 1))
                            act.activation(MHT[:, :, :], bank4(5), ACT.Identity, bias=vec("norm_b"),
                                           scale=vec("norm_g")).then_inc(sem["m2_xpt"], 1)
                        k, j = divmod(s - 5 - 2, 3)
                        if j == 0 and 0 <= k < 8:
                            act.wait_ge(sem["m2_nm"], v("m2_nm", k + 1))
                            if k >= 2:
                                act.wait_ge(sem["m2_pd_ps"], v("m2_pd_ps", k - 1))
                            for b in range(NB):
                                last = act.activation(ED[k % 2][:, b, :], bank(4 + k % 2, 128 * b, 128 * b + 128), ACT.Exp,
                                                      bias=NM2[:, k, b:b + 1], accum_out=ZZ2[:, k, b:b + 1])
                            last.then_inc(sem["m2_ex"], 1)
                        k, j = divmod(s - 5 - 5, 3)
                        if j == 0 and 0 <= k < 8:
                            act.wait_ge(sem["m2_pd_ps"], v("m2_pd_ps", k + 1))
                            if k >= 2:
                                act.wait_ge(sem["m2_sl_ps"], v("m2_sl_ps", k - 1))
                            copy(PD[k % 2][:, :, :], bank4(6), "m2_pd")
                        e, j = divmod(s - M2E, 3)
                        if 0 <= e < E2 and j < 2:
                            act.wait_ge(sem["m2_gu_ps"], v("m2_gu_ps", 2 * e + j + 1))
                            if e:
                                act.wait_ge(sem["m2_ht"], v("m2_ht", 2 * (e - 1) + j + 1))
                            act.activation(GL[:, j, :], bank(4 + j, 0, 256), ACT.Gelu,
                                           bias=VT2[:, 2 * e + j:2 * e + j + 1]).then_inc(sem["m2_gelu"], 1)
                        if 1 <= e <= E2 and j == 2:
                            f = e - 1
                            act.wait_ge(sem["m2_dn_ps"], v("m2_dn_ps", f + 1))
                            if f >= 4:
                                act.wait_ge(sem["m2_es_ps"], v("m2_es_ps", f // 2 - 1))
                            act.activation(EO[f // 2 % 2][:, :, SL2 * (f % 2):SL2 * (f % 2) + SL2],
                                           bank(6, 0, 256).rearrange("p (b s) -> p b s", b=NB), ACT.Identity,
                                           bias=vec("bd", f)).then_inc(sem["m2_eo"], 1)
                        if j == 1 and e % 2 == 1 and 3 <= e <= 17:
                            k = (e - 3) // 2
                            act.wait_ge(sem["m2_es_ps"], v("m2_es_ps", k + 1))
                            copy(ES[:, k, :, :], bank4(7), "m2_es")
                        b, j = divmod(s - M2C, 3)
                        if 0 <= b < NB and j == 1:
                            act.wait_ge(sem["m2_nr"], v("m2_nr", b + 1))
                            if b:
                                act.wait_ge(sem["m2_ct_ps"], v("m2_ct_ps", 2 * b))
                            act.activation(EC.rearrange("p (a s) -> p a s", a=2), PS[:, 4:6, :], ACT.Exp,
                                           bias=NR2[:, 0, b:b + 1], accum_out=NR2[:, 1, b:b + 1]).then_inc(sem["m2_ec"], 1)
                            if b >= 2:
                                act.wait_ge(sem["m2_cm_ps"], v("m2_cm_ps", b - 1))
                            for h in range(2):
                                act.wait_ge(sem["m2_ct_ps"], v("m2_ct_ps", 2 * b + h + 1))
                                act.activation(CTT[b % 2][:, 4 * h:4 * h + 4, :], bank4(6), ACT.Copy).then_inc(sem["m2_ctt"], 1)
                        yield
                return run(), M2N

            def m3(g, p, prev):
                v = turn(g, "m3")

                def run():
                    first(act, g, prev)
                    for s in range(M3N):
                        if s == 4:
                            act.wait_ge(sem["mn_xh_ps"], v("mn_xh_ps", 1))
                            act.activation(MHT[:, :, :], bank4(5), ACT.Copy, scale=vec("scale3")).then_inc(sem["m3_xpt"], 1)
                            act.activation(SQT[:, :, :], bank4(5), ACT.Square, scale=vec("scale3")).then_inc(sem["m3_xpt"], 1)
                        if s == 8:
                            act.wait_ge(sem["m3_oh_ps"], v("m3_oh_ps", 1))
                            copy(OHT[0:E3, :], bank(5, 0, T, E3), "m3_oht")
                        if s == 10:
                            for e in range(E3):
                                act.wait_ge(sem["m3_mk_ps"], v("m3_mk_ps", e + 1))
                                copy(MK[:, e, :], bank(5 + e % 3), "m3_mk")
                        e, j = divmod(s - 11, 4)
                        if 0 <= e < E3 and j % 2 == 0:
                            n = 2 * e + j // 2
                            act.wait_ge(sem["m3_up_ps"], v("m3_up_ps", n + 1))
                            if n >= 2:
                                act.wait_ge(sem["m3_hm"], v("m3_hm", n - 1))
                            act.activation(SG[n % 2], bank(5 + 2 * n % 3), ACT.Silu).then_inc(sem["m3_silu"], 1)
                        if s == M3N - 3:
                            act.wait_ge(sem["m3_dn_ps"], v("m3_dn_ps", 2 * E3))
                            copy(YT3[:, :, :], bank4(4), "m3_yt")
                        yield
                return run(), M3N

            phases(act, a1, m1, lambda *a: attention("a2", *a), m2, lambda *a: attention("a3", *a), m3)

        @block.vector
        def _(dve):
            n_sb = [0]

            def did(ins):
                n_sb[0] += 1
                ins.then_inc(setup["va"], 1)
                dve.wait_ge(setup["va"], n_sb[0])

            dve.memset(PASS[:, 0:1], 0.0).then_inc(sem["m3_out"], BASE["m3_out"])
            dve.memset(PASS[:, 1:2], 0.0).then_inc(sem["m3_stored"], BASE["m3_stored"])
            dve.wait_ge(setup["iota"], 4)
            for r in range(2):
                last = dve.tensor_copy(M8[64 * r:64 * r + 64, :], BD[64 * r:64 * r + 64, HU * r:HU * r + HU, 0])
            last.then_inc(setup["m8"], 1)
            dve.wait_ge(setup["slot_in"], 16)
            for k in range(8):
                last = dve.bn_stats(SST[:, k, :], SE[:, k, :])
            did(last)
            for k in range(8):
                last = dve.bn_aggr(SMV[:, k, :], SST[:, k, :])
            last.then_inc(setup["sb"], 1)
            dve.wait_ge(setup["small_in"], 16 * 10)
            dve.tensor_scalar(MB1[:, :], MKI[:, 0, :], 0.0, -BIG, ALU.is_equal, ALU.mult)
            did(dve.tensor_scalar(MB2[:, :], MKI[:, 1, :], 0.0, -1e20, ALU.is_equal, ALU.mult))
            dve.tensor_reduce(BSC[:, 0:4], RFC[:, :, :], AX.X, ALU.add, apply_absolute_value=True)
            did(dve.tensor_reduce(BSC[:, 4:5], RPJ[:, :, :], AX.XY, ALU.add, apply_absolute_value=True))
            dve.tensor_scalar(BSC[:, 0:4], BSC[:, 0:4], 1.0 / D, 1e-5, ALU.mult, ALU.max)
            did(dve.tensor_scalar(BSC[:, 4:5], BSC[:, 4:5], 1.0 / F0, 1e-5, ALU.mult, ALU.max))
            dve.tensor_scalar(BSC[:, 5:10], BSC[:, 0:5], 0.5, None, ALU.mult)
            did(dve.tensor_scalar(BSC[:, 10:15], BSC[:, 0:5], -0.5, None, ALU.mult))
            for raw, col in ((RFC, 0), (RPJ, 4)):
                for c in range(4):
                    k = col + c if raw is RFC else 4
                    dve.tensor_scalar(TP[:, c, :], raw[:, c, :], BSC[:, 5 + k:6 + k], None, ALU.is_gt)
                    last = dve.tensor_scalar(TM[:, c, :], raw[:, c, :], BSC[:, 10 + k:11 + k], None, ALU.is_lt)
                did(last)
                did(dve.tensor_tensor(TP[:, :, :], TP[:, :, :], TM[:, :, :], ALU.subtract))
                did(dve.tensor_tensor(TP[:, :, :], TP[:, :, :], raw[:, :, :], ALU.subtract))
                did(dve.tensor_tensor(TP[:, :, :], TP[:, :, :], raw[:, :, :], ALU.add))
                for c in range(4):
                    k = col + c if raw is RFC else 4
                    last = dve.tensor_scalar(raw[:, c, :], TP[:, c, :], BSC[:, k:k + 1], None, ALU.mult)
                did(last)
            dve.wait_ge(setup["ps"], 2)
            dve.tensor_copy(UT[0:16, :, :], bank4(4, 128, 16))
            dve.tensor_copy(FBT[0:16, :], bank(5, 0, 16, 16))
            dve.tensor_copy(A8[0:HD, :], bank(5, 32, 32 + HD, HD))
            dve.wait_ge(setup["m8"], 1)
            dve.tensor_tensor(BDV[:, :], bank(5, 128, 256), BD[:, :, :].rearrange("p h d -> p (h d)"),
                              ALU.mult).then_inc(setup["sb"], 1)
            dve.wait_ge(setup["ps"], 3)
            dve.tensor_copy(FBV[0:16, :], bank(6, 0, 128, 16))
            dve.tensor_copy(W2O[:, :], bank(6, 128, 256))
            dve.tensor_tensor(BDA[:, :], bank(6, 256, 384), BD[:, :, :].rearrange("p h d -> p (h d)"),
                              ALU.mult).then_inc(setup["sb"], 1)
            dve.wait_ge(setup["bc_in"], 16 * 9)
            dve.wait_ge(setup["ps"], 4)
            for c in range(4):
                last = dve.scalar_tensor_tensor(RFC[:, c, :], bank(7, 128 * c, 128 * c + 128), SCL[:, 0:1], RFC[:, c, :],
                                                ALU.mult, ALU.add)
            last.then_inc(setup["sb"], 1)
            dve.wait_ge(setup["slot_rs"], 2)
            for k in range(8):
                last = dve.tensor_scalar(SE[:, k, :], SE[:, k, :], SMV[:, k, 0:1], SRS[:, k:k + 1],
                                         ALU.subtract, ALU.mult)
            last.then_inc(setup["sb"], 1)
            dve.wait_ge(setup["act"], 1)
            dve.tensor_scalar(SGB[:, 0:1], vec("slot_g"), SCL[:, 1:2], None, ALU.mult)
            dve.tensor_scalar(SGB[:, 1:2], vec("slot_b"), SCL[:, 1:2], None, ALU.mult)
            dve.tensor_scalar(CM2[:, :], VT1[:, VC["cent"]:VC["cent"] + E3], -2.0, None, ALU.mult)
            dve.tensor_tensor(CSQ[:, :], VT1[:, VC["cent"]:VC["cent"] + E3], VT1[:, VC["cent"]:VC["cent"] + E3],
                              ALU.mult).then_inc(setup["sb"], 1)

            def scale_w1():
                dve.wait_ge(setup["ps"], 7)
                dve.tensor_tensor(B1P[:, :], bank(4, 0, 4 * E1), VT1[:, VC["b1"]:VC["b1"] + 4 * E1], ALU.add)
                for e in range(E1):
                    last = dve.tensor_scalar(W1[:, e, :], W1[:, e, :], vec("gamma", e), None, ALU.mult)
                last.then_inc(setup["sb"], 1)

            def stats(v, fam, j, x, st, mv):
                for b in range(NB):
                    last = dve.bn_stats(st[:, b, :], x[:, b, :])
                last.then_inc(sem[f"{fam}_mv"], 1)
                dve.wait_ge(sem[f"{fam}_mv"], v(f"{fam}_mv", 2 * j + 1))
                dve.memset(PASS[:, 2:3], 0.0)
                for b in range(NB):
                    last = dve.bn_aggr(mv[:, b, :], st[:, b, :])
                last.then_inc(sem[f"{fam}_mv"], 1)

            def norm(v, fam, j, x, xn, mv, rs):
                dve.wait_ge(sem[f"{fam}_rs"], v(f"{fam}_rs", 2 * j + 2))
                for b in range(NB):
                    last = dve.tensor_scalar(xn[:, b, :], x[:, b, :], mv[:, b, 0:1], rs[:, b:b + 1], ALU.subtract, ALU.mult)
                last.then_inc(sem[f"{fam}_xn"], 1)

            def a1(g, p, prev):
                v = turn(g)
                x = X[p]

                def after(name, k=1):
                    dve.wait_ge(sem["a1_" + name], v("a1_" + name, k))

                def run():
                    first(dve, g, prev)
                    arrived(dve, x_in, g, p)
                    if prev is None:
                        dve.wait_ge(setup["iota"], 2)
                    for s in range(A1N):
                        if s == A1S["ct_ps"]:
                            stats(v, "a1", 0, x, AST, AMV)
                        if s == A1S["xn0"]:
                            norm(v, "a1", 0, x, AN, AMV, ARS)
                        if s == A1S["kv_sb"]:
                            after("kv_ps", 1)
                            dve.tensor_tensor(QK[0:S2, 1, :, :], bank4(3, 128, S2),
                                              BC[0:S2, BK0, :].unsqueeze(1).to_broadcast([S2, NB, D]), ALU.add)
                            after("kv_ps", 2)
                            dve.tensor_tensor(VV[0:S2, :, 0:D], bank4(0, 128, S2),
                                              BC[0:S2, BV0, :].unsqueeze(1).to_broadcast([S2, NB, D]),
                                              ALU.add).then_inc(sem["a1_kv_sb"], 1)
                        if s == A1S["q_sb"]:
                            after("q_ps")
                            dve.tensor_tensor(QK[:, 0, :, :], bank4(2),
                                              BC[:, BQ0, :].unsqueeze(1).to_broadcast([128, NB, D]),
                                              ALU.add).then_inc(sem["a1_q"], 1)
                            qk = QK[:, :, :, :].rearrange("p a b (h d) -> p (a b h) d", h=H)
                            after("q", 1)
                            after("kv_sb")
                            dve.tensor_reduce(QKM[:, :], qk, AX.X, ALU.max).then_inc(sem["a1_q"], 1)
                            after("q", 2)
                            dve.tensor_tensor(qk, qk, QKM[:, :].unsqueeze(2).to_broadcast([128, 128, HD]),
                                              ALU.subtract).then_inc(sem["a1_q"], 1)
                        if s == A1S["qk"]:
                            qk = QK[:, :, :, :].rearrange("p a b (h d) -> p (a b h) d", h=H)
                            after("exp")
                            dve.tensor_reduce(QKS[:, :], qk, AX.X, ALU.add).then_inc(sem["a1_qk"], 1)
                            after("qk", 1)
                            dve.reciprocal(QKR[:, :], QKS[:, :]).then_inc(sem["a1_qk"], 1)
                            after("qk", 2)
                            dve.tensor_tensor(qk, qk, QKR[:, :].unsqueeze(2).to_broadcast([128, 128, HD]),
                                              ALU.mult).then_inc(sem["a1_qk"], 1)
                        if s == A1S["kvm"]:
                            for h in range(2):
                                after("kvs_ps", h + 1)
                                ps = bank((1, 3)[h]).rearrange("p (b n) -> p b n", b=2)
                                dve.tensor_tensor(KVM[:, 2 * h:2 * h + 2, 0:D], ps[:, :, 0:D],
                                                  BD[:, :, :].rearrange("p h d -> p (h d)").unsqueeze(1).to_broadcast([128, 2, D]),
                                                  ALU.mult)
                                last = dve.tensor_tensor(KVM[:, 2 * h:2 * h + 2, D:D + H], ps[:, :, D:D + 1].to_broadcast([128, 2, H]),
                                                         BD[:, :, 0].unsqueeze(1).to_broadcast([128, 2, H]), ALU.mult)
                            last.then_inc(sem["a1_kvm"], 1)
                        if s == A1S["o"]:
                            for h in range(2):
                                after("num_ps", h + 1)
                                ps = bank((0, 1)[h]).rearrange("p (b n) -> p b n", b=2)
                                last = dve.reciprocal(DIN[:, 2 * h:2 * h + 2, :], ps[:, :, D:D + H])
                            last.then_inc(sem["a1_o"], 1)
                            after("o", 1)
                            for h in range(2):
                                ps = bank((0, 1)[h]).rearrange("p (b n) -> p b n", b=2)
                                for b in range(2):
                                    last = dve.tensor_tensor(OO[:, 2 * h + b, :].rearrange("p (h d) -> p h d", h=H),
                                                             ps[:, b, 0:D].rearrange("p (h d) -> p h d", h=H),
                                                             DIN[:, 2 * h + b, :].unsqueeze(2).to_broadcast([128, H, HD]), ALU.mult)
                            last.then_inc(sem["a1_o"], 1)
                            after("o", 2)
                            dve.tensor_tensor(OO[:, :, :], OO[:, :, :], QK[:, 0, :, :], ALU.add).then_inc(sem["a1_o"], 1)
                        if s == A1S["x0"]:
                            after("proj_ps")
                            after("xb")
                            dve.tensor_tensor(x[:, :, :], bank4(3), x[:, :, :], ALU.add).then_inc(sem["a1_x"], 1)
                            after("x", 1)
                            stats(v, "a1", 1, x, AST, AMV)
                        if s == A1S["xn1"]:
                            norm(v, "a1", 1, x, AN, AMV, ARS)
                        if s in (A1S["relu01"], A1S["relu23"]):
                            for c in (0, 1) if s == A1S["relu01"] else (2, 3):
                                after("relu", c + 1)
                                dve.scalar_tensor_tensor(R2[:, c, :], bank((1, 2, 3, 0)[c]), 0.0, R1[:, c % 2, :],
                                                         ALU.max, ALU.mult).then_inc(sem["a1_sq"], 1)
                        if s == A1S["x1"]:
                            after("dn_ps")
                            dve.tensor_tensor(x[:, :, :], bank4(1), x[:, :, :], ALU.add).then_inc(sem["a1_x"], 1)
                            after("x", 2)
                            stats(v, "a1", 2, x, AST, AMV)
                        if s == A1S["xn2"]:
                            norm(v, "a1", 2, x, AN, AMV, ARS)
                        if s == A1S["nm"]:
                            after("s_ps")
                            dve.tensor_tensor(SS[:, :, :], bank4(3, S2), MB1[:, :].unsqueeze(1).to_broadcast([128, NB, S2]),
                                              ALU.add).then_inc(sem["a1_nm"], 1)
                            after("nm", 1)
                            dve.tensor_reduce(NM1[:, :], SS[:, :, :], AX.X, ALU.max, negate=True).then_inc(sem["a1_nm"], 1)
                        if s == A1S["pt"]:
                            after("p")
                            dve.reciprocal(RM1[:, :], SM1[:, :]).then_inc(sem["a1_rsm"], 1)
                        if s == A1S["done"]:
                            after("pv_ps")
                            after("rsm")
                            for b in range(NB):
                                last = dve.scalar_tensor_tensor(x[:, b, :], bank(1, 128 * b, 128 * b + 128), RM1[:, b:b + 1],
                                                                x[:, b, :], ALU.mult, ALU.add)
                            last.then_inc(sem["a1_done"], 1)
                        yield
                return run(), A1N

            def attention(ph, g, p, prev):
                v = turn(g, ph)
                x = X[p]

                def after(name, k=1):
                    own = ("a3_" if name in ("k_ps", "kt", "v_ps", "v32") else "at_") + name
                    dve.wait_ge(sem[own], v(own, k))

                def run():
                    first(dve, g, prev, ("m1_done" if ph == "a2" else "m2_done", 1))
                    for s in range(ATN):
                        if s == 0:
                            stats(v, "at", 0, x, AST, AMV)
                        if s == 2:
                            norm(v, "at", 0, x, AN, AMV, ARS)
                        if s == 3 and ph == "a3":
                            after("v_ps")
                            dve.tensor_tensor(V32[0:S2, :, :], bank4(3, 128, S2),
                                              BC[0:S2, BV3, :].unsqueeze(1).to_broadcast([S2, NB, D]),
                                              ALU.add).then_inc(sem["a3_v32"], 1)
                        for u in range(UNITS):
                            r, b = u % 2, u // 2
                            j = s - 7 - 4 * u
                            sp = PS[:, 2 * r:2 * r + 2, 0:4 * S2].rearrange("p a (h k) -> p a h k", h=4)
                            if j == 1:
                                after("s_ps", u + 1)
                                dve.tensor_reduce(MXU[:, r, :].rearrange("p (a h) -> p a h", a=2), sp, AX.X,
                                                  ALU.max).then_inc(sem["at_sub"], 1)
                                after("sub", 2 * u + 1)
                                if u >= 2:
                                    after("et_ps", u - 1)
                                elif ph == "a3":
                                    after("v", 2)
                                dve.tensor_tensor(EE[r][:, :, :].rearrange("p (a h) k -> p a h k", a=2), sp,
                                                  MXU[:, r, :].rearrange("p (a h) -> p a h", a=2).unsqueeze(3).to_broadcast([128, 2, 4, S2]),
                                                  ALU.subtract).then_inc(sem["at_sub"], 1)
                            if j == 4:
                                after("eth", u + 1)
                                dve.tensor_tensor(ETL[r][0:S2].rearrange("p (a h) n -> p a (h n)", a=2), PS[0:S2, 2 * r:2 * r + 2, :],
                                                  ETH[r][0:S2].rearrange("p (a h) n -> p a (h n)", a=2),
                                                  ALU.subtract).then_inc(sem["at_etl"], 1)
                            if j == 6:
                                after("pv_ps", u + 1)
                                o = bank(2 * r, 0, HU * (HD + 1)).rearrange("p (h d) -> p h d", h=HU)
                                dve.reciprocal(RDU[:, r, :], o[:, :, HD]).then_inc(sem["at_on"], 1)
                                after("on", 2 * u + 1)
                                dve.tensor_tensor(OB[:, b, 64 * r:64 * r + 64].rearrange("p (h d) -> p h d", h=HU), o[:, :, 0:HD],
                                                  RDU[:, r, :].unsqueeze(2).to_broadcast([128, HU, HD]),
                                                  ALU.mult).then_inc(sem["at_on"], 1)
                        if s == ATN - 1:
                            after("proj_ps")
                            after("xb")
                            dve.tensor_tensor(x[:, :, :], bank4(1), x[:, :, :], ALU.add).then_inc(sem[f"{ph}_done"], 1)
                        yield
                return run(), ATN

            def head(g, v, x, stored):
                yield
                yield
                if stored and (g[0] is not None or g[1] > 0):
                    dve.wait_ge(sem["m3_stored"], v("m3_stored", 0))
                norm(v, "mn", 0, x, MN, MMV, MRS)
                dve.wait_ge(sem["mn_rs"], v("mn_rs", 6))
                dve.wait_ge(sem["mn_xn"], v("mn_xn", 1))
                for b in range(NB):
                    last = dve.tensor_scalar(MH[:, b, :], MN[:, b, :], MF[:, 2, b:b + 1], None, ALU.mult)
                last.then_inc(sem["mn_xh"], 1)
                yield

            def m1(g, p, prev):
                v = turn(g, "m1")
                x = X[p]

                def after(name, k=1):
                    dve.wait_ge(sem["m1_" + name], v("m1_" + name, k))

                def link(ins, k):
                    ins.then_inc(sem["m1_top"], 1)
                    after("top", k)

                def run():
                    first(dve, g, prev, ("a1_done", 1))
                    stats(v, "mn", 0, x, MST, MMV)
                    yield from head(g, v, x, stored=(p == 0))
                    for s in range(3, M1N):
                        def wide(k):
                            return SM4[:, k, :].unsqueeze(2).to_broadcast([128, NB, E1])
                        if s == 6:
                            after("sc_ps")
                            rank = RANK[:, :].unsqueeze(1).to_broadcast([128, NB, E1])
                            link(dve.tensor_copy(SMALL[:, 0], bank(7, 0, NB * E1).rearrange("p (b e) -> p b e", b=NB)), 1)
                            link(dve.tensor_reduce(SM4[:, 0, :], SMALL[:, 0], AX.X, ALU.max), 2)
                            link(dve.tensor_tensor(SMALL[:, 1], SMALL[:, 0], wide(0), ALU.is_equal), 3)
                            link(dve.tensor_tensor(SMALL[:, 2], SMALL[:, 1], rank, ALU.mult), 4)
                            link(dve.tensor_reduce(SM4[:, 4, :], SMALL[:, 2], AX.X, ALU.max), 5)
                            link(dve.tensor_tensor(SMALL[:, 3], SMALL[:, 2], wide(4), ALU.is_equal), 6)
                            link(dve.tensor_scalar(SMALL[:, 4], SMALL[:, 3], -BIG, None, ALU.mult), 7)
                            link(dve.tensor_tensor(SMALL[:, 5], SMALL[:, 4], SMALL[:, 0], ALU.add), 8)
                            link(dve.tensor_reduce(SM4[:, 1, :], SMALL[:, 5], AX.X, ALU.max), 9)
                            link(dve.tensor_tensor(SMALL[:, 6], SMALL[:, 5], wide(1), ALU.is_equal), 10)
                            link(dve.tensor_tensor(SMALL[:, 7], SMALL[:, 6], rank, ALU.mult), 11)
                            link(dve.tensor_reduce(SM4[:, 5, :], SMALL[:, 7], AX.X, ALU.max), 12)
                            link(dve.tensor_tensor(SMALL[:, 8], SMALL[:, 7], wide(5), ALU.is_equal), 13)
                            link(dve.tensor_tensor(SM4[:, 2, :], SM4[:, 1, :], SM4[:, 0, :], ALU.subtract), 14)
                        if s == 8:
                            after("e2")
                            link(dve.tensor_scalar(SM4[:, 6, :], SM4[:, 3, :], 1.0, None, ALU.add), 15)
                            link(dve.reciprocal(SM4[:, 7, :], SM4[:, 6, :]), 16)
                            dve.tensor_tensor(SMALL[:, 9], SMALL[:, 3], wide(7), ALU.mult)
                            link(dve.tensor_tensor(SMALL[:, 10], SMALL[:, 8], wide(7), ALU.mult), 17)
                            link(dve.tensor_tensor(SMALL[:, 11], SMALL[:, 10], wide(3), ALU.mult), 18)
                            dve.tensor_tensor(SMALL[:, 12], SMALL[:, 11], SMALL[:, 9], ALU.add).then_inc(sem["m1_top"], 1)
                        if s >= 11 + 7 and (s - 11) % 4 == 3:
                            e = (s - 11) // 4 - 1
                            after("dn_ps", 4 * e + 4)
                            after("ring", 5 * e + 5)
                            if e >= 2:
                                after("acc", e - 1)
                            dst = ACC[:, :, :].rearrange("p b n -> p (b n)") if e == 0 else YT[:, :]
                            dve.scalar_tensor_tensor(dst, bank(4), vec("b2", e), CBC[:, e, :],
                                                     ALU.add, ALU.mult).then_inc(sem["m1_t"], 1)
                            if e:
                                after("t", e + 1)
                                dve.tensor_tensor(ACC[:, :, :].rearrange("p b n -> p (b n)"), ACC[:, :, :].rearrange("p b n -> p (b n)"),
                                                  YT[:, :], ALU.add).then_inc(sem["m1_acc"], 1)
                        if s == M1N - 1:
                            after("y_ps")
                            after("xx")
                            dve.tensor_tensor(x[:, :, :], bank4(5), x[:, :, :], ALU.add).then_inc(sem["m1_done"], 1)
                        yield
                return run(), M1N

            def m2(g, p, prev):
                v = turn(g, "m2")
                x = X[p]

                def after(name, k=1):
                    dve.wait_ge(sem["m2_" + name], v("m2_" + name, k))

                def run():
                    first(dve, g, prev, ("a2_done", 1))
                    stats(v, "mn", 0, x, MST, MMV)
                    yield from head(g, v, x, stored=False)
                    for s in range(3, M2N):
                        k, j = divmod(s - 5, 3)
                        if j == 1 and 0 <= k < 8:
                            after("lt_ps", k + 1)
                            dve.tensor_reduce(NM2[:, k, :], bank4(4 + k % 2), AX.X, ALU.max, negate=True).then_inc(sem["m2_nm"], 1)
                        k, j = divmod(s - 5 - 3, 3)
                        if j == 0 and 0 <= k < 8:
                            after("ex", k + 1)
                            dve.reciprocal(RZ2[:, k, :], ZZ2[:, k, :]).then_inc(sem["m2_rz"], 1)
                        k, j = divmod(s - 5 - 7, 3)
                        if j == 0 and 0 <= k < 8:
                            after("sl_ps", k + 1)
                            for a in range(2):
                                last = dve.tensor_scalar(SL[:, 2 * k + a, :, :], bank4(7)[:, :, 64 * a:64 * a + 64], vec("norm_g"),
                                                         vec("norm_b"), ALU.mult, ALU.add)
                            last.then_inc(sem["m2_sl"], 1)
                        e, j = divmod(s - M2E, 3)
                        if 0 <= e < E2 and j < 2:
                            after("gelu", 2 * e + j + 1)
                            if e >= 2:
                                after("dn_ps", e - 1)
                            dve.scalar_tensor_tensor(HT[e % 2][:, j, :], bank(4 + j, 256, 512), VT2[:, 32 + 2 * e + j:33 + 2 * e + j],
                                                     GL[:, j, :], ALU.add, ALU.mult).then_inc(sem["m2_ht"], 1)
                        b, j = divmod(s - M2C, 3)
                        if 0 <= b < NB and j == 0:
                            after("l_ps", b + 1)
                            dve.tensor_reduce(NR2[:, 0, b:b + 1], PS[:, 4:6, :], AX.XY, ALU.max, negate=True).then_inc(sem["m2_nr"], 1)
                        if s == M2N - 1:
                            after("ec", NB)
                            dve.reciprocal(NR2[:, 2, :], NR2[:, 1, :]).then_inc(sem["m2_nr"], 1)
                            after("nr", NB + 1)
                            after("cm_ps", NB)
                            for b in range(NB):
                                last = dve.scalar_tensor_tensor(x[:, b, :], bank(7, 128 * b, 128 * b + 128), NR2[:, 2, b:b + 1],
                                                                x[:, b, :], ALU.mult, ALU.add)
                            last.then_inc(sem["m2_done"], 1)
                        yield
                return run(), M2N

            def m3(g, p, prev):
                v = turn(g, "m3")
                x = X[p]

                def after(name, k=1):
                    dve.wait_ge(sem["m3_" + name], v("m3_" + name, k))

                def link(ins, k):
                    ins.then_inc(sem["m3_top"], 1)
                    after("top", k)

                def run():
                    first(dve, g, prev, ("a3_done", 1))
                    stats(v, "mn", 0, x, MST, MMV)
                    yield from head(g, v, x, stored=(p == 1))
                    for s in range(3, M3N):
                        if s == 6:
                            after("ds_ps")
                            link(dve.tensor_copy(SMALL[:, 0], bank(7, 0, NB * E3).rearrange("p (b e) -> p b e", b=NB)), 1)
                            link(dve.tensor_reduce(SM4[:, 0, :], SMALL[:, 0], AX.X, ALU.min), 2)
                            link(dve.tensor_tensor(SMALL[:, 1], SMALL[:, 0], SM4[:, 0, :].unsqueeze(2).to_broadcast([128, NB, E3]),
                                                   ALU.is_equal), 3)
                            link(dve.tensor_tensor(SMALL[:, 2], SMALL[:, 1], RANK[:, :].unsqueeze(1).to_broadcast([128, NB, E3]),
                                                   ALU.mult), 4)
                            link(dve.tensor_reduce(SM4[:, 1, :], SMALL[:, 2], AX.X, ALU.max), 5)
                            dve.tensor_tensor(SMALL[:, 3], SMALL[:, 2], SM4[:, 1, :].unsqueeze(2).to_broadcast([128, NB, E3]),
                                              ALU.is_equal).then_inc(sem["m3_top"], 1)
                        for e in range(E3):
                            if s == max(10, 11 + 4 * e - 4):
                                after("mk", e + 1)
                                after("xpt", 1)
                                if e >= 2:
                                    after("up_ps", 2 * e - 2)
                                dve.tensor_tensor(XM[e % 2], MHT[:, :, :].rearrange("p b n -> p (b n)"), MK[:, e, :],
                                                  ALU.mult).then_inc(sem["m3_xm"], 1)
                        e, j = divmod(s - 11, 4)
                        if 0 <= e < E3 and j % 2 == 0:
                            n = 2 * e + j // 2
                            after("silu", n + 1)
                            if n >= 4:
                                after("dn_ps", n - 3)
                            dve.tensor_tensor(HM[n % 4], bank(5 + (2 * n + 1) % 3), SG[n % 2], ALU.mult).then_inc(sem["m3_hm"], 1)
                        if s == M3N - 1:
                            after("y_ps")
                            after("xx")
                            dve.tensor_tensor(MN[:, :, :], bank4(5), MN[:, :, :], ALU.add).then_inc(sem["m3_out"], 1)
                        yield
                return run(), M3N

            phases(dve, a1, m1, lambda *a: attention("a2", *a), m2, lambda *a: attention("a3", *a), m3, scale_w1)

        @block.tensor
        def _(pe):
            mm = pe.matmul

            def flip(k, src, rows=128, cols=128, n=4):
                for b in range(n):
                    last = pe.transpose(PS[0:cols, k, rows * b:rows * b + rows], src[0:rows, b, :], IDN[0:rows, 0:rows])
                return last

            pe.wait_ge(setup["iota"], 4)
            pe.wait_ge(setup["m8"], 1)
            pe.wait_ge(setup["mat_in"], 16 * 27)
            flip(0, RAW[:, 0:4, :])
            flip(1, RAW[:, 4:6, :], n=2)
            pe.transpose(PS[:, 2, 0:NV1], VEC1[0:NV1, :], IDN[0:NV1, 0:NV1])
            pe.transpose(PS[:, 2, 128:192], VEC2[0:64, :], IDN[0:64, 0:64])
            mm(bank(3, 0, 128), RAW[:, RW1Q, :], RAW[:, RW1K, :], start=True, stop=True).then_inc(setup["ps"], 1)
            pe.wait_ge(setup["small_in"], 16 * 10)
            flip(4, RU, 128, 16)
            pe.transpose(PS[0:16, 5, 0:16], RFB[0:16, :], IDN[0:16, 0:16])
            mm(bank(5, 32, 32 + HD, HD), R8[0:HD, 0, :], R8[0:HD, 1, :], start=True, stop=True)
            e8 = E8[:, :, :].rearrange("k h d -> k (h d)")
            mm(bank(5, 128, 256), e8, R8[0:HD, 2, :].unsqueeze(1).to_broadcast([HD, H, HD]), start=True,
               stop=True).then_inc(setup["ps"], 1)
            pe.wait_ge(setup["sb"], 2)
            pe.wait_ge(setup["act"], 1)
            mm(bank(6, 0, 128, 16), FBT[0:16, :], RVV[0:16, :], start=True, stop=True)
            mm(bank(6, 128, 256), BDV[:, :], WT1[:, 1, :], start=True, stop=True)
            mm(bank(6, 256, 384), e8, A8[0:HD, :].unsqueeze(1).to_broadcast([HD, H, HD]), start=True,
               stop=True).then_inc(setup["ps"], 1)
            pe.wait_ge(setup["sb"], 3)
            for c in range(4):
                last = mm(bank(7, 128 * c, 128 * c + 128), UT[0:16, c, :], FBV[0:16, :], start=True, stop=True)
            last.then_inc(setup["ps"], 1)
            pe.wait_ge(setup["sb"], 4)
            flip(0, RPJ)
            flip(1, RFC).then_inc(setup["ps"], 1)
            pe.wait_ge(setup["sb"], 5)
            flip(2, SE[:, 0:4, :])
            flip(3, SE[:, 4:8, :]).then_inc(setup["ps"], 1)

            def beta_w1():
                pe.wait_ge(setup["w1_in"], 16)
                for e in range(E1):
                    for c in range(4):
                        last = mm(bank(4, 4 * e + c, 4 * e + c + 1), W1[:, e, 128 * c:128 * c + 128], vec("beta", e),
                                  start=True, stop=True)
                last.then_inc(setup["ps"], 1)

            def a1(g, p, prev):
                v = turn(g)

                def after(name, k=1):
                    pe.wait_ge(sem["a1_" + name], v("a1_" + name, k))

                def inc(ins, name):
                    ins.then_inc(sem["a1_" + name], 1)

                def run():
                    first(pe, g, prev)
                    arrived(pe, c_in, g, p)
                    if prev is None:
                        pe.wait_ge(setup["act"], 2)
                    for s in range(A1N):
                        if s == A1S["ct_ps"]:
                            flip(1, C[p], S2, D).then_inc(sem["a1_ct_ps"], 1)
                        if s == A1S["kv_ps"]:
                            after("ct")
                            for b in range(NB):
                                last = mm(bank(3, 128 * b, 128 * b + 128, S2), CT[p][:, b, :], WT0[:, 1, :], start=True, stop=True)
                            last.then_inc(sem["a1_kv_ps"], 1)
                            for b in range(NB):
                                last = mm(bank(0, 128 * b, 128 * b + 128, S2), CT[p][:, b, :], WT0[:, 2, :], start=True, stop=True)
                            last.then_inc(sem["a1_kv_ps"], 1)
                        for j in range(3):
                            if s == A1S[f"xn_ps{j}"]:
                                after("xn", j + 1)
                                flip(1 if j == 0 else 0, AN).then_inc(sem["a1_xn_ps"], 1)
                        if s == A1S["q_ps"]:
                            after("xnt", 1)
                            for b in range(NB):
                                last = mm(bank(2, 128 * b, 128 * b + 128), ANT[:, b, :], WT0[:, 0, :], start=True, stop=True)
                            last.then_inc(sem["a1_q_ps"], 1)
                        if s == A1S["kvs_ps"]:
                            after("qk", 3)
                            for h in range(2):
                                for b in range(2):
                                    last = mm(bank((1, 3)[h], 256 * b, 256 * b + D + 1), QK[0:S2, 1, 2 * h + b, :],
                                              VV[0:S2, 2 * h + b, :], start=True, stop=True)
                                last.then_inc(sem["a1_kvs_ps"], 1)
                            flip(2, QK[:, 0]).then_inc(sem["a1_qt_ps"], 1)
                        if s == A1S["num_ps"]:
                            after("kvm")
                            after("qt")
                            for h in range(2):
                                for b in range(2):
                                    last = mm(bank((0, 1)[h], 256 * b, 256 * b + D + H), AQT[:, 2 * h + b, :],
                                              KVM[:, 2 * h + b, :], start=True, stop=True)
                                last.then_inc(sem["a1_num_ps"], 1)
                        if s == A1S["ot_ps"]:
                            after("o", 3)
                            flip(2, OO).then_inc(sem["a1_ot_ps"], 1)
                        if s == A1S["proj_ps"]:
                            after("ot")
                            for b in range(NB):
                                last = mm(bank(3, 128 * b, 128 * b + 128), ANT[:, b, :], WT0[:, 3, :], start=True, stop=True)
                            last.then_inc(sem["a1_proj_ps"], 1)
                        if s in (A1S["h01"], A1S["h23"]):
                            after("xnt", 2)
                            for c in (0, 1) if s == A1S["h01"] else (2, 3):
                                mm(bank((1, 2, 3, 0)[c]), WFC[:, 128 * c:128 * c + 128], ANT[:, :, :], start=True,
                                   stop=True).then_inc(sem["a1_h_ps"], 1)
                        if s == A1S["dn_ps"]:
                            after("sq", 4)
                            for b in range(NB):
                                for c in range(4):
                                    last = mm(bank(1, 128 * b, 128 * b + 128), R2[:, c, 128 * b:128 * b + 128], WPJ[:, c, :],
                                              start=(c == 0), stop=(c == 3))
                            last.then_inc(sem["a1_dn_ps"], 1)
                        if s == A1S["v_ps"]:
                            for b in range(NB):
                                last = mm(bank(2, 128 * b, 128 * b + 128, S2), CT[p][:, b, :], WT1[:, 0, :], start=True, stop=True)
                            last.then_inc(sem["a1_v_ps"], 1)
                            after("xnt", 3)
                            mm(bank(1), A1[:, :], ANT[:, :, :], start=True, stop=True).then_inc(sem["a1_t_ps"], 1)
                        if s == A1S["s_ps"]:
                            after("t_sb")
                            for b in range(NB):
                                last = mm(bank(3, S2 * b, S2 * b + S2), AQT[:, b, :], CT[p][:, b, :], start=True, stop=True)
                            last.then_inc(sem["a1_s_ps"], 1)
                        if s == A1S["pt_ps"]:
                            after("p")
                            for b in range(NB):
                                last = pe.transpose(bank(0, 128 * b, 128 * b + 128, S2), SS[:, b, :], IDN[:, :])
                            last.then_inc(sem["a1_pt_ps"], 1)
                        if s == A1S["pv_ps"]:
                            after("pt")
                            after("v_sb")
                            for b in range(NB):
                                last = mm(bank(1, 128 * b, 128 * b + 128), PTT[0:S2, b, :], V1[0:S2, b, :], start=True, stop=True)
                            last.then_inc(sem["a1_pv_ps"], 1)
                        yield
                return run(), A1N

            def attention(ph, g, p, prev):
                v = turn(g, ph)

                def after(name, k=1):
                    own = ("a3_" if name in ("k_ps", "kt", "v_ps", "v32") else "at_") + name
                    pe.wait_ge(sem[own], v(own, k))

                def run():
                    first(pe, g, prev)
                    for s in range(ATN):
                        if s == 1 and ph == "a3":
                            mm(bank(2, 0, NB * S2), W3[:, 1, :], CT[p][:, :, :], start=True, stop=True).then_inc(sem["a3_k_ps"], 1)
                            for b in range(NB):
                                last = mm(bank(3, 128 * b, 128 * b + 128, S2), CT[p][:, b, :], W3[:, 2, :], start=True, stop=True)
                            last.then_inc(sem["a3_v_ps"], 1)
                        if s == 3:
                            after("xn")
                            flip(0, AN).then_inc(sem["at_xn_ps"], 1)
                        if s == 5:
                            after("xnt")
                            mm(bank(1), BDA[:, :] if ph == "a2" else W3[:, 0, :], ANT[:, :, :], start=True,
                               stop=True).then_inc(sem["at_q_ps"], 1)
                        for u in range(UNITS):
                            r, b = u % 2, u // 2
                            j = s - 7 - 4 * u
                            if j == 0:
                                if u == 0:
                                    after("qt")
                                if r == 0:
                                    after("kb", b + 1)
                                if u >= 2:
                                    after("on", 2 * u - 2)
                                elif ph == "a3":
                                    after("kt")
                                    after("v32")
                                for q in range(2):
                                    last = mm(bank(2 * r + q, 0, 4 * S2), AQT[64 * r:64 * r + 64, b, :],
                                              KB[b % 2][64 * r:64 * r + 64, 4 * q:4 * q + 4, :], start=True, stop=(ph == "a3"))
                                    if ph == "a2":
                                        last = mm(bank(2 * r + q, 0, 4 * S2), IDB[:, :],
                                                  MB2[:, :].unsqueeze(1).to_broadcast([128, 4, S2]), start=False, stop=True)
                                last.then_inc(sem["at_s_ps"], 1)
                            if j == 3:
                                after("exp", u + 1)
                                for h in range(HU):
                                    last = pe.transpose(bank(2 * r + h // 4, 128 * (h % 4), 128 * (h % 4) + 128, S2),
                                                        EE[r][:, h, :], IDN[:, :])
                                last.then_inc(sem["at_et_ps"], 1)
                            if j == 5:
                                after("etl", u + 1)
                                if u == 0:
                                    after("v", 2)
                                for h in range(HU):
                                    dst = bank(2 * r, (HD + 1) * h, (HD + 1) * h + HD + 1)
                                    hh = HU * r + h
                                    mm(dst, ETH[r][0:S2, h, :], VAH[:, b, hh, :], start=True, stop=False)
                                    mm(dst, ETH[r][0:S2, h, :], VAL[:, b, hh, :], start=False, stop=False)
                                    last = mm(dst, ETL[r][0:S2, h, :], VAH[:, b, hh, :], start=False, stop=True)
                                last.then_inc(sem["at_pv_ps"], 1)
                        if s == ATN - 4:
                            after("on", 2 * UNITS)
                            flip(0, OB).then_inc(sem["at_ot_ps"], 1)
                        if s == ATN - 2:
                            after("ot")
                            for b in range(NB):
                                last = mm(bank(1, 128 * b, 128 * b + 128), ANT[:, b, :], W2O[:, :] if ph == "a2" else W3[:, 3, :],
                                          start=True, stop=True)
                            last.then_inc(sem["at_proj_ps"], 1)
                        yield
                return run(), ATN

            def m1(g, p, prev):
                v = turn(g, "m1")

                def after(name, k=1):
                    pe.wait_ge(sem["m1_" + name], v("m1_" + name, k))

                def run():
                    first(pe, g, prev)
                    if p == 0:
                        pe.wait_ge(setup["sb"], 7)
                        pe.wait_ge(setup["w2_in"], 16 * (E1 + 1))
                    for s in range(M1N):
                        if s == 3:
                            pe.wait_ge(sem["mn_xn"], v("mn_xn", 1))
                            flip(5, MN).then_inc(sem["m1_xn_ps"], 1)
                            pe.wait_ge(sem["mn_xh"], v("mn_xh", 1))
                            flip(6, MH).then_inc(sem["mn_xh_ps"], 1)
                        if s == 5:
                            after("xht", 1)
                            for b in range(NB):
                                last = mm(bank(7, E1 * b, E1 * b + E1), MNT[:, b, :], WGT[:, :], start=True, stop=True)
                            last.then_inc(sem["m1_sc_ps"], 1)
                        if s == 9:
                            after("top", 19)
                            for b in range(NB):
                                last = pe.transpose(bank(7, 128 * b, 128 * b + 128, E1), SMALL[:, 12, b, :], IDN[:, :])
                            last.then_inc(sem["m1_cw_ps"], 1)
                        if s >= 11:
                            e, c = divmod(s - 11, 4)
                            if e < E1:
                                if e == 0 and c == 0:
                                    after("xht", 2)
                                    after("cwt")
                                n = 5 * e + c
                                if n >= 3:
                                    after("ring", n - 2)
                                mm(bank(5 + n % 3), W1[:, e, 128 * c:128 * c + 128], MHT[:, :, :], start=True,
                                   stop=True).then_inc(sem["m1_up_ps"], 1)
                            if 1 <= e <= E1:
                                if c == 0 and e >= 2:
                                    after("t", e - 1)
                                after("ring", 5 * (e - 1) + c + 1)
                                mm(bank(4), W2[:, e - 1, c, :], HID[:, c, :], start=(c == 0),
                                   stop=(c == 3)).then_inc(sem["m1_dn_ps"], 1)
                            if e < E1 and c == 3:
                                n = 5 * e + 4
                                after("ring", n - 2)
                                mm(bank(5 + n % 3), IDN[0:E1, e:e + 1].to_broadcast([E1, 128]), CWT[0:E1, :], start=True,
                                   stop=True).then_inc(sem["m1_cb_ps"], 1)
                        if s == M1N - 2:
                            after("acc", E1 - 1)
                            flip(5, ACC).then_inc(sem["m1_y_ps"], 1)
                        yield
                return run(), M1N

            def m2(g, p, prev):
                v = turn(g, "m2")

                def after(name, k=1):
                    pe.wait_ge(sem["m2_" + name], v("m2_" + name, k))

                def run():
                    first(pe, g, prev)
                    if p == 0:
                        pe.wait_ge(setup["l2_in"], 16 * (E2 + 2))
                    for s in range(M2N):
                        if s == 3:
                            pe.wait_ge(sem["mn_xh"], v("mn_xh", 1))
                            flip(5, MH).then_inc(sem["mn_xh_ps"], 1)
                        k, j = divmod(s - 5, 3)
                        if j == 0 and 0 <= k < 8:
                            if k == 0:
                                after("xpt")
                            if k >= 2:
                                after("ex", k - 1)
                            mm(bank(4 + k % 2), SET[:, 128 * k:128 * k + 128], MHT[:, :, :], start=True,
                               stop=True).then_inc(sem["m2_lt_ps"], 1)
                        k, j = divmod(s - 5 - 4, 3)
                        if j == 0 and 0 <= k < 8:
                            after("ed", k + 1)
                            if k:
                                after("pd", k)
                            flip(6, ED[k % 2]).then_inc(sem["m2_pd_ps"], 1)
                        k, j = divmod(s - 5 - 6, 3)
                        if j == 0 and 0 <= k < 8:
                            after("pd", k + 1)
                            if k:
                                after("sl", k)
                            for b in range(NB):
                                last = mm(bank(7, 128 * b, 128 * b + 128), MH[:, b, :], PD[k % 2][:, b, :], start=True, stop=True)
                            last.then_inc(sem["m2_sl_ps"], 1)
                        e, j = divmod(s - M2E, 3)
                        if 0 <= e < E2 and j < 2:
                            if e == 0:
                                after("sl", 8)
                            else:
                                after("ht", 2 * (e - 1) + j + 1)
                            mm(bank(4 + j, 0, 256), WG[:, e, 128 * j:128 * j + 128], SL[:, e, :, :], start=True, stop=True)
                            mm(bank(4 + j, 256, 512), WU[:, e, 128 * j:128 * j + 128], SL[:, e, :, :], start=True,
                               stop=True).then_inc(sem["m2_gu_ps"], 1)
                        if j == 1 and e % 2 == 1 and 3 <= e <= 17:
                            k = (e - 3) // 2
                            after("eo", 2 * k + 2)
                            if k:
                                after("es", k)
                            flip(7, EO[k % 2]).then_inc(sem["m2_es_ps"], 1)
                        if 1 <= e <= E2 and j == 2:
                            f = e - 1
                            after("ht", 2 * f + 2)
                            if f:
                                after("eo", f)
                            for c in range(2):
                                last = mm(bank(6, 0, 256), WD[:, f, c, :], HT[f % 2][:, c, :], start=(c == 0), stop=(c == 1))
                            last.then_inc(sem["m2_dn_ps"], 1)
                        b, j = divmod(s - M2C, 3)
                        if 0 <= b < NB and j == 0:
                            if b:
                                after("ec", b)
                            else:
                                after("es", 8)
                            for h in range(2):
                                last = mm(bank(4 + h), MHT[:, b, :], SET[:, 512 * h:512 * h + 512], start=True, stop=True)
                            last.then_inc(sem["m2_l_ps"], 1)
                        if 0 <= b < NB and j == 1:
                            after("ec", b + 1)
                            for h in range(2):
                                if 2 * b + h:
                                    after("ctt", 2 * b + h)
                                flip(6, EC.rearrange("p (k s) -> p k s", k=8)[:, 4 * h:4 * h + 4, :]).then_inc(sem["m2_ct_ps"], 1)
                        if 0 <= b < NB and j == 2:
                            after("ctt", 2 * b + 2)
                            for k in range(8):
                                last = mm(bank(7, 128 * b, 128 * b + 128), CTT[b % 2][:, k, :], ES[:, k, b, :],
                                          start=(k == 0), stop=(k == 7))
                            last.then_inc(sem["m2_cm_ps"], 1)
                        yield
                return run(), M2N

            def m3(g, p, prev):
                v = turn(g, "m3")

                def after(name, k=1):
                    pe.wait_ge(sem["m3_" + name], v("m3_" + name, k))

                def run():
                    first(pe, g, prev)
                    if p == 0:
                        pe.wait_ge(setup["l3_in"], 16 * (E3 + 1))
                    for s in range(M3N):
                        if s == 3:
                            pe.wait_ge(sem["mn_xh"], v("mn_xh", 1))
                            flip(5, MH).then_inc(sem["mn_xh_ps"], 1)
                        if s == 5:
                            after("xpt", 2)
                            for b in range(NB):
                                dst = bank(7, E3 * b, E3 * b + E3)
                                mm(dst, MHT[:, b, :], CM2[:, :], start=True, stop=False)
                                mm(dst, SQT[:, b, :], ONE[:, :], start=False, stop=False)
                                last = mm(dst, ONE[:, 0:1].to_broadcast([128, 128]), CSQ[:, :], start=False, stop=True)
                            last.then_inc(sem["m3_ds_ps"], 1)
                        if s == 7:
                            after("top", 6)
                            for b in range(NB):
                                last = pe.transpose(bank(5, 128 * b, 128 * b + 128, E3), SMALL[:, 3, b, :], IDN[:, :])
                            last.then_inc(sem["m3_oh_ps"], 1)
                        if s == 9:
                            after("oht")
                        if s == 10:
                            for e in range(E3):
                                if e >= 3:
                                    after("mk", e - 2)
                                mm(bank(5 + e % 3), IDB[0:E3, e:e + 1].to_broadcast([E3, 128]), OHT[0:E3, :], start=True,
                                   stop=True).then_inc(sem["m3_mk_ps"], 1)
                        if s == M3N - 2:
                            after("yt")
                            flip(5, YT3).then_inc(sem["m3_y_ps"], 1)
                        e, j = divmod(s - 11, 4)
                        if 0 <= e < E3 and j % 2 == 0:
                            c = j // 2
                            n = 2 * e + c
                            if c == 0:
                                after("xm", e + 1)
                            if n == 0:
                                after("mk", E3)
                            if n >= 2:
                                after("hm", n - 1)
                            mm(bank(5 + 2 * n % 3), WA[:, e, F3 + 128 * c:F3 + 128 * c + 128], XM[e % 2], start=True, stop=True)
                            if n >= 1:
                                after("silu", n)
                            mm(bank(5 + (2 * n + 1) % 3), WA[:, e, 128 * c:128 * c + 128], XM[e % 2], start=True,
                               stop=True).then_inc(sem["m3_up_ps"], 1)
                        if 0 <= s - 11 - 2 and (s - 11) % 2 == 0 and (s - 11) // 2 - 1 < 2 * E3:
                            n = (s - 11) // 2 - 1
                            after("hm", n + 1)
                            mm(bank(4), WB[:, n // 2, n % 2, :], HM[n % 4], start=(n == 0), stop=(n == 2 * E3 - 1)).then_inc(sem["m3_dn_ps"], 1)
                        yield
                return run(), M3N

            phases(pe, a1, m1, lambda *a: attention("a2", *a), m2, lambda *a: attention("a3", *a), m3, beta_w1)

        @block.sync
        def _(sp):
            xg = t["x"].rearrange("(g b) n d -> g n b d", b=NB)
            cg = t["ctx_1024"].rearrange("(g b) n d -> g n b d", b=NB)
            og = out.rearrange("(g b) n d -> g n b d", b=NB)

            def row(name, width=128):
                ap = t[name]
                if len(ap.shape) == 1:
                    return ap.rearrange("(a d) -> a d", d=width)
                return ap.rearrange("a (c d) -> (a c) d", d=width)

            def load(dst, src, name):
                sp.dma_start(dst, src).then_inc(setup[name], 16)

            def tile(g, p):
                sp.dma_start(X[p][:, :, :], xg[g]).then_inc(x_in[p], 16)

            def context(g, p):
                sp.dma_start(C[p][:, :, :], cg[g]).then_inc(c_in[p], 16)

            tile(0, 0)
            context(0, 0)
            for k, name in ((RW0Q, "L0_xattn_Wq"), (RW0K, "L0_xattn_Wk"), (RW0V, "L0_xattn_Wv"), (RW0P, "L0_xattn_Wp"),
                            (RW1V, "L1_xattn_Wv"), (RW2O, "L2_xattn_Wo"), (RW1Q, "L1_xattn_Wq"), (RW1K, "L1_xattn_Wk")):
                load(RAW[:, k, :], t[name], "mat_in")
            for k, name in enumerate(("L3_xattn_Wq", "L3_xattn_Wk", "L3_xattn_Wv", "L3_xattn_Wo")):
                load(W3[:, k, :], t[name], "mat_in")
            at = 0
            for name in ("L1_ffn_gamma", "L1_ffn_beta", "L1_ffn_b2", "L1_ffn_b1", "L2_ffn_norm_g", "L2_ffn_norm_b",
                         "L2_ffn_slot_g", "L2_ffn_slot_b", "L3_xattn_bq", "L3_xattn_bk", "L3_ffn_scale", "L2_ffn_bd",
                         "L3_ffn_centroids"):
                src = row(name)
                load(VEC1[at:at + src.shape[0], :], src, "mat_in")
                at += src.shape[0]
            load(VEC2[0:32, :], row("L2_ffn_bg"), "mat_in")
            load(VEC2[32:64, :], row("L2_ffn_bu"), "mat_in")
            load(SE[:, :, :], t["L2_ffn_slot_embeds"].rearrange("e s d -> (e s) d").rearrange("(k p) d -> p k d", p=128), "slot_in")
            load(MKI[:, 0, :], t["mask_SxS2_ik1"], "small_in")
            load(MKI[:, 1, :], t["mask_1x1xSxS2_ik0"].rearrange("a b s t -> (a b s) t"), "small_in")
            load(RFC[:, :, :], t["L0_ffn_w_fc"].rearrange("(c f) d -> f c d", f=128), "small_in")
            load(RPJ[:, :, :], t["L0_ffn_w_proj"].rearrange("d (c f) -> d c f", f=128), "small_in")
            load(RU[:, :, :], t["L0_ffn_u"].rearrange("(c f) r -> f c r", f=128), "small_in")
            load(RFB[0:16, :], t["L0_ffn_fast_b"], "small_in")
            load(RVV[0:16, :], t["L0_ffn_v"], "small_in")
            for k, name in enumerate(("L2_xattn_Wq", "L2_xattn_Wk", "L2_xattn_Wv")):
                load(R8[0:HD, k, :], t[name], "small_in")
            for k, name in ((BQ0, "L0_xattn_bq"), (BK0, "L0_xattn_bk"), (BV0, "L0_xattn_bv"), (BP0, "L0_xattn_bp"),
                            (BO2, "L2_xattn_bo"), (BV3, "L3_xattn_bv"), (BO3, "L3_xattn_bo")):
                load(BC[:, k, :], row(name).to_broadcast([128, D]), "bc_in")
            load(SCL[:, 0:1], row("L0_ffn_gate", 1).to_broadcast([128, 1]), "bc_in")
            load(SCL[:, 1:2], row("L2_ffn_scale", 1).to_broadcast([128, 1]), "bc_in")
            load(W1[:, :, :], t["L1_ffn_W1"].rearrange("e d f -> d e f"), "w1_in")
            if groups > 1:
                tile(1, 1)
                context(1, 1)
            load(WGT[:, :], t["L1_ffn_Wg"], "w2_in")
            for e in range(E1):
                load(W2[:, e, :, :], t["L1_ffn_W2"][e].rearrange("(c p) d -> p c d", p=128), "w2_in")
            load(WG[:, :, :], t["L2_ffn_Wg"].rearrange("e d f -> d e f"), "l2_in")
            load(WU[:, :, :], t["L2_ffn_Wu"].rearrange("e d f -> d e f"), "l2_in")
            for e in range(E2):
                load(WD[:, e, :, :], t["L2_ffn_Wd"][e].rearrange("(c p) d -> p c d", p=128), "l2_in")
            load(WA[:, :, :], t["L3_ffn_up_w"].rearrange("e d f -> d e f"), "l3_in")
            for e in range(E3):
                load(WB[:, e, :, :], t["L3_ffn_down_w"][e].rearrange("(c p) d -> p c d", p=128), "l3_in")

            def pair(i, last):
                values = None if last else Pair(sp, i)

                def group(k):
                    return (None, 2 * i + k) if last else (values, k)
                if not last:
                    for p in range(2):
                        v = turn(group(p), "a2")
                        sp.wait_ge(sem["at_v"], v("at_v", 2))
                        context(2 * i + 2 + p, p)
                for p in range(2):
                    v = turn(group(p))
                    if not last:
                        sp.wait_ge(sem["m3_xx"], v("m3_xx", 1))
                        tile(2 * i + 2 + p, p)
                    sp.wait_ge(sem["m3_out"], v("m3_out", 1))
                    sp.dma_start(og[2 * i + p], MN[:, :, :]).then_inc(sem["m3_stored"], 16)

            pairs = groups // 2
            if pairs > 1:
                with sp.Fori(0, pairs - 1) as i:
                    pair(i, False)
            pair(pairs - 1, True)
            sp.wait_ge(sem["m3_stored"], BASE["m3_stored"] + PER["m3_stored"] * groups)


def kernel(**inputs):
    import numpy as _np
    import concourse.bacc as _bacc
    from concourse import mybir as _mybir
    from concourse.bass_utils import run_bass_kernel_spmd as _run

    nc = _bacc.Bacc("TRN2", target_bir_lowering=False, num_devices=1)
    arrays, aps = {}, {}
    for name, a in inputs.items():
        if name == "itok_BxS2_0_2047":
            continue
        a = _np.ascontiguousarray(a)
        if a.ndim == 0:
            a = a.reshape(1)
        arrays[f"in_{name}_dram"] = a
        aps[name] = nc.dram_tensor(f"in_{name}_dram", a.shape, _mybir.dt.from_np(a.dtype), kind="ExternalInput").ap()
    out = nc.dram_tensor("out_0_dram", (NBATCH, N, D), F32, kind="ExternalOutput").ap()
    build(nc, aps, out)
    r = _run(nc, [arrays], core_ids=[0])
    return r.results[0]["out_0_dram"]
```

```python
from contextlib import ExitStack

import concourse.bass as bass
from concourse import mybir

F32 = mybir.dt.float32
BF16 = mybir.dt.bfloat16
F16 = mybir.dt.float16
I32 = mybir.dt.int32
ALU = mybir.AluOpType
ACT = mybir.ActivationFunctionType
AX = mybir.AxisListType

NBATCH, N, D = 32, 128, 128
S2 = 120
NB = 4
G = NBATCH // NB
T = NB * N
H, HD = 16, 8
E1, F1 = 8, 512
E2, SL2, F2 = 16, 64, 256
NS = E2 * SL2
E3, F3 = 8, 256
F0 = 512
HU = 8
UNITS = NB * H // HU
LN_EPS = 1e-5
BIG = 1e30
WS = 16.0

PER = {}


def per(phase, **counts):
    for name, n in counts.items():
        PER[f"{phase}_{name}"] = n


per("a1", ct_ps=1, ct=1, mv=9, rs=3, xn=3, xn_ps=3, xnt=3,
    xb=1, kv_ps=2, kv_sb=1, q_ps=1, q=3, exp=1, qk=3,
    kvs_ps=2, qt_ps=1, kvm=1, qt=1, num_ps=2, o=3, ot_ps=1, ot=1, proj_ps=1, x=2,
    h_ps=4, relu=4, sq=4, dn_ps=1,
    v_ps=1, v_sb=1, t_ps=1, t_sb=1, s_ps=1, nm=2, p=1, rsm=1, pt_ps=1, pt=1, pv_ps=1, done=1)
per("at", mv=3, rs=1, xn=1, xn_ps=1, xnt=1, xb=1, q_ps=1, qt=1,
    v=2, kb=NB, s_ps=UNITS, sub=2 * UNITS, exp=UNITS, et_ps=UNITS, eth=UNITS, etl=UNITS,
    pv_ps=UNITS, on=2 * UNITS, ot_ps=1, ot=1, proj_ps=1)
per("a2", done=1)
per("a3", k_ps=1, kt=1, v_ps=1, v32=1, done=1)
per("mn", mv=4, rs=2, xn=1, xh=1, xh_ps=1)
per("m1", xx=1, xn_ps=1, xht=2, xlo=1, sc_ps=1, top=22, e2=1, cw_ps=1, cwt=1, cb_ps=E1, ring=5 * E1,
    up_ps=4 * E1, dn_ps=4 * E1, t=E1, acc=E1 - 1, y_ps=1, done=1)
per("m2", xpt=1, lt_ps=8, nm=8, ex=8, rz=8, ed=8, pd_ps=8, pd=8, sl_ps=8, sl=8,
    gu_ps=2 * E2, gelu=2 * E2, ht=2 * E2, dn_ps=E2, eo=E2, es_ps=8, es=8,
    mx=8, mxt_ps=1, hl=3, nmt_ps=1, nmt=1, l_ps=8, ctt=8, cm_ps=8, nr=2, done=1)
per("m3", xx=1, xpt=2, ds_ps=1, top=6, oh_ps=1, oht=1, mk_ps=E3, mk=E3, xm=E3, up_ps=2 * E3,
    silu=2 * E3, sg=2 * E3, hm=2 * E3, dn_ps=2 * E3, yt=1, y_ps=1, out=1)
PER["m3_stored"] = 16
BASE = dict(m3_out=1)
TURNS = dict(a1=2, at=4, a2=2, a3=2, mn=6, m1=2, m2=2, m3=2)
START = dict(a2=dict(at=0), a3=dict(at=2), m1=dict(mn=0), m2=dict(mn=2), m3=dict(mn=4))

A1S = dict(ct_ps=0, rs0=1, ct=1, xn0=2, kv_ps=2, xn_ps0=3, kv_sb=3, xnt0=4, q_ps=5, q_sb=6, exp=7, qk=8, kvs_ps=9,
           kvm=10, qt=10, num_ps=11, o=12, ot_ps=13, ot=14, proj_ps=15, x0=16, rs1=17, xn1=18, xn_ps1=19, xnt1=20,
           h01=21, relu01=22, h23=22, relu23=23, dn_ps=24, x1=25, rs2=26, xn2=27, xn_ps2=28, xnt2=29, v_ps=30,
           t_sb=31, s_ps=32, nm=33, p=34, pt_ps=35, pt=36, pv_ps=37, done=38)
A1N = 39
ATN = 7 + 4 * (UNITS - 1) + 7 + 1 + 4
M1H = 11
M1N = M1H + 4 * (E1 + 1) + 2
M2H = 5
M2E = 5 + 3 * 7 + 8 + 1
M2C = M2E + 3 * (E2 + 2)
M2N = M2C + 2 * 8 + 2
M3H = 9
M3N = 11 + 4 * E3 + 2 + 2


SLOTS = dict(m1a1=(2.0, 0.0), m1a2=(1.062, 0.0), m2a2=(0.722, -0.3),
             m2a3=(2.5, 0.0), m3a3=(2.5, 0.0), m3a1=(2.5, 0.0))


def weave(slot, moe, att, head):
    (ng, nn), (ag, an), (hg, hn) = moe, att, head
    wh, shift = SLOTS[slot]
    after = [1.0] * an + [wh] * hn
    a, at = 0, 0.0
    for n in range(nn):
        next(ng, None)
        while a < an + hn and (at + after[a] / 2) / sum(after) <= (n + 1 + shift) / nn:
            next(ag if a < an else hg, None)
            at += after[a]
            a += 1
    for k in range(a, an + hn):
        next(ag if k < an else hg, None)
    for g in (ng, ag, hg):
        for _ in g:
            raise AssertionError("a phase has more steps than it says")


def alone(*phases):
    for gen, n in phases:
        for _ in gen:
            pass


class Pair:

    def __init__(self, eng, i):
        self.eng, self.i, self.n = eng, i, 0
        self.regs = [eng.alloc_register(f"value{k}") for k in range(4)]

    def times(self, a, b):
        reg = self.regs[self.n % len(self.regs)]
        self.n += 1
        self.eng.reg_mul(reg, self.i, a)
        self.eng.reg_add(reg, reg, b)
        return reg



def build(nc, t, out, groups=G):
    ctx = ExitStack()
    with ctx:
        def sb(name, shape, dt=F32):
            return ctx.enter_context(nc.sbuf_tensor(name, shape, dt))

        sem = {name: ctx.enter_context(nc.semaphore(name)) for name in PER}
        x_in = [ctx.enter_context(nc.semaphore(f"x{p}_in")) for p in range(2)]
        c_in = [ctx.enter_context(nc.semaphore(f"c{p}_in")) for p in range(2)]
        setup = {name: ctx.enter_context(nc.semaphore("setup_" + name)) for name in (
            "small_in", "mat_in", "slot_in", "w1_in", "w2_in", "l2_in", "l3_in", "m8", "iota", "ps", "sb",
            "act", "slot_rs", "bc_in", "va")}

        W1 = sb("W1", [D, E1, F1])
        W2 = sb("W2", [128, E1, F1 // 128, D])
        WG = sb("WG", [D, E2, F2])
        WU = sb("WU", [D, E2, F2])
        WD = sb("WD", [128, E2, F2 // 128, D])
        WA = sb("WA", [D, E3, 2 * F3])
        WB = sb("WB", [128, E3, F3 // 128, D])
        SET = sb("SET", [D, NS])
        WFC = sb("WFC", [D, F0])
        WPJ = sb("WPJ", [128, F0 // 128, D])
        WT0 = sb("WT0", [D, 4, D])
        WT1 = sb("WT1", [D, 2, D])
        A1 = sb("A1", [D, D])
        BDA = sb("BDA", [D, D])
        W2O = sb("W2O", [D, D])
        W3 = sb("W3", [D, 4, D])
        BC = sb("BC", [128, 7, D])
        BQ0, BK0, BV0, BP0, BO2, BV3, BO3 = range(7)
        VT1 = sb("VT1", [D, 96])
        VT2 = sb("VT2", [D, 64])
        WGT = sb("WGT", [D, E1])
        B1P = sb("B1P", [128, 4 * E1])
        CM2 = sb("CM2", [D, E3])
        CSQ = sb("CSQ", [D, E3])
        SGB = sb("SGB", [D, 2])
        SCL = sb("SCL", [128, 2])
        IDN = sb("IDN", [128, 128])
        IDB = sb("IDB", [128, 128], BF16)
        ONE = sb("ONE", [128, E3])
        BD = sb("BD", [128, H, HD])
        M8 = sb("M8", [128, HU])
        E8 = sb("E8", [HD, H, HD])
        RANK = sb("RANK", [128, E1])
        PASS = sb("PASS", [128, 3])
        EXPO = sb("EXPO", [128, 8])
        MB1 = sb("MB1", [128, S2])
        MB2 = sb("MB2", [128, S2], BF16)

        X = [sb(f"X{p}", [128, NB, D]) for p in range(2)]
        C = [sb(f"C{p}", [S2, NB, D]) for p in range(2)]
        CT = [sb(f"CT{p}", [D, NB, S2]) for p in range(2)]

        AN = sb("AN", [128, NB, D])
        ANT = sb("ANT", [128, NB, D])
        AQT = sb("AQT", [128, NB, D])
        AST = sb("AST", [128, NB, 6])
        AMV = sb("AMV", [128, NB, 2])
        AVE = sb("AVE", [128, NB])
        ARS = sb("ARS", [128, NB])
        AA = sb("AA", [128, 5888])
        VAH = sb("VAH", [S2, NB, H, HD + 1], F16)
        VAL = sb("VAL", [S2, NB, H, HD + 1], F16)

        def aa(at, n, *shape):
            ap = AA[:, at:at + n]
            if len(shape) == 2:
                ap = ap.rearrange("p (a b) -> p a b", a=shape[0])
            if len(shape) == 3:
                ap = ap.rearrange("p (a b c) -> p a b c", a=shape[0], b=shape[1])
            return ap

        QK = aa(0, 1024, 2, NB, D)
        VV = aa(1024, NB * (D + 1), NB, D + 1)
        KVM = aa(1600, NB * 144, NB, 144)
        QKM = aa(2240, 128)
        QKS = aa(2368, 128)
        QKR = aa(2496, 128)
        OO = aa(2624, 512, NB, D)
        DIN = aa(3136, NB * H, NB, H)
        R1 = aa(0, 1024, 2, T)
        R2 = aa(1024, 2048, 4, T)
        SS = aa(3072, NB * S2, NB, S2)
        PTT = aa(3584, 512, NB, N)
        V1 = aa(4096, 512, NB, D)
        SQT = aa(2048, 512, NB, N)
        NM1 = aa(4608, NB)
        SM1 = aa(4616, NB)
        RM1 = aa(4624, NB)
        KB = [aa(0, HU * S2, HU, S2), aa(960, HU * S2, HU, S2)]
        EE = [aa(1920, HU * S2, HU, S2), aa(2880, HU * S2, HU, S2)]
        ETH = [aa(3840 + 512 * r, 512).bitcast(F16).rearrange("p (h n) -> p h n", h=HU) for r in range(2)]
        ETL = [aa(4864 + 512 * r, 512).bitcast(F16).rearrange("p (h n) -> p h n", h=HU) for r in range(2)]
        V32 = aa(1920, 512, NB, D)
        MXU = sb("MXU", [128, 2, HU])
        RDU = sb("RDU", [128, 2, HU])
        OB = AN

        MH = sb("MH", [128, NB, D])
        MHTS = [sb(f"MHT{p}", [128, NB, D]) for p in range(2)]
        CWTS = [sb(f"CWT{p}", [2 * E1, T], F16) for p in range(2)]
        MF = sb("MF", [128, 2, NB])
        SMALL = sb("SMALL", [128, 13, NB, E1])
        SM4 = sb("SM4", [128, 8, NB])
        MA = sb("MA", [128, 7200])

        def ma(at, n, *shape):
            ap = MA[:, at:at + n]
            if len(shape) == 2:
                ap = ap.rearrange("p (a b) -> p a b", a=shape[0])
            if len(shape) == 3:
                ap = ap.rearrange("p (a b c) -> p a b c", a=shape[0], b=shape[1])
            return ap

        CBC = ma(0, 4096, E1, T)
        HID = ma(4096, 2048, 4, T)
        YT = ma(6144, 512)
        ACC = ma(6656, 512, NB, N)
        SL = ma(0, 4096, E2, NB, SL2)
        ES = ma(0, 8 * NB * (D + 1), 8, NB, D + 1)
        ED = [ma(4128 + 512 * i, 512, NB, N) for i in range(2)]
        PD = [ma(5152 + 512 * i, 512, NB, N) for i in range(2)]
        GL = ma(4128, 512, 2, NB * SL2)
        HT = [ma(4640 + 512 * i, 512, 2, NB * SL2) for i in range(2)]
        EO = [ma(5664 + 512 * i, 512, NB, 2 * SL2) for i in range(2)]
        MXS = ma(6688, 512, NB, N)
        NMT = ma(6688, 256).bitcast(BF16)
        CTT = [ma(4128 + 512 * i, 512, NB, N) for i in range(2)]
        HLF = SMALL[:, 0:1].rearrange("p a b e -> p (a b e)")[:, 0:2 * NB].rearrange("p (b a) -> p b a", b=NB)
        MX4 = SM4[:, 0, :]
        MXH = SM4[:, 1, :].bitcast(BF16)[:, 0:NB]
        CWF = SMALL[:, 0:2].rearrange("p a b e -> p (a b e)").rearrange("p (b a) -> p b a", b=NB)
        CWH = SMALL[:, 2:3].rearrange("p a b e -> p (a b e)").bitcast(F16)[:, 0:NB * E1].rearrange("p (b a) -> p b a", b=NB)
        NM2 = sb("NM2", [128, 8, NB])
        ZZ2 = sb("ZZ2", [128, 8, NB])
        RZ2 = sb("RZ2", [128, 8, NB])
        NR2 = sb("NR2", [128, NB])
        SEL = sb("SEL", [2 * E1, E1], F16)
        ONB = sb("ONB", [2, 128], BF16)
        MK = ma(0, 2048).bitcast(BF16).rearrange("p (e n) -> p e n", e=E3)
        XM = [ma(2048 + 512 * i, 512) for i in range(2)]
        SG = [ma(3072 + 512 * i, 512) for i in range(2)]
        HM = [ma(4096 + 512 * i, 512) for i in range(4)]
        YT3 = ma(6144, 512, NB, N)

        RAW = ma(0, 1024, 8, D)
        RW0Q, RW0K, RW0V, RW0P, RW1V, RW2O, RW1Q, RW1K = range(8)
        RFC = ma(1024, 512, 4, D)
        RPJ = ma(1536, 512, 4, 128)
        RU = ma(2048, 64, 4, 16)
        RFB = ma(2112, 16)
        RVV = ma(2128, 128)
        R8 = ma(2256, 24, 3, HD)
        UT = ma(2304, 512, 4, 128)
        FBT = ma(2816, 16)
        FBV = ma(2832, 128)
        A8 = ma(2960, HD)
        BDV = ma(2968, 128)
        TP = ma(3104, 512, 4, D)
        TM = ma(3616, 512, 4, D)
        BSC = ma(4128, 16)
        SE = ma(4160, 1024, 8, D)
        VEC1 = ma(5184, 128)
        VEC2 = ma(5312, 128)
        MKI = ma(5440, 240).bitcast(I32).rearrange("p (a b) -> p a b", a=2)
        SST = ma(5680, 48, 8, 6)
        SMV = ma(5728, 16, 8, 2)
        SVE = ma(5744, 8)
        SRS = ma(5752, 8)
        MKF = ma(5760, S2)

        W1S = W1[:, :, :].bitcast(F16)
        W1G = ma(0, 4096, E1, F1)
        HALVES = [slice(0, E1 // 2), slice(E1 // 2, E1)]

        PS = ctx.enter_context(nc.psum_tensor("PS", [128, 8, 512], F32))

        def bank(k, lo=0, hi=512, rows=128):
            return PS[0:rows, k, lo:hi]

        def bank4(k, n=128, rows=128):
            return PS[0:rows, k, 0:4 * n].rearrange("p (b n) -> p b n", b=4)

        VC = {}
        at = 0
        for name, n in (("gamma", 8), ("beta", 8), ("b2", 8), ("b1", 32), ("norm_g", 1), ("norm_b", 1), ("slot_g", 1),
                        ("slot_b", 1), ("bq3", 1), ("bk3", 1), ("scale3", 1), ("bd", 16), ("cent", 8)):
            VC[name] = at
            at += n
        NV1 = at

        def vec(name, k=0):
            return VT1[:, VC[name] + k:VC[name] + k + 1]

        def turn(g, phase="a1"):
            i, off = g

            def v(name, k):
                n, turns = PER[name], TURNS[name[:2]]
                k = k + BASE.get(name, 0)
                t = turns * (off // 2) + START.get(phase, {}).get(name[:2], 0) + off % 2
                return t * n + k if i is None else i.times(turns * n, t * n + k)
            return v

        block = ctx.enter_context(nc.Block())

        def phases(eng, a1, m1, a2, m2, a3, m3, between=None):
            pairs = groups // 2

            def pair(i, last):
                def group(k):
                    return (None, 2 * i + k) if isinstance(i, int) else (i, k)
                A, B = group(0), group(1)
                weave("m1a1", m1(A, 0, range(M1H, M1N), ("m3_out", group(-1))),
                       a1(B, 1, ("a1_done", A)), m1(B, 1, range(M1H)))
                weave("m1a2", m1(B, 1, range(M1H, M1N), ("m1_done", A)),
                       a2(A, 0, ("a1_done", B)), m2(A, 0, range(M2H)))
                weave("m2a2", m2(A, 0, range(M2H, M2N), ("m1_done", B)),
                       a2(B, 1, ("a2_done", A)), m2(B, 1, range(M2H)))
                weave("m2a3", m2(B, 1, range(M2H, M2N), ("m2_done", A)),
                       a3(A, 0, ("a2_done", B)), m3(A, 0, range(M3H)))
                weave("m3a3", m3(A, 0, range(M3H, M3N), ("m2_done", B)),
                       a3(B, 1, ("a3_done", A)), m3(B, 1, range(M3H)))
                body = m3(B, 1, range(M3H, M3N), ("m3_out", A))
                if last:
                    alone(body)
                else:
                    C = group(2)
                    weave("m3a1", body, a1(C, 0, ("a3_done", B)), m1(C, 0, range(M1H)))

            alone(a1((None, 0), 0, None), m1((None, 0), 0, range(M1H)))
            if between is not None:
                between()
            if pairs > 1:
                with eng.Fori(0, pairs - 1) as i:
                    pair(Pair(eng, i), False)
            pair(pairs - 1, True)

        def last_of(eng, name, g):
            if g[0] is not None or g[1] >= 0:
                eng.wait_ge(sem[name], turn(g)(name, PER[name]))

        def first(eng, g, prev, *own):
            for name, k in own:
                eng.wait_ge(sem[name], turn(g)(name, k))
            if prev is not None:
                last_of(eng, *prev)

        def arrived(eng, sems, g, p):
            i, off = g
            eng.wait_ge(sems[p], 16 * (off // 2 + 1) if i is None else i.times(16, 16 * (off // 2 + 1)))

        @block.gpsimd
        def _(pool):
            pool.memset(IDN[:, :], 0.0)
            pool.memset(IDB[:, :], 0.0)
            pool.memset(ONE[:, :], 1.0)
            pool.memset(BD[:, :, :], 1.0)
            pool.memset(E8[:, :, :], 0.0)
            pool.memset(EXPO[:, :], -0.5)
            pool.memset(QK[:, :, :, :], 0.0)
            pool.memset(SEL[:, :], 0.0)
            pool.memset(ONB[:, :], 1.0)
            pool.memset(VAH[:, :, :, HD:HD + 1], 1.0)
            pool.memset(VAL[:, :, :, HD:HD + 1], 0.0).then_inc(setup["iota"], 1)
            pool.iota(RANK[:, :], [[-1, E1]], base=E1, channel_multiplier=0,
                      allow_small_or_imprecise_dtypes=True).then_inc(setup["iota"], 1)
            pool.wait_ge(setup["iota"], 2)
            for m in (IDN, IDB):
                pool.affine_select(out=m[:, :], in_=m[:, :], compare_op=ALU.not_equal, fill=1.0, base=0,
                                   pattern=[[-1, 128]], channel_multiplier=1)
            for k in range(2):
                sel = pool.affine_select(out=SEL[:, :], in_=SEL[:, :], compare_op=ALU.not_equal, fill=1.0, base=-E1 * k,
                                         pattern=[[-1, E1]], channel_multiplier=1)
                sel.then_inc(setup["iota"], 1)
                pool.wait_ge(setup["iota"], k + 3)
            pool.affine_select(out=E8[:, :, :], in_=E8[:, :, :], compare_op=ALU.not_equal, fill=1.0, base=0,
                               pattern=[[0, H], [-1, HD]], channel_multiplier=1)
            pool.affine_select(out=BD[:, :, :], in_=BD[:, :, :], compare_op=ALU.is_ge, fill=0.0, base=0,
                               pattern=[[-HD, H], [0, HD]], channel_multiplier=1).then_inc(setup["iota"], 1)
            pool.wait_ge(setup["iota"], 5)
            pool.affine_select(out=BD[:, :, :], in_=BD[:, :, :], compare_op=ALU.is_ge, fill=0.0, base=HD - 1,
                               pattern=[[HD, H], [0, HD]], channel_multiplier=-1).then_inc(setup["iota"], 1)
            pool.wait_ge(setup["sb"], 1)
            pool.tensor_scalar(SVE[:, :], SMV[:, :, 1], LN_EPS, None, ALU.add).then_inc(setup["slot_rs"], 1)
            pool.wait_ge(setup["slot_rs"], 1)
            pool.tensor_tensor(SRS[:, :], SVE[:, :], EXPO[:, 0:8], ALU.pow).then_inc(setup["slot_rs"], 1)

            def rstd(v, fam, j=0):
                pool.wait_ge(sem[f"{fam}_mv"], v(f"{fam}_mv", 3 * j + 3))
                pool.tensor_tensor(ARS[:, :], AVE[:, :], EXPO[:, 0:NB], ALU.pow).then_inc(sem[f"{fam}_rs"], 1)

            def rstd2(v):
                pool.wait_ge(sem["mn_mv"], v("mn_mv", 4))
                pool.tensor_tensor(MF[:, 1, :], MF[:, 0, :], EXPO[:, 0:NB], ALU.pow).then_inc(sem["mn_rs"], 1)

            def a1(g, p, prev):
                v = turn(g)

                def run():
                    first(pool, g, prev)
                    arrived(pool, x_in, g, p)
                    if prev is None:
                        pool.wait_ge(setup["bc_in"], 16 * 9)
                    yield
                    for s in range(1, A1N):
                        if s == A1S["xn0"]:
                            pool.wait_ge(sem["a1_xn"], v("a1_xn", 1))
                            pool.tensor_tensor(X[p][:, :, :], X[p][:, :, :], BC[:, BP0, :].unsqueeze(1).to_broadcast([128, NB, D]),
                                               ALU.add).then_inc(sem["a1_xb"], 1)
                        if s in (A1S["rs0"], A1S["rs1"], A1S["rs2"]):
                            rstd(v, "a1", (A1S["rs0"], A1S["rs1"], A1S["rs2"]).index(s))
                        yield
                return run(), A1N

            def attention(ph, g, p, prev):
                v = turn(g, ph)

                def run():
                    first(pool, g, prev, ("m1_done" if ph == "a2" else "m2_done", 1))
                    yield
                    rstd(v, "at")
                    yield
                    pool.wait_ge(sem["at_xn"], v("at_xn", 1))
                    bo = BO2 if ph == "a2" else BO3
                    pool.tensor_tensor(X[p][:, :, :], X[p][:, :, :], BC[:, bo, :].unsqueeze(1).to_broadcast([128, NB, D]),
                                       ALU.add).then_inc(sem["at_xb"], 1)
                    for s in range(2, ATN):
                        if s == 4:
                            v32 = C[p] if ph == "a2" else V32
                            if ph == "a3":
                                pool.wait_ge(sem["a3_v32"], v("a3_v32", 1))
                            src = v32[0:S2, :, :].rearrange("p b (h d) -> p (b h) d", h=H)
                            high = VAH[:, :, :, 0:HD].rearrange("p b h d -> p (b h) d")
                            low = VAL[:, :, :, 0:HD].rearrange("p b h d -> p (b h) d")
                            pool.tensor_tensor(high, src, ONE[0:S2, :].unsqueeze(1).to_broadcast([S2, NB * H, HD]),
                                               ALU.mult).then_inc(sem["at_v"], 1)
                            pool.wait_ge(sem["at_v"], v("at_v", 1))
                            pool.tensor_tensor(low, src, high, ALU.subtract).then_inc(sem["at_v"], 1)
                        for b in range(NB):
                            if s == (5 + 8 * b if b else 3):
                                if b >= 2:
                                    pool.wait_ge(sem["at_s_ps"], v("at_s_ps", 2 * b - 2))
                                if ph == "a3":
                                    pool.wait_ge(sem["a3_kt"], v("a3_kt", 1))
                                pool.tensor_tensor(KB[b % 2][:, :, :], CT[p][:, b, :].unsqueeze(1).to_broadcast([128, HU, S2]),
                                                   M8[:, :].unsqueeze(2).to_broadcast([128, HU, S2]),
                                                   ALU.mult).then_inc(sem["at_kb"], 1)
                        yield
                return run(), ATN

            def m1(g, p, steps, prev=None):
                v = turn(g, "m1")

                def run():
                    for s in steps:
                        if s == 1:
                            rstd(v, "mn")
                            rstd2(v)
                        if s == 3:
                            pool.wait_ge(sem["mn_xh"], v("mn_xh", 1))
                            pool.tensor_tensor(X[p][:, :, :], X[p][:, :, :], AN[:, :, :], ALU.add).then_inc(sem["m1_xx"], 1)
                        yield
                return run(), len(steps)

            def m2(g, p, steps, prev=None):
                v = turn(g, "m2")

                def run():
                    for s in steps:
                        if s == 1:
                            rstd(v, "mn")
                            rstd2(v)
                        k, j = divmod(s - 5 - 3, 3)
                        if j == 0 and 0 <= k < 8:
                            pool.wait_ge(sem["m2_rz"], v("m2_rz", k + 1))
                            pool.tensor_tensor(ED[k % 2][:, :, :], ED[k % 2][:, :, :],
                                               RZ2[:, k, :].unsqueeze(2).to_broadcast([128, NB, N]),
                                               ALU.mult).then_inc(sem["m2_ed"], 1)
                        yield
                return run(), len(steps)

            def m3(g, p, steps, prev=None):
                v = turn(g, "m3")

                def run():
                    for s in steps:
                        if s == 1:
                            rstd(v, "mn")
                            rstd2(v)
                        if s == 3:
                            pool.wait_ge(sem["mn_xh"], v("mn_xh", 1))
                            pool.tensor_tensor(X[p][:, :, :], X[p][:, :, :], AN[:, :, :], ALU.add).then_inc(sem["m3_xx"], 1)
                        yield
                return run(), len(steps)

            phases(pool, a1, m1, lambda *a: attention("a2", *a), m2, lambda *a: attention("a3", *a), m3)

        @block.scalar
        def _(act):
            def copy(dst, src, name):
                act.activation(dst, src, ACT.Copy).then_inc(sem[name], 1)

            act.wait_ge(setup["ps"], 1)
            act.activation(WT0[:, :, :], bank4(0), ACT.Copy)
            act.activation(WT1[:, :, :], bank(1, 0, 256).rearrange("p (a b) -> p a b", a=2), ACT.Copy)
            act.activation(VT1[:, 0:NV1], bank(2, 0, NV1), ACT.Copy)
            act.activation(VT2[:, :], bank(2, 128, 192), ACT.Copy)
            act.activation(A1[:, :], bank(3, 0, 128), ACT.Copy).then_inc(setup["act"], 1)
            act.wait_ge(setup["ps"], 5)
            act.activation(WPJ[:, :, :], bank4(0), ACT.Copy)
            act.activation(WFC[:, :], bank(1), ACT.Copy)
            act.wait_ge(setup["ps"], 6)
            act.wait_ge(setup["sb"], 6)
            for k in range(2):
                last = act.activation(SET[:, 512 * k:512 * k + 512], bank(2 + k), ACT.Identity,
                                      bias=SGB[:, 1:2], scale=SGB[:, 0:1])
            last.then_inc(setup["act"], 1)

            def a1(g, p, prev):
                v = turn(g)

                def run():
                    first(act, g, prev)
                    for s in range(A1N):
                        if s == A1S["ct"]:
                            act.wait_ge(sem["a1_ct_ps"], v("a1_ct_ps", 1))
                            copy(CT[p][:, :, :], bank4(1, S2), "a1_ct")
                        for j in range(3):
                            if s == A1S[f"xnt{j}"]:
                                act.wait_ge(sem["a1_xn_ps"], v("a1_xn_ps", j + 1))
                                copy(ANT[:, :, :], bank4(1 if j == 0 else 0), "a1_xnt")
                        if s == A1S["exp"]:
                            act.wait_ge(sem["a1_q"], v("a1_q", 3))
                            act.activation(QK[:, :, :, :], QK[:, :, :, :], ACT.Exp).then_inc(sem["a1_exp"], 1)
                        if s == A1S["qt"]:
                            act.wait_ge(sem["a1_qt_ps"], v("a1_qt_ps", 1))
                            copy(AQT[:, :, :], bank4(2), "a1_qt")
                        if s == A1S["ot"]:
                            act.wait_ge(sem["a1_ot_ps"], v("a1_ot_ps", 1))
                            copy(ANT[:, :, :], bank4(2), "a1_ot")
                        if s in (A1S["relu01"], A1S["relu23"]):
                            for c in (0, 1) if s == A1S["relu01"] else (2, 3):
                                act.wait_ge(sem["a1_h_ps"], v("a1_h_ps", c + 1))
                                if c >= 2:
                                    act.wait_ge(sem["a1_sq"], v("a1_sq", c - 1))
                                act.activation(R1[:, c % 2, :], bank((1, 2, 3, 0)[c]), ACT.Relu).then_inc(sem["a1_relu"], 1)
                        if s == A1S["t_sb"]:
                            act.wait_ge(sem["a1_v_ps"], v("a1_v_ps", 1))
                            copy(V1[0:S2, :, :], bank4(2, D, S2), "a1_v_sb")
                            act.wait_ge(sem["a1_t_ps"], v("a1_t_ps", 1))
                            act.activation(AQT[:, :, :], bank4(1), ACT.Copy, scale=float(D) ** -0.5).then_inc(sem["a1_t_sb"], 1)
                        if s == A1S["p"]:
                            act.wait_ge(sem["a1_nm"], v("a1_nm", 2))
                            for b in range(NB):
                                last = act.activation(SS[:, b, :], SS[:, b, :], ACT.Exp, bias=NM1[:, b:b + 1],
                                                      accum_out=SM1[:, b:b + 1])
                            last.then_inc(sem["a1_p"], 1)
                        if s == A1S["pt"]:
                            act.wait_ge(sem["a1_pt_ps"], v("a1_pt_ps", 1))
                            copy(PTT[0:S2, :, :], bank4(0, N, S2), "a1_pt")
                        yield
                return run(), A1N

            def attention(ph, g, p, prev):
                v = turn(g, ph)

                def run():
                    first(act, g, prev)
                    for s in range(ATN):
                        if s == 4:
                            act.wait_ge(sem["at_xn_ps"], v("at_xn_ps", 1))
                            copy(ANT[:, :, :], bank4(0), "at_xnt")
                        if s == 2 and ph == "a3":
                            act.wait_ge(sem["a3_k_ps"], v("a3_k_ps", 1))
                            act.wait_ge(sem["a3_v_ps"], v("a3_v_ps", 1))
                            act.activation(CT[p][:, :, :], bank4(2, S2), ACT.Identity, bias=vec("bk3")).then_inc(sem["a3_kt"], 1)
                        if s == 6:
                            act.wait_ge(sem["at_q_ps"], v("at_q_ps", 1))
                            if ph == "a2":
                                copy(AQT[:, :, :], bank4(1), "at_qt")
                            else:
                                act.activation(AQT[:, :, :], bank4(1), ACT.Identity, bias=vec("bq3")).then_inc(sem["at_qt"], 1)
                        for u in range(UNITS):
                            r = u % 2
                            j = s - 7 - 4 * u
                            if j == 2:
                                act.wait_ge(sem["at_sub"], v("at_sub", 2 * u + 2))
                                act.activation(EE[r][:, :, :], EE[r][:, :, :], ACT.Exp,
                                               scale=float(HD) ** -0.5).then_inc(sem["at_exp"], 1)
                            if j == 3:
                                act.wait_ge(sem["at_et_ps"], v("at_et_ps", u + 1))
                                if u >= 2:
                                    act.wait_ge(sem["at_pv_ps"], v("at_pv_ps", u - 1))
                                act.activation(ETH[r][0:S2].rearrange("p (a h) n -> p a (h n)", a=2), PS[0:S2, 2 * r:2 * r + 2, :],
                                               ACT.Copy).then_inc(sem["at_eth"], 1)
                        if s == ATN - 3:
                            act.wait_ge(sem["at_ot_ps"], v("at_ot_ps", 1))
                            copy(ANT[:, :, :], bank4(0), "at_ot")
                        yield
                return run(), ATN

            def m1(g, p, steps, prev=None):
                v = turn(g, "m1")
                MHT = MHTS[p]

                def run():
                    first(act, g, prev)
                    for s in steps:
                        if s == 4:
                            act.wait_ge(sem["m1_xn_ps"], v("m1_xn_ps", 1))
                            copy(ANT[:, :, :], bank4(0), "m1_xht")
                            act.wait_ge(sem["mn_xh_ps"], v("mn_xh_ps", 1))
                            copy(MHT[:, :, :].rearrange("p b n -> p (b n)").bitcast(F16)[:, 0:T], bank(1), "m1_xht")
                        if s == 7:
                            act.wait_ge(sem["m1_top"], v("m1_top", 14))
                            act.activation(SM4[:, 3, :], SM4[:, 2, :], ACT.Exp).then_inc(sem["m1_e2"], 1)
                        if s == 10:
                            act.wait_ge(sem["m1_cw_ps"], v("m1_cw_ps", 1))
                            copy(CWTS[p][:, :], bank(3, 0, T, 2 * E1), "m1_cwt")
                        if s >= 11:
                            e, c = divmod(s - 11, 4)
                            if e < E1:
                                act.wait_ge(sem["m1_up_ps"], v("m1_up_ps", 4 * e + c + 1))
                                if e:
                                    act.wait_ge(sem["m1_dn_ps"], v("m1_dn_ps", 4 * (e - 1) + c + 1))
                                act.activation(HID[:, c, :], bank(5 + (5 * e + c) % 3), ACT.Relu, scale=1.0 / WS,
                                               bias=B1P[:, 4 * e + c:4 * e + c + 1]).then_inc(sem["m1_ring"], 1)
                                if c == 3:
                                    act.wait_ge(sem["m1_cb_ps"], v("m1_cb_ps", e + 1))
                                    act.activation(CBC[:, e, :], bank(5 + (5 * e + 4) % 3), ACT.Copy).then_inc(sem["m1_ring"], 1)
                        yield
                return run(), len(steps)

            def m2(g, p, steps, prev=None):
                v = turn(g, "m2")
                MHT = MHTS[p]

                def run():
                    first(act, g, prev)
                    for s in steps:
                        if s == 4:
                            act.wait_ge(sem["mn_xh_ps"], v("mn_xh_ps", 1))
                            act.activation(MHT[:, :, :], bank4(0), ACT.Identity, bias=vec("norm_b"),
                                           scale=vec("norm_g")).then_inc(sem["m2_xpt"], 1)
                        k, j = divmod(s - 5 - 2, 3)
                        if j == 0 and 0 <= k < 8:
                            act.wait_ge(sem["m2_nm"], v("m2_nm", k + 1))
                            act.wait_ge(sem["m2_mx"], v("m2_mx", k + 1))
                            if k >= 2:
                                act.wait_ge(sem["m2_pd_ps"], v("m2_pd_ps", k - 1))
                            for b in range(NB):
                                last = act.activation(ED[k % 2][:, b, :], bank(4 + k % 2, 128 * b, 128 * b + 128), ACT.Exp,
                                                      bias=NM2[:, k, b:b + 1], accum_out=ZZ2[:, k, b:b + 1])
                            last.then_inc(sem["m2_ex"], 1)
                        k, j = divmod(s - 5 - 6,3)
                        if j == 0 and 0 <= k < 8:
                            act.wait_ge(sem["m2_pd_ps"], v("m2_pd_ps", k + 1))
                            if k >= 2:
                                act.wait_ge(sem["m2_sl_ps"], v("m2_sl_ps", k - 1))
                            copy(PD[k % 2][:, :, :], bank4(6), "m2_pd")
                        e, j = divmod(s - M2E, 3)
                        if 0 <= e < E2 and j < 2:
                            act.wait_ge(sem["m2_gu_ps"], v("m2_gu_ps", 2 * e + j + 1))
                            if e:
                                act.wait_ge(sem["m2_ht"], v("m2_ht", 2 * (e - 1) + j + 1))
                            act.activation(GL[:, j, :], bank(4 + j, 0, 256), ACT.Gelu,
                                           bias=VT2[:, 2 * e + j:2 * e + j + 1]).then_inc(sem["m2_gelu"], 1)
                        if 1 <= e <= E2 and j == 2:
                            f = e - 1
                            act.wait_ge(sem["m2_dn_ps"], v("m2_dn_ps", f + 1))
                            if f >= 4:
                                act.wait_ge(sem["m2_es_ps"], v("m2_es_ps", f // 2 - 1))
                            act.activation(EO[f // 2 % 2][:, :, SL2 * (f % 2):SL2 * (f % 2) + SL2],
                                           bank(6, 0, 256).rearrange("p (b s) -> p b s", b=NB), ACT.Identity,
                                           bias=vec("bd", f)).then_inc(sem["m2_eo"], 1)
                        if j == 1 and e % 2 == 1 and 3 <= e <= 17:
                            k = (e - 3) // 2
                            act.wait_ge(sem["m2_es_ps"], v("m2_es_ps", k + 1))
                            copy(ES[:, k, :, 0:D], bank4(7), "m2_es")
                        if s == M2E + 6:
                            act.wait_ge(sem["m2_nmt_ps"], v("m2_nmt_ps", 1))
                            copy(NMT[0:2, 0:T], bank(7, 0, T, 2), "m2_nmt")
                        k, j = divmod(s - M2C, 2)
                        if 0 <= k < 8 and j == 1:
                            act.wait_ge(sem["m2_l_ps"], v("m2_l_ps", k + 1))
                            if k >= 2:
                                act.wait_ge(sem["m2_cm_ps"], v("m2_cm_ps", k - 1))
                            act.activation(CTT[k % 2][:, :, :], bank4(4 + k % 2), ACT.Exp).then_inc(sem["m2_ctt"], 1)
                        yield
                return run(), len(steps)

            def m3(g, p, steps, prev=None):
                v = turn(g, "m3")
                MHT = MHTS[p]
                OHT = CWTS[p].bitcast(BF16)

                def run():
                    first(act, g, prev)
                    for s in steps:
                        if s == 4:
                            act.wait_ge(sem["mn_xh_ps"], v("mn_xh_ps", 1))
                            act.activation(MHT[:, :, :], bank4(1), ACT.Copy, scale=vec("scale3")).then_inc(sem["m3_xpt"], 1)
                            act.activation(SQT[:, :, :], bank4(1), ACT.Square, scale=vec("scale3")).then_inc(sem["m3_xpt"], 1)
                        if s == 8:
                            act.wait_ge(sem["m3_oh_ps"], v("m3_oh_ps", 1))
                            copy(OHT[0:E3, :], bank(3, 0, T, E3), "m3_oht")
                        if s == 10:
                            for e in range(E3):
                                act.wait_ge(sem["m3_mk_ps"], v("m3_mk_ps", e + 1))
                                copy(MK[:, e, :], bank(5 + e % 3), "m3_mk")
                        e, j = divmod(s - 11, 4)
                        if 0 <= e < E3 and j % 2 == 0:
                            n = 2 * e + j // 2
                            act.wait_ge(sem["m3_up_ps"], v("m3_up_ps", n + 1))
                            if n >= 2:
                                act.wait_ge(sem["m3_hm"], v("m3_hm", n - 1))
                            act.activation(SG[n % 2], bank(5 + 2 * n % 3), ACT.Tanh, scale=0.5).then_inc(sem["m3_silu"], 1)
                        if s == M3N - 3:
                            act.wait_ge(sem["m3_dn_ps"], v("m3_dn_ps", 2 * E3))
                            act.activation(YT3[:, :, :], bank4(4), ACT.Copy, scale=0.5).then_inc(sem["m3_yt"], 1)
                        yield
                return run(), len(steps)

            def high_w1():
                for k, part in enumerate(HALVES):
                    act.wait_ge(setup["sb"], 7 + k)
                    act.activation(W1S[:, part, 0:F1], W1G[:, part, :], ACT.Copy).then_inc(setup["act"], 1)

            phases(act, a1, m1, lambda *a: attention("a2", *a), m2, lambda *a: attention("a3", *a), m3, high_w1)

        @block.vector
        def _(dve):
            n_sb = [0]

            def did(ins):
                n_sb[0] += 1
                ins.then_inc(setup["va"], 1)
                dve.wait_ge(setup["va"], n_sb[0])

            dve.memset(PASS[:, 0:1], 0.0).then_inc(sem["m3_out"], BASE["m3_out"])
            dve.wait_ge(setup["iota"], 6)
            for r in range(2):
                last = dve.tensor_copy(M8[64 * r:64 * r + 64, :], BD[64 * r:64 * r + 64, HU * r:HU * r + HU, 0])
            last.then_inc(setup["m8"], 1)
            dve.wait_ge(setup["slot_in"], 16)
            for k in range(8):
                last = dve.bn_stats(SST[:, k, :], SE[:, k, :])
            did(last)
            for k in range(8):
                last = dve.bn_aggr(SMV[:, k, :], SST[:, k, :])
            last.then_inc(setup["sb"], 1)
            dve.wait_ge(setup["small_in"], 16 * 10)
            dve.tensor_scalar(MB1[:, :], MKI[:, 0, :], 0.0, -BIG, ALU.is_equal, ALU.mult)
            did(dve.tensor_scalar(MB2[:, :], MKI[:, 1, :], 0.0, -1e20, ALU.is_equal, ALU.mult))
            dve.tensor_reduce(BSC[:, 0:4], RFC[:, :, :], AX.X, ALU.add, apply_absolute_value=True)
            did(dve.tensor_reduce(BSC[:, 4:5], RPJ[:, :, :], AX.XY, ALU.add, apply_absolute_value=True))
            dve.tensor_scalar(BSC[:, 0:4], BSC[:, 0:4], 1.0 / D, 1e-5, ALU.mult, ALU.max)
            did(dve.tensor_scalar(BSC[:, 4:5], BSC[:, 4:5], 1.0 / F0, 1e-5, ALU.mult, ALU.max))
            dve.tensor_scalar(BSC[:, 5:10], BSC[:, 0:5], 0.5, None, ALU.mult)
            did(dve.tensor_scalar(BSC[:, 10:15], BSC[:, 0:5], -0.5, None, ALU.mult))
            for raw, col in ((RFC, 0), (RPJ, 4)):
                for c in range(4):
                    k = col + c if raw is RFC else 4
                    dve.tensor_scalar(TP[:, c, :], raw[:, c, :], BSC[:, 5 + k:6 + k], None, ALU.is_gt)
                    last = dve.tensor_scalar(TM[:, c, :], raw[:, c, :], BSC[:, 10 + k:11 + k], None, ALU.is_lt)
                did(last)
                did(dve.tensor_tensor(TP[:, :, :], TP[:, :, :], TM[:, :, :], ALU.subtract))
                did(dve.tensor_tensor(TP[:, :, :], TP[:, :, :], raw[:, :, :], ALU.subtract))
                did(dve.tensor_tensor(TP[:, :, :], TP[:, :, :], raw[:, :, :], ALU.add))
                for c in range(4):
                    k = col + c if raw is RFC else 4
                    last = dve.tensor_scalar(raw[:, c, :], TP[:, c, :], BSC[:, k:k + 1], None, ALU.mult)
                did(last)
            dve.wait_ge(setup["ps"], 2)
            dve.tensor_copy(UT[0:16, :, :], bank4(4, 128, 16))
            dve.tensor_copy(FBT[0:16, :], bank(5, 0, 16, 16))
            dve.tensor_copy(A8[0:HD, :], bank(5, 32, 32 + HD, HD))
            dve.wait_ge(setup["m8"], 1)
            dve.tensor_tensor(BDV[:, :], bank(5, 128, 256), BD[:, :, :].rearrange("p h d -> p (h d)"),
                              ALU.mult).then_inc(setup["sb"], 1)
            dve.wait_ge(setup["ps"], 3)
            dve.tensor_copy(FBV[0:16, :], bank(6, 0, 128, 16))
            dve.tensor_copy(W2O[:, :], bank(6, 128, 256))
            dve.tensor_tensor(BDA[:, :], bank(6, 256, 384), BD[:, :, :].rearrange("p h d -> p (h d)"),
                              ALU.mult).then_inc(setup["sb"], 1)
            dve.wait_ge(setup["bc_in"], 16 * 9)
            dve.wait_ge(setup["ps"], 4)
            for c in range(4):
                last = dve.scalar_tensor_tensor(RFC[:, c, :], bank(7, 128 * c, 128 * c + 128), SCL[:, 0:1], RFC[:, c, :],
                                                ALU.mult, ALU.add)
            last.then_inc(setup["sb"], 1)
            dve.wait_ge(setup["slot_rs"], 2)
            for k in range(8):
                last = dve.tensor_scalar(SE[:, k, :], SE[:, k, :], SMV[:, k, 0:1], SRS[:, k:k + 1],
                                         ALU.subtract, ALU.mult)
            last.then_inc(setup["sb"], 1)
            dve.wait_ge(setup["act"], 1)
            dve.tensor_scalar(SGB[:, 0:1], vec("slot_g"), SCL[:, 1:2], None, ALU.mult)
            dve.tensor_scalar(SGB[:, 1:2], vec("slot_b"), SCL[:, 1:2], None, ALU.mult)
            dve.tensor_scalar(CM2[:, :], VT1[:, VC["cent"]:VC["cent"] + E3], -2.0, None, ALU.mult)
            dve.tensor_tensor(CSQ[:, :], VT1[:, VC["cent"]:VC["cent"] + E3], VT1[:, VC["cent"]:VC["cent"] + E3],
                              ALU.mult).then_inc(setup["sb"], 1)

            def scale_w1():
                dve.wait_ge(setup["ps"], 7)
                dve.tensor_tensor(B1P[:, :], bank(4, 0, 4 * E1), VT1[:, VC["b1"]:VC["b1"] + 4 * E1], ALU.add)
                for part in HALVES:
                    for e in range(part.start, part.stop):
                        last = dve.tensor_scalar(W1G[:, e, :], W1[:, e, :], vec("gamma", e), WS, ALU.mult, ALU.mult)
                    last.then_inc(setup["sb"], 1)
                for k, part in enumerate(HALVES):
                    dve.wait_ge(setup["act"], 3 + k)
                    dve.tensor_tensor(W1S[:, part, F1:2 * F1], W1G[:, part, :], W1S[:, part, 0:F1],
                                      ALU.subtract).then_inc(setup["sb"], 1)

            def stats(v, fam, j, x, st, mv, eps=None):
                for b in range(NB):
                    last = dve.bn_stats(st[:, b, :], x[:, b, :])
                last.then_inc(sem[f"{fam}_mv"], 1)
                dve.wait_ge(sem[f"{fam}_mv"], v(f"{fam}_mv", 3 * j + 1))
                dve.memset(PASS[:, 2:3], 0.0)
                for b in range(NB):
                    last = dve.bn_aggr(mv[:, b, :], st[:, b, :])
                last.then_inc(sem[f"{fam}_mv"], 1)
                dve.wait_ge(sem[f"{fam}_mv"], v(f"{fam}_mv", 3 * j + 2))
                dve.tensor_scalar(AVE[:, :], mv[:, :, 1], LN_EPS, None, ALU.add).then_inc(sem[f"{fam}_mv"], 1)
                if fam == "mn":
                    dve.tensor_scalar(MF[:, 0, :], mv[:, :, 1], 1.0 + eps, eps * LN_EPS, ALU.mult,
                                      ALU.add).then_inc(sem["mn_mv"], 1)

            def norm(v, fam, j, x, xn, mv, rs):
                dve.wait_ge(sem[f"{fam}_rs"], v(f"{fam}_rs", j + 1))
                for b in range(NB):
                    last = dve.tensor_scalar(xn[:, b, :], x[:, b, :], mv[:, b, 0:1], rs[:, b:b + 1], ALU.subtract, ALU.mult)
                last.then_inc(sem[f"{fam}_xn"], 1)

            def a1(g, p, prev):
                v = turn(g)
                x = X[p]

                def after(name, k=1):
                    dve.wait_ge(sem["a1_" + name], v("a1_" + name, k))

                def run():
                    first(dve, g, prev)
                    arrived(dve, x_in, g, p)
                    if prev is None:
                        dve.wait_ge(setup["iota"], 2)
                    for s in range(A1N):
                        if s == A1S["ct_ps"]:
                            stats(v, "a1", 0, x, AST, AMV)
                        if s == A1S["xn0"]:
                            norm(v, "a1", 0, x, AN, AMV, ARS)
                        if s == A1S["kv_sb"]:
                            after("kv_ps", 1)
                            dve.tensor_tensor(QK[0:S2, 1, :, :], bank4(3, 128, S2),
                                              BC[0:S2, BK0, :].unsqueeze(1).to_broadcast([S2, NB, D]), ALU.add)
                            dve.memset(VV[:, :, D:D + 1], 1.0)
                            after("kv_ps", 2)
                            dve.tensor_tensor(VV[0:S2, :, 0:D], bank4(0, 128, S2),
                                              BC[0:S2, BV0, :].unsqueeze(1).to_broadcast([S2, NB, D]),
                                              ALU.add).then_inc(sem["a1_kv_sb"], 1)
                        if s == A1S["q_sb"]:
                            after("q_ps")
                            dve.tensor_tensor(QK[:, 0, :, :], bank4(2),
                                              BC[:, BQ0, :].unsqueeze(1).to_broadcast([128, NB, D]),
                                              ALU.add).then_inc(sem["a1_q"], 1)
                            qk = QK[:, :, :, :].rearrange("p a b (h d) -> p (a b h) d", h=H)
                            after("q", 1)
                            after("kv_sb")
                            dve.tensor_reduce(QKM[:, :], qk, AX.X, ALU.max).then_inc(sem["a1_q"], 1)
                            after("q", 2)
                            dve.tensor_tensor(qk, qk, QKM[:, :].unsqueeze(2).to_broadcast([128, 128, HD]),
                                              ALU.subtract).then_inc(sem["a1_q"], 1)
                        if s == A1S["qk"]:
                            qk = QK[:, :, :, :].rearrange("p a b (h d) -> p (a b h) d", h=H)
                            after("exp")
                            dve.tensor_reduce(QKS[:, :], qk, AX.X, ALU.add).then_inc(sem["a1_qk"], 1)
                            after("qk", 1)
                            dve.reciprocal(QKR[:, :], QKS[:, :]).then_inc(sem["a1_qk"], 1)
                            after("qk", 2)
                            dve.tensor_tensor(qk, qk, QKR[:, :].unsqueeze(2).to_broadcast([128, 128, HD]),
                                              ALU.mult).then_inc(sem["a1_qk"], 1)
                        if s == A1S["kvm"]:
                            for h in range(2):
                                after("kvs_ps", h + 1)
                                ps = bank((1, 3)[h]).rearrange("p (b n) -> p b n", b=2)
                                dve.tensor_tensor(KVM[:, 2 * h:2 * h + 2, 0:D], ps[:, :, 0:D],
                                                  BD[:, :, :].rearrange("p h d -> p (h d)").unsqueeze(1).to_broadcast([128, 2, D]),
                                                  ALU.mult)
                                last = dve.tensor_tensor(KVM[:, 2 * h:2 * h + 2, D:D + H], ps[:, :, D:D + 1].to_broadcast([128, 2, H]),
                                                         BD[:, :, 0].unsqueeze(1).to_broadcast([128, 2, H]), ALU.mult)
                            last.then_inc(sem["a1_kvm"], 1)
                        if s == A1S["o"]:
                            for h in range(2):
                                after("num_ps", h + 1)
                                ps = bank((0, 1)[h]).rearrange("p (b n) -> p b n", b=2)
                                last = dve.reciprocal(DIN[:, 2 * h:2 * h + 2, :], ps[:, :, D:D + H])
                            last.then_inc(sem["a1_o"], 1)
                            after("o", 1)
                            for h in range(2):
                                ps = bank((0, 1)[h]).rearrange("p (b n) -> p b n", b=2)
                                for b in range(2):
                                    last = dve.tensor_tensor(OO[:, 2 * h + b, :].rearrange("p (h d) -> p h d", h=H),
                                                             ps[:, b, 0:D].rearrange("p (h d) -> p h d", h=H),
                                                             DIN[:, 2 * h + b, :].unsqueeze(2).to_broadcast([128, H, HD]), ALU.mult)
                            last.then_inc(sem["a1_o"], 1)
                            after("o", 2)
                            dve.tensor_tensor(OO[:, :, :], OO[:, :, :], QK[:, 0, :, :], ALU.add).then_inc(sem["a1_o"], 1)
                        if s == A1S["x0"]:
                            after("proj_ps")
                            after("xb")
                            dve.tensor_tensor(x[:, :, :], bank4(3), x[:, :, :], ALU.add).then_inc(sem["a1_x"], 1)
                            after("x", 1)
                            stats(v, "a1", 1, x, AST, AMV)
                        if s == A1S["xn1"]:
                            norm(v, "a1", 1, x, AN, AMV, ARS)
                        if s in (A1S["relu01"], A1S["relu23"]):
                            for c in (0, 1) if s == A1S["relu01"] else (2, 3):
                                after("relu", c + 1)
                                dve.scalar_tensor_tensor(R2[:, c, :], bank((1, 2, 3, 0)[c]), 0.0, R1[:, c % 2, :],
                                                         ALU.max, ALU.mult).then_inc(sem["a1_sq"], 1)
                        if s == A1S["x1"]:
                            after("dn_ps")
                            dve.tensor_tensor(x[:, :, :], bank4(1), x[:, :, :], ALU.add).then_inc(sem["a1_x"], 1)
                            after("x", 2)
                            stats(v, "a1", 2, x, AST, AMV)
                        if s == A1S["xn2"]:
                            norm(v, "a1", 2, x, AN, AMV, ARS)
                        if s == A1S["nm"]:
                            after("s_ps")
                            dve.tensor_tensor(SS[:, :, :], bank4(3, S2), MB1[:, :].unsqueeze(1).to_broadcast([128, NB, S2]),
                                              ALU.add).then_inc(sem["a1_nm"], 1)
                            after("nm", 1)
                            dve.tensor_reduce(NM1[:, :], SS[:, :, :], AX.X, ALU.max, negate=True).then_inc(sem["a1_nm"], 1)
                        if s == A1S["pt"]:
                            after("p")
                            dve.reciprocal(RM1[:, :], SM1[:, :]).then_inc(sem["a1_rsm"], 1)
                        if s == A1S["done"]:
                            after("pv_ps")
                            after("rsm")
                            for b in range(NB):
                                last = dve.scalar_tensor_tensor(x[:, b, :], bank(1, 128 * b, 128 * b + 128), RM1[:, b:b + 1],
                                                                x[:, b, :], ALU.mult, ALU.add)
                            last.then_inc(sem["a1_done"], 1)
                        yield
                return run(), A1N

            def attention(ph, g, p, prev):
                v = turn(g, ph)
                x = X[p]

                def after(name, k=1):
                    own = ("a3_" if name in ("k_ps", "kt", "v_ps", "v32") else "at_") + name
                    dve.wait_ge(sem[own], v(own, k))

                def run():
                    first(dve, g, prev, ("m1_done" if ph == "a2" else "m2_done", 1))
                    for s in range(ATN):
                        if s == 0:
                            stats(v, "at", 0, x, AST, AMV)
                        if s == 2:
                            norm(v, "at", 0, x, AN, AMV, ARS)
                        if s == 3 and ph == "a3":
                            after("v_ps")
                            dve.tensor_tensor(V32[0:S2, :, :], bank4(3, 128, S2),
                                              BC[0:S2, BV3, :].unsqueeze(1).to_broadcast([S2, NB, D]),
                                              ALU.add).then_inc(sem["a3_v32"], 1)
                        for u in range(UNITS):
                            r, b = u % 2, u // 2
                            j = s - 7 - 4 * u
                            sp = PS[:, 2 * r:2 * r + 2, 0:4 * S2].rearrange("p a (h k) -> p a h k", h=4)
                            if j == 1:
                                after("s_ps", u + 1)
                                dve.tensor_reduce(MXU[:, r, :].rearrange("p (a h) -> p a h", a=2), sp, AX.X,
                                                  ALU.max).then_inc(sem["at_sub"], 1)
                                after("sub", 2 * u + 1)
                                if u >= 2:
                                    after("et_ps", u - 1)
                                elif ph == "a3":
                                    after("v", 2)
                                dve.tensor_tensor(EE[r][:, :, :].rearrange("p (a h) k -> p a h k", a=2), sp,
                                                  MXU[:, r, :].rearrange("p (a h) -> p a h", a=2).unsqueeze(3).to_broadcast([128, 2, 4, S2]),
                                                  ALU.subtract).then_inc(sem["at_sub"], 1)
                            if j == 4:
                                after("eth", u + 1)
                                dve.tensor_tensor(ETL[r][0:S2].rearrange("p (a h) n -> p a (h n)", a=2), PS[0:S2, 2 * r:2 * r + 2, :],
                                                  ETH[r][0:S2].rearrange("p (a h) n -> p a (h n)", a=2),
                                                  ALU.subtract).then_inc(sem["at_etl"], 1)
                            if j == 6:
                                after("pv_ps", u + 1)
                                o = bank(2 * r, 0, HU * (HD + 1)).rearrange("p (h d) -> p h d", h=HU)
                                dve.reciprocal(RDU[:, r, :], o[:, :, HD]).then_inc(sem["at_on"], 1)
                                after("on", 2 * u + 1)
                                dve.tensor_tensor(OB[:, b, 64 * r:64 * r + 64].rearrange("p (h d) -> p h d", h=HU), o[:, :, 0:HD],
                                                  RDU[:, r, :].unsqueeze(2).to_broadcast([128, HU, HD]),
                                                  ALU.mult).then_inc(sem["at_on"], 1)
                        if s == ATN - 1:
                            after("proj_ps")
                            after("xb")
                            dve.tensor_tensor(x[:, :, :], bank4(1), x[:, :, :], ALU.add).then_inc(sem[f"{ph}_done"], 1)
                        yield
                return run(), ATN

            def head(s, v, x, eps, *own):
                if s == 0:
                    for name in own:
                        dve.wait_ge(sem[name], v(name, 1))
                    stats(v, "mn", 0, x, AST, AMV, eps)
                if s == 2:
                    norm(v, "mn", 0, x, AN, AMV, ARS)
                    dve.wait_ge(sem["mn_rs"], v("mn_rs", 2))
                    for b in range(NB):
                        last = dve.tensor_scalar(MH[:, b, :], x[:, b, :], AMV[:, b, 0:1], MF[:, 1, b:b + 1],
                                                 ALU.subtract, ALU.mult)
                    last.then_inc(sem["mn_xh"], 1)

            def m1(g, p, steps, prev=None):
                v = turn(g, "m1")
                MHT = MHTS[p]
                x = X[p]

                def after(name, k=1):
                    dve.wait_ge(sem["m1_" + name], v("m1_" + name, k))

                def link(ins, k):
                    ins.then_inc(sem["m1_top"], 1)
                    after("top", k)

                def run():
                    first(dve, g, prev)
                    for s in steps:
                        head(s, v, x, 1e-6, "a1_done")
                        if s == 4:
                            after("xht", 2)
                            flat = MHT[:, :, :].rearrange("p b n -> p (b n)").bitcast(F16)
                            dve.tensor_tensor(flat[:, T:2 * T], bank(1), flat[:, 0:T], ALU.subtract).then_inc(sem["m1_xlo"], 1)

                        def wide(k):
                            return SM4[:, k, :].unsqueeze(2).to_broadcast([128, NB, E1])
                        if s == 6:
                            after("sc_ps")
                            rank = RANK[:, :].unsqueeze(1).to_broadcast([128, NB, E1])
                            link(dve.tensor_copy(SMALL[:, 0], bank(2, 0, NB * E1).rearrange("p (b e) -> p b e", b=NB)), 1)
                            link(dve.tensor_reduce(SM4[:, 0, :], SMALL[:, 0], AX.X, ALU.max), 2)
                            link(dve.tensor_tensor(SMALL[:, 1], SMALL[:, 0], wide(0), ALU.is_equal), 3)
                            link(dve.tensor_tensor(SMALL[:, 2], SMALL[:, 1], rank, ALU.mult), 4)
                            link(dve.tensor_reduce(SM4[:, 4, :], SMALL[:, 2], AX.X, ALU.max), 5)
                            link(dve.tensor_tensor(SMALL[:, 3], SMALL[:, 2], wide(4), ALU.is_equal), 6)
                            link(dve.tensor_scalar(SMALL[:, 4], SMALL[:, 3], -BIG, None, ALU.mult), 7)
                            link(dve.tensor_tensor(SMALL[:, 5], SMALL[:, 4], SMALL[:, 0], ALU.add), 8)
                            link(dve.tensor_reduce(SM4[:, 1, :], SMALL[:, 5], AX.X, ALU.max), 9)
                            link(dve.tensor_tensor(SMALL[:, 6], SMALL[:, 5], wide(1), ALU.is_equal), 10)
                            link(dve.tensor_tensor(SMALL[:, 7], SMALL[:, 6], rank, ALU.mult), 11)
                            link(dve.tensor_reduce(SM4[:, 5, :], SMALL[:, 7], AX.X, ALU.max), 12)
                            link(dve.tensor_tensor(SMALL[:, 8], SMALL[:, 7], wide(5), ALU.is_equal), 13)
                            link(dve.tensor_tensor(SM4[:, 2, :], SM4[:, 1, :], SM4[:, 0, :], ALU.subtract), 14)
                        if s == 8:
                            after("e2")
                            link(dve.tensor_scalar(SM4[:, 6, :], SM4[:, 3, :], 1.0, None, ALU.add), 15)
                            link(dve.reciprocal(SM4[:, 7, :], SM4[:, 6, :]), 16)
                            dve.tensor_tensor(SMALL[:, 9], SMALL[:, 3], wide(7), ALU.mult)
                            link(dve.tensor_tensor(SMALL[:, 10], SMALL[:, 8], wide(7), ALU.mult), 17)
                            link(dve.tensor_tensor(SMALL[:, 11], SMALL[:, 10], wide(3), ALU.mult), 18)
                            link(dve.tensor_tensor(SMALL[:, 12], SMALL[:, 11], SMALL[:, 9], ALU.add), 19)
                            link(dve.tensor_copy(CWH, SMALL[:, 12]), 20)
                            dve.tensor_copy(CWF[:, :, 0:E1], CWH).then_inc(sem["m1_top"], 1)
                            dve.tensor_tensor(CWF[:, :, E1:2 * E1], SMALL[:, 12], CWH, ALU.subtract).then_inc(sem["m1_top"], 1)
                        if s >= 11 + 7 and (s - 11) % 4 == 3:
                            e = (s - 11) // 4 - 1
                            after("dn_ps", 4 * e + 4)
                            after("ring", 5 * e + 5)
                            if e >= 2:
                                after("acc", e - 1)
                            dst = ACC[:, :, :].rearrange("p b n -> p (b n)") if e == 0 else YT[:, :]
                            dve.scalar_tensor_tensor(dst, bank(4), vec("b2", e), CBC[:, e, :],
                                                     ALU.add, ALU.mult).then_inc(sem["m1_t"], 1)
                            if e:
                                after("t", e + 1)
                                dve.tensor_tensor(ACC[:, :, :].rearrange("p b n -> p (b n)"), ACC[:, :, :].rearrange("p b n -> p (b n)"),
                                                  YT[:, :], ALU.add).then_inc(sem["m1_acc"], 1)
                        if s == M1N - 1:
                            after("y_ps")
                            after("xx")
                            dve.tensor_tensor(x[:, :, :], bank4(5), x[:, :, :], ALU.add).then_inc(sem["m1_done"], 1)
                        yield
                return run(), len(steps)

            def m2(g, p, steps, prev=None):
                v = turn(g, "m2")
                MHT = MHTS[p]
                x = X[p]

                def after(name, k=1):
                    dve.wait_ge(sem["m2_" + name], v("m2_" + name, k))

                def run():
                    first(dve, g, prev)
                    for s in steps:
                        head(s, v, x, LN_EPS, "a2_done")
                        k, j = divmod(s - 5, 3)
                        if j == 1 and 0 <= k < 8:
                            after("lt_ps", k + 1)
                            if k:
                                after("mx", k)
                            dve.tensor_reduce(NM2[:, k, :], bank4(4 + k % 2), AX.X, ALU.max, negate=True).then_inc(sem["m2_nm"], 1)
                            last = dve.tensor_copy(MXS[:, :, :], bank4(4)) if k == 0 else \
                                dve.tensor_tensor(MXS[:, :, :], bank4(4 + k % 2), MXS[:, :, :], ALU.max)
                            last.then_inc(sem["m2_mx"], 1)
                        k, j = divmod(s - 5 - 3, 3)
                        if j == 0 and 0 <= k < 8:
                            after("ex", k + 1)
                            dve.reciprocal(RZ2[:, k, :], ZZ2[:, k, :]).then_inc(sem["m2_rz"], 1)
                        k, j = divmod(s - 5 - 8,3)
                        if j == 0 and 0 <= k < 8:
                            after("sl_ps", k + 1)
                            for a in range(2):
                                last = dve.tensor_scalar(SL[:, 2 * k + a, :, :], bank4(7)[:, :, 64 * a:64 * a + 64], vec("norm_g"),
                                                         vec("norm_b"), ALU.mult, ALU.add)
                            last.then_inc(sem["m2_sl"], 1)
                        e, j = divmod(s - M2E, 3)
                        if 0 <= e < E2 and j < 2:
                            after("gelu", 2 * e + j + 1)
                            if e >= 2:
                                after("dn_ps", e - 1)
                            dve.scalar_tensor_tensor(HT[e % 2][:, j, :], bank(4 + j, 256, 512), VT2[:, 32 + 2 * e + j:33 + 2 * e + j],
                                                     GL[:, j, :], ALU.add, ALU.mult).then_inc(sem["m2_ht"], 1)
                        if s == M2E + 3:
                            after("mxt_ps")
                            dve.tensor_reduce(MX4, bank4(7), AX.X, ALU.max, negate=True).then_inc(sem["m2_hl"], 1)
                            after("hl", 1)
                            dve.tensor_copy(MXH, MX4).then_inc(sem["m2_hl"], 1)
                            after("hl", 2)
                            dve.tensor_copy(HLF[:, :, 0], MXH)
                            dve.tensor_tensor(HLF[:, :, 1], MX4, MXH, ALU.subtract).then_inc(sem["m2_hl"], 1)
                        if s == M2C - 1:
                            after("dn_ps", E2)
                            dve.memset(ES[:, :, :, D:D + 1], 1.0).then_inc(sem["m2_nr"], 1)
                        if s == M2N - 1:
                            after("cm_ps", 8)
                            for h in range(2):
                                last = dve.reciprocal(NR2[:, 2 * h:2 * h + 2], PS[:, 6 + h, 0:2 * (D + 1)].rearrange("p (b n) -> p b n", b=2)[:, :, D])
                            last.then_inc(sem["m2_nr"], 1)
                            after("nr", 2)
                            for b in range(NB):
                                at = (D + 1) * (b % 2)
                                last = dve.scalar_tensor_tensor(x[:, b, :], bank(6 + b // 2, at, at + D), NR2[:, b:b + 1],
                                                                x[:, b, :], ALU.mult, ALU.add)
                            last.then_inc(sem["m2_done"], 1)
                        yield
                return run(), len(steps)

            def m3(g, p, steps, prev=None):
                v = turn(g, "m3")
                MHT = MHTS[p]
                x = X[p]

                def after(name, k=1):
                    dve.wait_ge(sem["m3_" + name], v("m3_" + name, k))

                def link(ins, k):
                    ins.then_inc(sem["m3_top"], 1)
                    after("top", k)

                def run():
                    first(dve, g, prev)
                    for s in steps:
                        head(s, v, x, 1e-6, "a3_done")
                        if s == 6:
                            after("ds_ps")
                            link(dve.tensor_copy(SMALL[:, 0], bank(2, 0, NB * E3).rearrange("p (b e) -> p b e", b=NB)), 1)
                            link(dve.tensor_reduce(SM4[:, 0, :], SMALL[:, 0], AX.X, ALU.min), 2)
                            link(dve.tensor_tensor(SMALL[:, 1], SMALL[:, 0], SM4[:, 0, :].unsqueeze(2).to_broadcast([128, NB, E3]),
                                                   ALU.is_equal), 3)
                            link(dve.tensor_tensor(SMALL[:, 2], SMALL[:, 1], RANK[:, :].unsqueeze(1).to_broadcast([128, NB, E3]),
                                                   ALU.mult), 4)
                            link(dve.tensor_reduce(SM4[:, 1, :], SMALL[:, 2], AX.X, ALU.max), 5)
                            dve.tensor_tensor(SMALL[:, 3], SMALL[:, 2], SM4[:, 1, :].unsqueeze(2).to_broadcast([128, NB, E3]),
                                              ALU.is_equal).then_inc(sem["m3_top"], 1)
                        for e in range(E3):
                            if s == max(10, 11 + 4 * e - 4):
                                after("mk", e + 1)
                                after("xpt", 1)
                                if e >= 2:
                                    after("up_ps", 2 * e - 2)
                                dve.tensor_tensor(XM[e % 2], MHT[:, :, :].rearrange("p b n -> p (b n)"), MK[:, e, :],
                                                  ALU.mult).then_inc(sem["m3_xm"], 1)
                        e, j = divmod(s - 11, 4)
                        if 0 <= e < E3 and j % 2 == 0:
                            n = 2 * e + j // 2
                            after("silu", n + 1)
                            if n >= 4:
                                after("dn_ps", n - 3)
                            dve.scalar_tensor_tensor(SG[n % 2], SG[n % 2], 1.0, bank(5 + 2 * n % 3), ALU.add,
                                                     ALU.mult).then_inc(sem["m3_sg"], 1)
                            after("sg", n + 1)
                            dve.tensor_tensor(HM[n % 4], bank(5 + (2 * n + 1) % 3), SG[n % 2], ALU.mult).then_inc(sem["m3_hm"], 1)
                        if s == M3N - 1:
                            after("y_ps")
                            after("xx")
                            dve.tensor_tensor(x[:, :, :], bank4(5), x[:, :, :], ALU.add).then_inc(sem["m3_out"], 1)
                        yield
                return run(), len(steps)

            phases(dve, a1, m1, lambda *a: attention("a2", *a), m2, lambda *a: attention("a3", *a), m3, scale_w1)

        @block.tensor
        def _(pe):
            mm = pe.matmul

            def flip(k, src, rows=128, cols=128, n=4):
                for b in range(n):
                    last = pe.transpose(PS[0:cols, k, rows * b:rows * b + rows], src[0:rows, b, :], IDN[0:rows, 0:rows])
                return last

            pe.wait_ge(setup["iota"], 6)
            pe.wait_ge(setup["m8"], 1)
            pe.wait_ge(setup["mat_in"], 16 * 27)
            flip(0, RAW[:, 0:4, :])
            flip(1, RAW[:, 4:6, :], n=2)
            pe.transpose(PS[:, 2, 0:NV1], VEC1[0:NV1, :], IDN[0:NV1, 0:NV1])
            pe.transpose(PS[:, 2, 128:192], VEC2[0:64, :], IDN[0:64, 0:64])
            mm(bank(3, 0, 128), RAW[:, RW1Q, :], RAW[:, RW1K, :], start=True, stop=True).then_inc(setup["ps"], 1)
            pe.wait_ge(setup["small_in"], 16 * 10)
            flip(4, RU, 128, 16)
            pe.transpose(PS[0:16, 5, 0:16], RFB[0:16, :], IDN[0:16, 0:16])
            mm(bank(5, 32, 32 + HD, HD), R8[0:HD, 0, :], R8[0:HD, 1, :], start=True, stop=True)
            e8 = E8[:, :, :].rearrange("k h d -> k (h d)")
            mm(bank(5, 128, 256), e8, R8[0:HD, 2, :].unsqueeze(1).to_broadcast([HD, H, HD]), start=True,
               stop=True).then_inc(setup["ps"], 1)
            pe.wait_ge(setup["sb"], 2)
            pe.wait_ge(setup["act"], 1)
            mm(bank(6, 0, 128, 16), FBT[0:16, :], RVV[0:16, :], start=True, stop=True)
            mm(bank(6, 128, 256), BDV[:, :], WT1[:, 1, :], start=True, stop=True)
            mm(bank(6, 256, 384), e8, A8[0:HD, :].unsqueeze(1).to_broadcast([HD, H, HD]), start=True,
               stop=True).then_inc(setup["ps"], 1)
            pe.wait_ge(setup["sb"], 3)
            for c in range(4):
                last = mm(bank(7, 128 * c, 128 * c + 128), UT[0:16, c, :], FBV[0:16, :], start=True, stop=True)
            last.then_inc(setup["ps"], 1)
            pe.wait_ge(setup["sb"], 4)
            flip(0, RPJ)
            flip(1, RFC).then_inc(setup["ps"], 1)
            pe.wait_ge(setup["sb"], 5)
            flip(2, SE[:, 0:4, :])
            flip(3, SE[:, 4:8, :]).then_inc(setup["ps"], 1)

            def beta_w1():
                pe.wait_ge(setup["w1_in"], 16)
                for e in range(E1):
                    for c in range(4):
                        last = mm(bank(4, 4 * e + c, 4 * e + c + 1), W1[:, e, 128 * c:128 * c + 128], vec("beta", e),
                                  start=True, stop=True)
                last.then_inc(setup["ps"], 1)

            def a1(g, p, prev):
                v = turn(g)

                def after(name, k=1):
                    pe.wait_ge(sem["a1_" + name], v("a1_" + name, k))

                def inc(ins, name):
                    ins.then_inc(sem["a1_" + name], 1)

                def run():
                    first(pe, g, prev)
                    arrived(pe, c_in, g, p)
                    if prev is None:
                        pe.wait_ge(setup["act"], 2)
                    for s in range(A1N):
                        if s == A1S["ct_ps"]:
                            flip(1, C[p], S2, D).then_inc(sem["a1_ct_ps"], 1)
                        if s == A1S["kv_ps"]:
                            after("ct")
                            for b in range(NB):
                                last = mm(bank(3, 128 * b, 128 * b + 128, S2), CT[p][:, b, :], WT0[:, 1, :], start=True, stop=True)
                            last.then_inc(sem["a1_kv_ps"], 1)
                            for b in range(NB):
                                last = mm(bank(0, 128 * b, 128 * b + 128, S2), CT[p][:, b, :], WT0[:, 2, :], start=True, stop=True)
                            last.then_inc(sem["a1_kv_ps"], 1)
                        for j in range(3):
                            if s == A1S[f"xn_ps{j}"]:
                                after("xn", j + 1)
                                flip(1 if j == 0 else 0, AN).then_inc(sem["a1_xn_ps"], 1)
                        if s == A1S["q_ps"]:
                            after("xnt", 1)
                            for b in range(NB):
                                last = mm(bank(2, 128 * b, 128 * b + 128), ANT[:, b, :], WT0[:, 0, :], start=True, stop=True)
                            last.then_inc(sem["a1_q_ps"], 1)
                        if s == A1S["kvs_ps"]:
                            after("qk", 3)
                            for h in range(2):
                                for b in range(2):
                                    last = mm(bank((1, 3)[h], 256 * b, 256 * b + D + 1), QK[0:S2, 1, 2 * h + b, :],
                                              VV[0:S2, 2 * h + b, :], start=True, stop=True)
                                last.then_inc(sem["a1_kvs_ps"], 1)
                            flip(2, QK[:, 0]).then_inc(sem["a1_qt_ps"], 1)
                        if s == A1S["num_ps"]:
                            after("kvm")
                            after("qt")
                            for h in range(2):
                                for b in range(2):
                                    last = mm(bank((0, 1)[h], 256 * b, 256 * b + D + H), AQT[:, 2 * h + b, :],
                                              KVM[:, 2 * h + b, :], start=True, stop=True)
                                last.then_inc(sem["a1_num_ps"], 1)
                        if s == A1S["ot_ps"]:
                            after("o", 3)
                            flip(2, OO).then_inc(sem["a1_ot_ps"], 1)
                        if s == A1S["proj_ps"]:
                            after("ot")
                            for b in range(NB):
                                last = mm(bank(3, 128 * b, 128 * b + 128), ANT[:, b, :], WT0[:, 3, :], start=True, stop=True)
                            last.then_inc(sem["a1_proj_ps"], 1)
                        if s in (A1S["h01"], A1S["h23"]):
                            after("xnt", 2)
                            for c in (0, 1) if s == A1S["h01"] else (2, 3):
                                mm(bank((1, 2, 3, 0)[c]), WFC[:, 128 * c:128 * c + 128], ANT[:, :, :], start=True,
                                   stop=True).then_inc(sem["a1_h_ps"], 1)
                        if s == A1S["dn_ps"]:
                            after("sq", 4)
                            for b in range(NB):
                                for c in range(4):
                                    last = mm(bank(1, 128 * b, 128 * b + 128), R2[:, c, 128 * b:128 * b + 128], WPJ[:, c, :],
                                              start=(c == 0), stop=(c == 3))
                            last.then_inc(sem["a1_dn_ps"], 1)
                        if s == A1S["v_ps"]:
                            for b in range(NB):
                                last = mm(bank(2, 128 * b, 128 * b + 128, S2), CT[p][:, b, :], WT1[:, 0, :], start=True, stop=True)
                            last.then_inc(sem["a1_v_ps"], 1)
                            after("xnt", 3)
                            mm(bank(1), A1[:, :], ANT[:, :, :], start=True, stop=True).then_inc(sem["a1_t_ps"], 1)
                        if s == A1S["s_ps"]:
                            after("t_sb")
                            for b in range(NB):
                                last = mm(bank(3, S2 * b, S2 * b + S2), AQT[:, b, :], CT[p][:, b, :], start=True, stop=True)
                            last.then_inc(sem["a1_s_ps"], 1)
                        if s == A1S["pt_ps"]:
                            after("p")
                            for b in range(NB):
                                last = pe.transpose(bank(0, 128 * b, 128 * b + 128, S2), SS[:, b, :], IDN[:, :])
                            last.then_inc(sem["a1_pt_ps"], 1)
                        if s == A1S["pv_ps"]:
                            after("pt")
                            after("v_sb")
                            for b in range(NB):
                                last = mm(bank(1, 128 * b, 128 * b + 128), PTT[0:S2, b, :], V1[0:S2, b, :], start=True, stop=True)
                            last.then_inc(sem["a1_pv_ps"], 1)
                        yield
                return run(), A1N

            def attention(ph, g, p, prev):
                v = turn(g, ph)

                def after(name, k=1):
                    own = ("a3_" if name in ("k_ps", "kt", "v_ps", "v32") else "at_") + name
                    pe.wait_ge(sem[own], v(own, k))

                def run():
                    first(pe, g, prev)
                    for s in range(ATN):
                        if s == 1 and ph == "a3":
                            mm(bank(2, 0, NB * S2), W3[:, 1, :], CT[p][:, :, :], start=True, stop=True).then_inc(sem["a3_k_ps"], 1)
                            for b in range(NB):
                                last = mm(bank(3, 128 * b, 128 * b + 128, S2), CT[p][:, b, :], W3[:, 2, :], start=True, stop=True)
                            last.then_inc(sem["a3_v_ps"], 1)
                        if s == 3:
                            after("xn")
                            flip(0, AN).then_inc(sem["at_xn_ps"], 1)
                        if s == 5:
                            after("xnt")
                            mm(bank(1), BDA[:, :] if ph == "a2" else W3[:, 0, :], ANT[:, :, :], start=True,
                               stop=True).then_inc(sem["at_q_ps"], 1)
                        for u in range(UNITS):
                            r, b = u % 2, u // 2
                            j = s - 7 - 4 * u
                            if j == 0:
                                if u == 0:
                                    after("qt")
                                if r == 0:
                                    after("kb", b + 1)
                                if u >= 2:
                                    after("on", 2 * u - 2)
                                elif ph == "a3":
                                    after("kt")
                                    after("v32")
                                for q in range(2):
                                    last = mm(bank(2 * r + q, 0, 4 * S2), AQT[64 * r:64 * r + 64, b, :],
                                              KB[b % 2][64 * r:64 * r + 64, 4 * q:4 * q + 4, :], start=True, stop=(ph == "a3"))
                                    if ph == "a2":
                                        last = mm(bank(2 * r + q, 0, 4 * S2), IDB[:, :],
                                                  MB2[:, :].unsqueeze(1).to_broadcast([128, 4, S2]), start=False, stop=True)
                                last.then_inc(sem["at_s_ps"], 1)
                            if j == 3:
                                after("exp", u + 1)
                                for h in range(HU):
                                    last = pe.transpose(bank(2 * r + h // 4, 128 * (h % 4), 128 * (h % 4) + 128, S2),
                                                        EE[r][:, h, :], IDN[:, :])
                                last.then_inc(sem["at_et_ps"], 1)
                            if j == 6:
                                after("etl", u + 1)
                                if u == 0:
                                    after("v", 2)
                                for h in range(HU):
                                    dst = bank(2 * r, (HD + 1) * h, (HD + 1) * h + HD + 1)
                                    hh = HU * r + h
                                    mm(dst, ETH[r][0:S2, h, :], VAH[:, b, hh, :], start=True, stop=False)
                                    mm(dst, ETH[r][0:S2, h, :], VAL[:, b, hh, :], start=False, stop=False)
                                    last = mm(dst, ETL[r][0:S2, h, :], VAH[:, b, hh, :], start=False, stop=True)
                                last.then_inc(sem["at_pv_ps"], 1)
                        if s == ATN - 4:
                            after("on", 2 * UNITS)
                            flip(0, OB).then_inc(sem["at_ot_ps"], 1)
                        if s == ATN - 2:
                            after("ot")
                            for b in range(NB):
                                last = mm(bank(1, 128 * b, 128 * b + 128), ANT[:, b, :], W2O[:, :] if ph == "a2" else W3[:, 3, :],
                                          start=True, stop=True)
                            last.then_inc(sem["at_proj_ps"], 1)
                        yield
                return run(), ATN

            def m1(g, p, steps, prev=None):
                v = turn(g, "m1")
                MHT = MHTS[p]

                def after(name, k=1):
                    pe.wait_ge(sem["m1_" + name], v("m1_" + name, k))

                def run():
                    first(pe, g, prev)
                    for s in steps:
                        if s == 5 and p == 0 and g[0] is None:
                            pe.wait_ge(setup["w2_in"], 16 * (E1 + 1))
                        if s == M1H and p == 0:
                            pe.wait_ge(setup["sb"], 10)
                        if s == 3:
                            pe.wait_ge(sem["mn_xn"], v("mn_xn", 1))
                            flip(0, AN).then_inc(sem["m1_xn_ps"], 1)
                            pe.wait_ge(sem["mn_xh"], v("mn_xh", 1))
                            flip(1, MH).then_inc(sem["mn_xh_ps"], 1)
                        if s == 5:
                            after("xht", 1)
                            for b in range(NB):
                                last = mm(bank(2, E1 * b, E1 * b + E1), ANT[:, b, :], WGT[:, :], start=True, stop=True)
                            last.then_inc(sem["m1_sc_ps"], 1)
                        if s == 9:
                            after("top", 22)
                            for b in range(NB):
                                last = pe.transpose(bank(3, 128 * b, 128 * b + 128, 2 * E1), CWF[:, b, :], IDN[:, :])
                            last.then_inc(sem["m1_cw_ps"], 1)
                        if s >= 11:
                            e, c = divmod(s - 11, 4)
                            if e < E1:
                                if e == 0 and c == 0:
                                    after("xht", 2)
                                    after("xlo")
                                    after("cwt")
                                n = 5 * e + c
                                if n >= 3:
                                    after("ring", n - 2)
                                flat = MHT[:, :, :].rearrange("p b n -> p (b n)").bitcast(F16)
                                high, low = (W1S[:, e, F1 * l + 128 * c:F1 * l + 128 * c + 128] for l in range(2))
                                mm(bank(5 + n % 3), high, flat[:, 0:T], start=True, stop=False)
                                mm(bank(5 + n % 3), high, flat[:, T:2 * T], start=False, stop=False)
                                mm(bank(5 + n % 3), low, flat[:, 0:T], start=False, stop=True).then_inc(sem["m1_up_ps"], 1)
                            if 1 <= e <= E1:
                                if c == 0 and e >= 2:
                                    after("t", e - 1)
                                after("ring", 5 * (e - 1) + c + 1)
                                mm(bank(4), W2[:, e - 1, c, :], HID[:, c, :], start=(c == 0),
                                   stop=(c == 3)).then_inc(sem["m1_dn_ps"], 1)
                            if e < E1 and c == 3:
                                n = 5 * e + 4
                                after("ring", n - 2)
                                mm(bank(5 + n % 3), SEL[:, e:e + 1].to_broadcast([2 * E1, 128]), CWTS[p][:, :], start=True,
                                   stop=True).then_inc(sem["m1_cb_ps"], 1)
                        if s == M1N - 2:
                            after("acc", E1 - 1)
                            flip(5, ACC).then_inc(sem["m1_y_ps"], 1)
                        yield
                return run(), len(steps)

            def m2(g, p, steps, prev=None):
                v = turn(g, "m2")
                MHT = MHTS[p]

                def after(name, k=1):
                    pe.wait_ge(sem["m2_" + name], v("m2_" + name, k))

                def run():
                    first(pe, g, prev)
                    for s in steps:
                        if s == M2H and p == 0:
                            pe.wait_ge(setup["l2_in"], 16 * (E2 + 2))
                        if s == 3:
                            pe.wait_ge(sem["mn_xh"], v("mn_xh", 1))
                            flip(0, MH).then_inc(sem["mn_xh_ps"], 1)
                        k, j = divmod(s - 5, 3)
                        if j == 0 and 0 <= k < 8:
                            if k == 0:
                                after("xpt")
                            if k >= 2:
                                after("ex", k - 1)
                                after("mx", k - 1)
                            mm(bank(4 + k % 2), SET[:, 128 * k:128 * k + 128], MHT[:, :, :], start=True,
                               stop=True).then_inc(sem["m2_lt_ps"], 1)
                        k, j = divmod(s - 5 - 5,3)
                        if j == 0 and 0 <= k < 8:
                            after("ed", k + 1)
                            if k:
                                after("pd", k)
                            flip(6, ED[k % 2]).then_inc(sem["m2_pd_ps"], 1)
                        k, j = divmod(s - 5 - 7,3)
                        if j == 0 and 0 <= k < 8:
                            after("pd", k + 1)
                            if k:
                                after("sl", k)
                            for b in range(NB):
                                last = mm(bank(7, 128 * b, 128 * b + 128), MH[:, b, :], PD[k % 2][:, b, :], start=True, stop=True)
                            last.then_inc(sem["m2_sl_ps"], 1)
                        e, j = divmod(s - M2E, 3)
                        if 0 <= e < E2 and j < 2:
                            if e == 0:
                                after("sl", 8)
                            else:
                                after("ht", 2 * (e - 1) + j + 1)
                            mm(bank(4 + j, 0, 256), WG[:, e, 128 * j:128 * j + 128], SL[:, e, :, :], start=True, stop=True)
                            mm(bank(4 + j, 256, 512), WU[:, e, 128 * j:128 * j + 128], SL[:, e, :, :], start=True,
                               stop=True).then_inc(sem["m2_gu_ps"], 1)
                        if j == 1 and e % 2 == 1 and 3 <= e <= 17:
                            k = (e - 3) // 2
                            after("eo", 2 * k + 2)
                            if k:
                                after("es", k)
                            flip(7, EO[k % 2]).then_inc(sem["m2_es_ps"], 1)
                        if 1 <= e <= E2 and j == 2:
                            f = e - 1
                            after("ht", 2 * f + 2)
                            if f:
                                after("eo", f)
                            for c in range(2):
                                last = mm(bank(6, 0, 256), WD[:, f, c, :], HT[f % 2][:, c, :], start=(c == 0), stop=(c == 1))
                            last.then_inc(sem["m2_dn_ps"], 1)
                        if s == M2E + 2:
                            after("mx", 8)
                            flip(7, MXS).then_inc(sem["m2_mxt_ps"], 1)
                        if s == M2E + 5:
                            after("hl", 3)
                            for b in range(NB):
                                last = pe.transpose(bank(7, 128 * b, 128 * b + 128, 2), HLF[:, b, :], IDN[:, :])
                            last.then_inc(sem["m2_nmt_ps"], 1)
                        k, j = divmod(s - M2C, 2)
                        if 0 <= k < 8 and j == 0:
                            if k >= 2:
                                after("ctt", k - 1)
                            if k == 0:
                                after("nmt")
                            mm(bank(4 + k % 2), SET[:, 128 * k:128 * k + 128], MHT[:, :, :], start=True, stop=False)
                            mm(bank(4 + k % 2), ONB[:, :], NMT[0:2, 0:T], start=False, stop=True).then_inc(sem["m2_l_ps"], 1)
                        k, j = divmod(s - M2C - 2, 2)
                        if 0 <= k < 8 and j == 0:
                            if k == 0:
                                after("es", 8)
                                after("nr", 1)
                            after("ctt", k + 1)
                            for b in range(NB):
                                at = (D + 1) * (b % 2)
                                last = mm(bank(6 + b // 2, at, at + D + 1), CTT[k % 2][:, b, :], ES[:, k, b, :],
                                          start=(k == 0 and b % 2 == 0), stop=(k == 7 and b % 2 == 1))
                            last.then_inc(sem["m2_cm_ps"], 1)
                        yield
                return run(), len(steps)

            def m3(g, p, steps, prev=None):
                v = turn(g, "m3")
                MHT = MHTS[p]
                OHT = CWTS[p].bitcast(BF16)

                def after(name, k=1):
                    pe.wait_ge(sem["m3_" + name], v("m3_" + name, k))

                def run():
                    first(pe, g, prev)
                    for s in steps:
                        if s == M3H and p == 0:
                            pe.wait_ge(setup["l3_in"], 16 * (E3 + 1))
                        if s == 3:
                            pe.wait_ge(sem["mn_xh"], v("mn_xh", 1))
                            flip(1, MH).then_inc(sem["mn_xh_ps"], 1)
                        if s == 5:
                            after("xpt", 2)
                            for b in range(NB):
                                dst = bank(2, E3 * b, E3 * b + E3)
                                mm(dst, MHT[:, b, :], CM2[:, :], start=True, stop=False)
                                mm(dst, SQT[:, b, :], ONE[:, :], start=False, stop=False)
                                last = mm(dst, ONE[:, 0:1].to_broadcast([128, 128]), CSQ[:, :], start=False, stop=True)
                            last.then_inc(sem["m3_ds_ps"], 1)
                        if s == 7:
                            after("top", 6)
                            for b in range(NB):
                                last = pe.transpose(bank(3, 128 * b, 128 * b + 128, E3), SMALL[:, 3, b, :], IDN[:, :])
                            last.then_inc(sem["m3_oh_ps"], 1)
                        if s == 9:
                            after("oht")
                        if s == 10:
                            for e in range(E3):
                                if e >= 3:
                                    after("mk", e - 2)
                                mm(bank(5 + e % 3), IDB[0:E3, e:e + 1].to_broadcast([E3, 128]), OHT[0:E3, :], start=True,
                                   stop=True).then_inc(sem["m3_mk_ps"], 1)
                        if s == M3N - 2:
                            after("yt")
                            flip(5, YT3).then_inc(sem["m3_y_ps"], 1)
                        e, j = divmod(s - 11, 4)
                        if 0 <= e < E3 and j % 2 == 0:
                            c = j // 2
                            n = 2 * e + c
                            if c == 0:
                                after("xm", e + 1)
                            if n == 0:
                                after("mk", E3)
                            if n >= 2:
                                after("hm", n - 1)
                            mm(bank(5 + 2 * n % 3), WA[:, e, F3 + 128 * c:F3 + 128 * c + 128], XM[e % 2], start=True, stop=True)
                            if n >= 1:
                                after("sg", n)
                            mm(bank(5 + (2 * n + 1) % 3), WA[:, e, 128 * c:128 * c + 128], XM[e % 2], start=True,
                               stop=True).then_inc(sem["m3_up_ps"], 1)
                        if 0 <= s - 11 - 2 and (s - 11) % 2 == 0 and (s - 11) // 2 - 1 < 2 * E3:
                            n = (s - 11) // 2 - 1
                            after("hm", n + 1)
                            mm(bank(4), WB[:, n // 2, n % 2, :], HM[n % 4], start=(n == 0), stop=(n == 2 * E3 - 1)).then_inc(sem["m3_dn_ps"], 1)
                        yield
                return run(), len(steps)

            phases(pe, a1, m1, lambda *a: attention("a2", *a), m2, lambda *a: attention("a3", *a), m3, beta_w1)

        @block.sync
        def _(sp):
            xg = t["x"].rearrange("(g b) n d -> g n b d", b=NB)
            cg = t["ctx_1024"].rearrange("(g b) n d -> g n b d", b=NB)
            og = out.rearrange("(g b) n d -> g n b d", b=NB)

            def row(name, width=128):
                ap = t[name]
                if len(ap.shape) == 1:
                    return ap.rearrange("(a d) -> a d", d=width)
                return ap.rearrange("a (c d) -> (a c) d", d=width)

            def load(dst, src, name):
                sp.dma_start(dst, src).then_inc(setup[name], 16)

            def tile(g, p):
                sp.dma_start(X[p][:, :, :], xg[g]).then_inc(x_in[p], 16)

            def context(g, p):
                sp.dma_start(C[p][:, :, :], cg[g]).then_inc(c_in[p], 16)

            tile(0, 0)
            context(0, 0)
            for k, name in ((RW0Q, "L0_xattn_Wq"), (RW0K, "L0_xattn_Wk"), (RW0V, "L0_xattn_Wv"), (RW0P, "L0_xattn_Wp"),
                            (RW1V, "L1_xattn_Wv"), (RW2O, "L2_xattn_Wo"), (RW1Q, "L1_xattn_Wq"), (RW1K, "L1_xattn_Wk")):
                load(RAW[:, k, :], t[name], "mat_in")
            for k, name in enumerate(("L3_xattn_Wq", "L3_xattn_Wk", "L3_xattn_Wv", "L3_xattn_Wo")):
                load(W3[:, k, :], t[name], "mat_in")
            at = 0
            for name in ("L1_ffn_gamma", "L1_ffn_beta", "L1_ffn_b2", "L1_ffn_b1", "L2_ffn_norm_g", "L2_ffn_norm_b",
                         "L2_ffn_slot_g", "L2_ffn_slot_b", "L3_xattn_bq", "L3_xattn_bk", "L3_ffn_scale", "L2_ffn_bd",
                         "L3_ffn_centroids"):
                src = row(name)
                load(VEC1[at:at + src.shape[0], :], src, "mat_in")
                at += src.shape[0]
            load(VEC2[0:32, :], row("L2_ffn_bg"), "mat_in")
            load(VEC2[32:64, :], row("L2_ffn_bu"), "mat_in")
            load(SE[:, :, :], t["L2_ffn_slot_embeds"].rearrange("e s d -> (e s) d").rearrange("(k p) d -> p k d", p=128), "slot_in")
            load(MKI[:, 0, :], t["mask_SxS2_ik1"], "small_in")
            load(MKI[:, 1, :], t["mask_1x1xSxS2_ik0"].rearrange("a b s t -> (a b s) t"), "small_in")
            load(RFC[:, :, :], t["L0_ffn_w_fc"].rearrange("(c f) d -> f c d", f=128), "small_in")
            load(RPJ[:, :, :], t["L0_ffn_w_proj"].rearrange("d (c f) -> d c f", f=128), "small_in")
            load(RU[:, :, :], t["L0_ffn_u"].rearrange("(c f) r -> f c r", f=128), "small_in")
            load(RFB[0:16, :], t["L0_ffn_fast_b"], "small_in")
            load(RVV[0:16, :], t["L0_ffn_v"], "small_in")
            for k, name in enumerate(("L2_xattn_Wq", "L2_xattn_Wk", "L2_xattn_Wv")):
                load(R8[0:HD, k, :], t[name], "small_in")
            for k, name in ((BQ0, "L0_xattn_bq"), (BK0, "L0_xattn_bk"), (BV0, "L0_xattn_bv"), (BP0, "L0_xattn_bp"),
                            (BO2, "L2_xattn_bo"), (BV3, "L3_xattn_bv"), (BO3, "L3_xattn_bo")):
                load(BC[:, k, :], row(name).to_broadcast([128, D]), "bc_in")
            load(SCL[:, 0:1], row("L0_ffn_gate", 1).to_broadcast([128, 1]), "bc_in")
            load(SCL[:, 1:2], row("L2_ffn_scale", 1).to_broadcast([128, 1]), "bc_in")
            load(W1[:, :, :], t["L1_ffn_W1"].rearrange("e d f -> d e f"), "w1_in")
            if groups > 1:
                tile(1, 1)
                context(1, 1)
            load(WGT[:, :], t["L1_ffn_Wg"], "w2_in")
            for e in range(E1):
                load(W2[:, e, :, :], t["L1_ffn_W2"][e].rearrange("(c p) d -> p c d", p=128), "w2_in")
            load(WG[:, :, :], t["L2_ffn_Wg"].rearrange("e d f -> d e f"), "l2_in")
            load(WU[:, :, :], t["L2_ffn_Wu"].rearrange("e d f -> d e f"), "l2_in")
            for e in range(E2):
                load(WD[:, e, :, :], t["L2_ffn_Wd"][e].rearrange("(c p) d -> p c d", p=128), "l2_in")
            load(WA[:, :, :], t["L3_ffn_up_w"].rearrange("e d f -> d e f"), "l3_in")
            for e in range(E3):
                load(WB[:, e, :, :], t["L3_ffn_down_w"][e].rearrange("(c p) d -> p c d", p=128), "l3_in")

            def pair(i, last):
                values = None if last else Pair(sp, i)

                def group(k):
                    return (None, 2 * i + k) if last else (values, k)
                if not last:
                    for p in range(2):
                        v = turn(group(p), "a2")
                        sp.wait_ge(sem["at_v"], v("at_v", 2))
                        context(2 * i + 2 + p, p)
                for p in range(2):
                    v = turn(group(p))
                    sp.wait_ge(sem["m3_out"], v("m3_out", 1))
                    sp.dma_start(og[2 * i + p], X[p][:, :, :]).then_inc(sem["m3_stored"], 16)
                    if not last:
                        sp.wait_ge(sem["m3_stored"], v("m3_stored", 16))
                        tile(2 * i + 2 + p, p)

            pairs = groups // 2
            if pairs > 1:
                with sp.Fori(0, pairs - 1) as i:
                    pair(i, False)
            pair(pairs - 1, True)
            sp.wait_ge(sem["m3_stored"], PER["m3_stored"] * groups)


def kernel(**inputs):
    import numpy as _np
    import concourse.bacc as _bacc
    from concourse import mybir as _mybir
    from concourse.bass_utils import run_bass_kernel_spmd as _run

    nc = _bacc.Bacc("TRN2", target_bir_lowering=False, num_devices=1)
    arrays, aps = {}, {}
    for name, a in inputs.items():
        if name == "itok_BxS2_0_2047":
            continue
        a = _np.ascontiguousarray(a)
        if a.ndim == 0:
            a = a.reshape(1)
        arrays[f"in_{name}_dram"] = a
        aps[name] = nc.dram_tensor(f"in_{name}_dram", a.shape, _mybir.dt.from_np(a.dtype), kind="ExternalInput").ap()
    out = nc.dram_tensor("out_0_dram", (NBATCH, N, D), F32, kind="ExternalOutput").ap()
    build(nc, aps, out)
    r = _run(nc, [arrays], core_ids=[0])
    return r.results[0]["out_0_dram"]
```
